# Optimizing a Trainium2 kernel written in Bass

```python
import numpy as np
import jax
import jax.numpy as jnp

def _softmax(x, axis=-1):
    return jax.nn.softmax(x, axis=axis)

def _gelu(x):
    return jax.nn.gelu(x, approximate=True)

def _silu(x):
    return jax.nn.silu(x)

def _sigmoid(x):
    return jax.nn.sigmoid(x)

def _layernorm(x, axis=-1, eps=1e-05):
    m = jnp.mean(x, axis=axis, keepdims=True)
    v = jnp.var(x, axis=axis, keepdims=True)
    return (x - m) / jnp.sqrt(v + eps)

def _scatter_add(tgt, idx, src, axis=0):
    return tgt.at[idx].add(src)

def _segment_sum(src, seg, n):
    return jax.ops.segment_sum(src, seg, n)
kernel_name = 'mk_gnn_resnorm_d4_gnn_r8_aab5c9'

def setup_inputs(seed: int=0):
    np.random.seed(seed)
    _w = jnp.asarray

    def _rec_inputs():
        import jax
        import jax.numpy as jnp
        _gk = jax.random.key(seed)
        x = -0.0003713 + 1 * jax.random.normal(jax.random.fold_in(_gk, 1), (12500, 128), jnp.float32)
        src = jax.random.randint(jax.random.fold_in(_gk, 2), (200000,), 0, 12500, jnp.int32)
        dst = jnp.minimum((12500 * jax.random.uniform(jax.random.fold_in(_gk, 3), (200000,)) ** 2.0).astype(jnp.int32), 99999)
        _o = jnp.argsort(dst, stable=True)
        src = src[_o]
        dst = dst[_o]
        edge_attr_4 = 0.000227908 + 0.99994 * jax.random.normal(jax.random.fold_in(_gk, 12), (200000, 4), jnp.float32)
        edge_attr_50 = 0.000164634 + 1.0002 * jax.random.normal(jax.random.fold_in(_gk, 13), (200000, 50), jnp.float32)
        edge_attr_8 = jax.random.uniform(jax.random.fold_in(_gk, 14), (200000, 8), jnp.float32, 0.0, 0.999999)
        edge_type_2 = jax.random.randint(jax.random.fold_in(_gk, 16), (200000,), 0, 2, jnp.int32)
        node_type_4 = jax.random.randint(jax.random.fold_in(_gk, 17), (12500,), 0, 4, jnp.int32)
        return (x, src, dst, edge_attr_4, edge_attr_50, edge_attr_8, edge_type_2, node_type_4)
    x, src, dst, edge_attr_4, edge_attr_50, edge_attr_8, edge_type_2, node_type_4 = _rec_inputs()

    def _L0_gnn_setup():
        import jax, jax.numpy as jnp
        import numpy as np
        N = 12500
        E = 200000
        D_IN = 128
        D_OUT = 128
        key = jax.random.key(seed)
        k1, k2, k3, k4 = jax.random.split(key, 4)
        H = jax.random.normal(k1, (N, D_IN), dtype=jnp.float32)
        src = jax.random.randint(k2, (E,), 0, N, dtype=jnp.int32)
        dst = jax.random.randint(k3, (E,), 0, N, dtype=jnp.int32)
        W = jax.random.normal(k4, (D_OUT, 2 * D_IN), dtype=jnp.float32) * 0.05
        b = jnp.zeros((D_OUT,), dtype=jnp.float32)
        return {'H': H, 'src': src, 'dst': dst, 'W': W, 'b': b}
    _L0_gnn_all = _L0_gnn_setup()
    _L0_gnn_in = {k: v for k, v in _L0_gnn_all.items() if k in ('W', 'b')}
    del _L0_gnn_all

    def _L1_gnn_setup():
        import jax, jax.numpy as jnp
        import numpy as np
        N_NODES = 6250
        N_EDGES = 100000
        NODE_DIM = 128
        EDGE_DIM = 50
        HIDDEN_DIM = 256

        def _linear_init(key, fan_in, fan_out):
            kw, kb = jax.random.split(key)
            bound = 1.0 / np.sqrt(fan_in)
            W = jax.random.uniform(kw, (fan_in, fan_out), minval=-bound, maxval=bound, dtype=jnp.float32)
            b = jax.random.uniform(kb, (fan_out,), minval=-bound, maxval=bound, dtype=jnp.float32)
            return (W, b)
        key = jax.random.key(seed)
        k1, k2, k3, k4, k5, k6, k7 = jax.random.split(key, 7)
        node_features = jax.random.normal(k1, (N_NODES, NODE_DIM), dtype=jnp.float32)
        edge_index = jax.random.randint(k2, (2, N_EDGES), 0, N_NODES, dtype=jnp.int32)
        edge_features = jax.random.normal(k3, (N_EDGES, EDGE_DIM), dtype=jnp.float32)
        msg_W1, msg_b1 = _linear_init(k4, 2 * NODE_DIM + EDGE_DIM, HIDDEN_DIM)
        msg_W2, msg_b2 = _linear_init(k5, HIDDEN_DIM, NODE_DIM)
        upd_W1, upd_b1 = _linear_init(k6, 2 * NODE_DIM, HIDDEN_DIM)
        upd_W2, upd_b2 = _linear_init(k7, HIDDEN_DIM, NODE_DIM)
        return {'node_features': node_features, 'edge_index': edge_index, 'edge_features': edge_features, 'msg_W1': msg_W1, 'msg_b1': msg_b1, 'msg_W2': msg_W2, 'msg_b2': msg_b2, 'upd_W1': upd_W1, 'upd_b1': upd_b1, 'upd_W2': upd_W2, 'upd_b2': upd_b2}
    _L1_gnn_all = _L1_gnn_setup()
    _L1_gnn_in = {k: v for k, v in _L1_gnn_all.items() if k in ('msg_W1', 'msg_b1', 'msg_W2', 'msg_b2', 'upd_W1', 'upd_b1', 'upd_W2', 'upd_b2')}
    del _L1_gnn_all

    def _L2_gnn_setup():
        import jax, jax.numpy as jnp
        import numpy as np
        MUL = 32
        N_NODES = 2048
        N_EDGES = 32768
        AVG_NEIGH = 16.0
        N_SPECIES = 4
        RADIAL_DIM = 8
        INV_SQRT3 = 0.5773502691896258
        key = jax.random.key(seed)
        ks = jax.random.split(key, 14)
        f32 = jnp.float32
        return {'node_features': jax.random.normal(ks[0], (N_NODES, 4 * MUL), dtype=f32), 'edge_sh': jax.random.normal(ks[1], (N_EDGES, 4), dtype=f32), 'radial_embedding': jax.random.uniform(ks[2], (N_EDGES, RADIAL_DIM), dtype=f32), 'W_up_s': jax.random.normal(ks[3], (MUL, MUL), dtype=f32), 'W_up_v': jax.random.normal(ks[4], (MUL, MUL), dtype=f32), 'W_r1': jax.random.normal(ks[5], (RADIAL_DIM, RADIAL_DIM), dtype=f32), 'W_r2': jax.random.normal(ks[6], (RADIAL_DIM, 4 * MUL), dtype=f32), 'W_dn_s': jax.random.normal(ks[7], (2 * MUL, 2 * MUL), dtype=f32), 'W_dn_v': jax.random.normal(ks[8], (2 * MUL, MUL), dtype=f32), 'W_sk_s': jax.random.normal(ks[9], (N_SPECIES, MUL, 2 * MUL), dtype=f32), 'W_sk_v': jax.random.normal(ks[10], (N_SPECIES, MUL, MUL), dtype=f32), 'senders': jax.random.randint(ks[11], (N_EDGES,), 0, N_NODES), 'receivers': jax.random.randint(ks[12], (N_EDGES,), 0, N_NODES), 'node_species': jax.random.randint(ks[13], (N_NODES,), 0, N_SPECIES)}
    _L2_gnn_all = _L2_gnn_setup()
    _L2_gnn_in = {k: v for k, v in _L2_gnn_all.items() if k in ('W_up_s', 'W_up_v', 'W_r1', 'W_r2', 'W_dn_s', 'W_dn_v', 'W_sk_s', 'W_sk_v')}
    del _L2_gnn_all

    def _L3_gnn_setup():
        import jax, jax.numpy as jnp
        import numpy as np
        IN_DIM = 128
        OUT_DIM = 128
        N_NODES = 1250
        N_EDGES = 80000
        key = jax.random.key(seed)
        ks = jax.random.split(key, 9)
        X = jax.random.normal(ks[0], (N_NODES, IN_DIM), dtype=jnp.float32)
        edge_index = jax.random.randint(ks[1], (2, N_EDGES), 0, N_NODES, dtype=jnp.int64)
        edge_types = jax.random.randint(ks[2], (N_EDGES,), 0, 2, dtype=jnp.int64)
        s = 1.0 / np.sqrt(IN_DIM)
        W_data = jax.random.uniform(ks[3], (OUT_DIM, IN_DIM), minval=-s, maxval=s, dtype=jnp.float32)
        b_data = jax.random.uniform(ks[4], (OUT_DIM,), minval=-s, maxval=s, dtype=jnp.float32)
        W_control = jax.random.uniform(ks[5], (OUT_DIM, IN_DIM), minval=-s, maxval=s, dtype=jnp.float32)
        b_control = jax.random.uniform(ks[6], (OUT_DIM,), minval=-s, maxval=s, dtype=jnp.float32)
        W_self = jax.random.uniform(ks[7], (OUT_DIM, IN_DIM), minval=-s, maxval=s, dtype=jnp.float32)
        b_self = jax.random.uniform(ks[8], (OUT_DIM,), minval=-s, maxval=s, dtype=jnp.float32)
        return {'X': X, 'edge_index': edge_index, 'edge_types': edge_types, 'W_data': W_data, 'b_data': b_data, 'W_control': W_control, 'b_control': b_control, 'W_self': W_self, 'b_self': b_self}
    _L3_gnn_all = _L3_gnn_setup()
    _L3_gnn_in = {k: v for k, v in _L3_gnn_all.items() if k in ('W_data', 'b_data', 'W_control', 'b_control', 'W_self', 'b_self')}
    del _L3_gnn_all
    return {'x': x, 'src': src, 'dst': dst, 'edge_attr_4': edge_attr_4, 'edge_attr_50': edge_attr_50, 'edge_attr_8': edge_attr_8, 'edge_type_2': edge_type_2, 'node_type_4': node_type_4, 'L0_gnn_W': _L0_gnn_in['W'], 'L0_gnn_b': _L0_gnn_in['b'], 'L1_gnn_msg_W1': _L1_gnn_in['msg_W1'], 'L1_gnn_msg_b1': _L1_gnn_in['msg_b1'], 'L1_gnn_msg_W2': _L1_gnn_in['msg_W2'], 'L1_gnn_msg_b2': _L1_gnn_in['msg_b2'], 'L1_gnn_upd_W1': _L1_gnn_in['upd_W1'], 'L1_gnn_upd_b1': _L1_gnn_in['upd_b1'], 'L1_gnn_upd_W2': _L1_gnn_in['upd_W2'], 'L1_gnn_upd_b2': _L1_gnn_in['upd_b2'], 'L2_gnn_W_up_s': _L2_gnn_in['W_up_s'], 'L2_gnn_W_up_v': _L2_gnn_in['W_up_v'], 'L2_gnn_W_r1': _L2_gnn_in['W_r1'], 'L2_gnn_W_r2': _L2_gnn_in['W_r2'], 'L2_gnn_W_dn_s': _L2_gnn_in['W_dn_s'], 'L2_gnn_W_dn_v': _L2_gnn_in['W_dn_v'], 'L2_gnn_W_sk_s': _L2_gnn_in['W_sk_s'], 'L2_gnn_W_sk_v': _L2_gnn_in['W_sk_v'], 'L3_gnn_W_data': _L3_gnn_in['W_data'], 'L3_gnn_b_data': _L3_gnn_in['b_data'], 'L3_gnn_W_control': _L3_gnn_in['W_control'], 'L3_gnn_b_control': _L3_gnn_in['b_control'], 'L3_gnn_W_self': _L3_gnn_in['W_self'], 'L3_gnn_b_self': _L3_gnn_in['b_self']}

def reference(x, src, dst, edge_attr_4, edge_attr_50, edge_attr_8, edge_type_2, node_type_4, L0_gnn_W, L0_gnn_b, L1_gnn_msg_W1, L1_gnn_msg_b1, L1_gnn_msg_W2, L1_gnn_msg_b2, L1_gnn_upd_W1, L1_gnn_upd_b1, L1_gnn_upd_W2, L1_gnn_upd_b2, L2_gnn_W_up_s, L2_gnn_W_up_v, L2_gnn_W_r1, L2_gnn_W_r2, L2_gnn_W_dn_s, L2_gnn_W_dn_v, L2_gnn_W_sk_s, L2_gnn_W_sk_v, L3_gnn_W_data, L3_gnn_b_data, L3_gnn_W_control, L3_gnn_b_control, L3_gnn_W_self, L3_gnn_b_self):
    import jax
    import jax.numpy as jnp

    def _L0_gnn_ref(H, src, dst, W, b):
        import jax, jax.numpy as jnp
        import numpy as np
        N = 12500
        E = 200000
        D_IN = 128
        D_OUT = 128
        gathered = H[dst]
        agg = jax.ops.segment_max(gathered, src, num_segments=N)
        deg = jax.ops.segment_sum(jnp.ones((src.shape[0],), jnp.float32), src, num_segments=N)
        H_neigh = jnp.where(deg[:, None] > 0, agg, 0.0)
        H_concat = jnp.concatenate([H, H_neigh], axis=1)
        return H_concat @ W.T + b

    def _L1_gnn_ref(node_features, edge_index, edge_features, msg_W1, msg_b1, msg_W2, msg_b2, upd_W1, upd_b1, upd_W2, upd_b2):
        import jax, jax.numpy as jnp
        import numpy as np
        N_NODES = 6250
        N_EDGES = 100000
        NODE_DIM = 128
        EDGE_DIM = 50
        HIDDEN_DIM = 256

        def _linear_init(key, fan_in, fan_out):
            kw, kb = jax.random.split(key)
            bound = 1.0 / np.sqrt(fan_in)
            W = jax.random.uniform(kw, (fan_in, fan_out), minval=-bound, maxval=bound, dtype=jnp.float32)
            b = jax.random.uniform(kb, (fan_out,), minval=-bound, maxval=bound, dtype=jnp.float32)
            return (W, b)
        src = edge_index[0]
        dst = edge_index[1]
        h_src = node_features[src]
        h_dst = node_features[dst]
        msg_in = jnp.concatenate([h_src, h_dst, edge_features], axis=-1)
        h = jax.nn.silu(msg_in @ msg_W1 + msg_b1)
        messages = h @ msg_W2 + msg_b2
        aggregated = jax.ops.segment_sum(messages, dst, num_segments=node_features.shape[0])
        upd_in = jnp.concatenate([node_features, aggregated], axis=-1)
        u = jax.nn.silu(upd_in @ upd_W1 + upd_b1)
        node_new = u @ upd_W2 + upd_b2
        return node_features + node_new

    def _L2_gnn_ref(node_features, edge_sh, radial_embedding, W_up_s, W_up_v, W_r1, W_r2, W_dn_s, W_dn_v, W_sk_s, W_sk_v, senders, receivers, node_species):
        import jax, jax.numpy as jnp
        import numpy as np
        MUL = 32
        N_NODES = 2048
        N_EDGES = 32768
        AVG_NEIGH = 16.0
        N_SPECIES = 4
        RADIAL_DIM = 8
        INV_SQRT3 = 0.5773502691896258
        n = node_features.shape[0]
        s = node_features[:, :MUL]
        v = node_features[:, MUL:].reshape(n, MUL, 3)
        s1 = s @ W_up_s * MUL ** (-0.5)
        v1 = jnp.einsum('nmi,mk->nki', v, W_up_v) * MUL ** (-0.5)
        ss = s1[senders]
        vs = v1[senders]
        yv = edge_sh[:, 1:4]
        m_v_tp = ss[:, :, None] * yv[:, None, :]
        m_s_tp = jnp.einsum('emi,ei->em', vs, yv) * INV_SQRT3
        h = jax.nn.silu(radial_embedding @ W_r1 * RADIAL_DIM ** (-0.5))
        w = h @ W_r2 * RADIAL_DIM ** (-0.5)
        w_ss, w_vs, w_vt, w_st = jnp.split(w, 4, axis=1)
        m_s = jnp.concatenate([ss * w_ss, m_s_tp * w_st], axis=1)
        m_v = jnp.concatenate([vs * w_vs[:, :, None], m_v_tp * w_vt[:, :, None]], axis=1)
        inv = AVG_NEIGH ** (-0.5)
        S = jax.ops.segment_sum(m_s, receivers, num_segments=n) * inv
        V = jax.ops.segment_sum(m_v.reshape(m_v.shape[0], -1), receivers, num_segments=n).reshape(n, 2 * MUL, 3) * inv
        g_s = S @ W_dn_s * (2 * MUL) ** (-0.5)
        g_v = jnp.einsum('nmi,mk->nki', V, W_dn_v) * (2 * MUL) ** (-0.5)
        sk_s = jnp.einsum('nm,nmk->nk', s, W_sk_s[node_species]) * MUL ** (-0.5)
        sk_v = jnp.einsum('nmi,nmk->nki', v, W_sk_v[node_species]) * MUL ** (-0.5)
        g_s = 0.5 * (g_s + sk_s)
        g_v = 0.5 * (g_v + sk_v)
        feat_s = jax.nn.silu(g_s[:, :MUL])
        gates = jax.nn.silu(g_s[:, MUL:])
        out_v = g_v * gates[:, :, None]
        return jnp.concatenate([feat_s, out_v.reshape(n, 3 * MUL)], axis=1)

    def _L3_gnn_ref(X, edge_index, edge_types, W_data, b_data, W_control, b_control, W_self, b_self):
        import jax, jax.numpy as jnp
        import numpy as np
        IN_DIM = 128
        OUT_DIM = 128
        N_NODES = 1250
        N_EDGES = 80000
        src, dst = (edge_index[0], edge_index[1])
        Xs = X[src]
        m_data = Xs @ W_data.T + b_data
        m_ctrl = Xs @ W_control.T + b_control
        msg = jnp.where((edge_types == 0)[:, None], m_data, m_ctrl)
        agg = jax.ops.segment_sum(msg, dst, num_segments=X.shape[0])
        out = agg + (X @ W_self.T + b_self)
        return jax.nn.relu(out)
    edge_index = jnp.stack([src, dst])
    x = _layernorm(x + _L0_gnn_ref(x, src, dst, L0_gnn_W, L0_gnn_b), axis=-1)
    x = _layernorm(x + _L1_gnn_ref(x, edge_index, edge_attr_50, L1_gnn_msg_W1, L1_gnn_msg_b1, L1_gnn_msg_W2, L1_gnn_msg_b2, L1_gnn_upd_W1, L1_gnn_upd_b1, L1_gnn_upd_W2, L1_gnn_upd_b2), axis=-1)
    x = _layernorm(x + _L2_gnn_ref(x, edge_attr_4, edge_attr_8, L2_gnn_W_up_s, L2_gnn_W_up_v, L2_gnn_W_r1, L2_gnn_W_r2, L2_gnn_W_dn_s, L2_gnn_W_dn_v, L2_gnn_W_sk_s, L2_gnn_W_sk_v, src, dst, node_type_4), axis=-1)
    x = _layernorm(x + _L3_gnn_ref(x, edge_index, edge_type_2, L3_gnn_W_data, L3_gnn_b_data, L3_gnn_W_control, L3_gnn_b_control, L3_gnn_W_self, L3_gnn_b_self), axis=-1)
    return x

_drawn_inputs = setup_inputs


def setup_inputs(seed=0):
    import zlib

    import numpy as np

    out = dict(_drawn_inputs(seed))
    spreads = {'L0_gnn_b': (0.0, 0.1)}
    factors = {'edge_attr_50': 4.431,
     'L1_gnn_msg_b1': 3.665,
     'L1_gnn_upd_b1': 7.322,
     'L3_gnn_b_self': 3.707}
    for name, (base, spread) in spreads.items():
        noise = np.random.default_rng([zlib.crc32(name.encode()), seed]).standard_normal(out[name].shape)
        drawn = base * np.exp(spread * noise) if base else spread * noise
        out[name] = jnp.asarray(drawn.astype(out[name].dtype))
    for name, factor in factors.items():
        out[name] = (out[name] * factor).astype(out[name].dtype)
    return out
```

```python
from contextlib import ExitStack

import concourse.bass as bass
from concourse import mybir

F32 = mybir.dt.float32
I32 = mybir.dt.int32
BF16 = mybir.dt.bfloat16
ALU = mybir.AluOpType
ACT = mybir.ActivationFunctionType
AX = mybir.AxisListType

P = 128
N = 12500
E = 200000
D = 128
NBLK = -(-N // P)
NLAST = N - (NBLK - 1) * P
HI = NBLK + 1
PADKEY = NBLK * P
TM = 1560
TE = 1568
TAIL = E - P * TM
NT = 1664
PC = 66
C_SRC, C_SPOS, C_DL, C_DL0 = 62, 63, 64, 65
XC = D + 1
FAR = 1 << 20
FARPOS = float(1 << 26)
NB = 4
G2 = 2
KB = 7
EPS = 1e-5
STEP = 2e34


def runs(groups, lags, depth, eng, step):
    assert groups % depth == 0 and max(lags) <= depth
    for turn in range(depth):
        for s, lag in enumerate(lags):
            if turn >= lag:
                step(s, turn - lag, (turn - lag) % depth, (turn - lag) // depth)
    with eng.Fori(1, groups // depth) as i:
        for turn in range(depth):
            for s, lag in enumerate(lags):
                back = (lag - turn + depth - 1) // depth if lag > turn else 0
                step(s, i * depth + (turn - lag), (turn - lag) % depth, i - back)
    for turn in range(groups, groups + max(lags)):
        for s, lag in enumerate(lags):
            if turn - lag < groups:
                step(s, turn - lag, (turn - lag) % depth, (turn - lag) // depth)


def wait(eng, sem, value):
    if not isinstance(value, int) or value > 0:
        eng.wait_ge(sem, value)


def two_before(b, r):
    return (b - 2, r + 1) if b >= 2 else (b + 2, r)


class Names:
    pass


class Phase:

    def __init__(self, nc, tag):
        self.nc, self.tag, self.ctx, self.semaphores = nc, tag, ExitStack(), []

    def __enter__(self):
        return self

    def __exit__(self, *a):
        self.ctx.close()
        self.nc.clear_and_free_semaphores(self.semaphores)
        self.nc.all_engine_barrier()

    def sb(self, name, shape, dt=F32):
        return self.ctx.enter_context(self.nc.sbuf_tensor(f"{self.tag}_{name}", shape, dt))

    def sbs(self, name, n, shape, dt=F32):
        return [self.sb(f"{name}{k}", shape, dt) for k in range(n)]

    def bank(self, name, dt=F32):
        cols = 512 if dt == F32 else 1024
        return self.ctx.enter_context(self.nc.psum_tensor(f"{self.tag}_{name}", [P, cols], dt))

    def sem(self, name):
        self.semaphores.append(self.nc.alloc_semaphore(f"{self.tag}_{name}"))
        return self.semaphores[-1]

    def sems(self, name, n=NB):
        return [self.sem(f"{name}{k}") for k in range(n)]

    def block(self):
        return self.ctx.enter_context(self.nc.Block())


def count_phase(nc, S, a):
    with Phase(nc, "count") as ph:
        zb = ph.sb("zb", [P, 2 * HI], BF16)
        tmpl = ph.sb("tmpl", [P, 26, PC])
        zx = ph.sb("zx", [P, 6, XC])
        types = ph.sb("types", [P, TE], I32)
        f0 = ph.sb("f0", [P, TE])
        dhi0 = ph.sb("dhi0", [P, TE])
        ti = ph.sb("ti", [P, TE], I32)
        ohd = ph.sbs("ohd", NB, [P, G2, P + 2 * HI], BF16)
        ohs = ph.sbs("ohs", NB, [P, G2, P + HI], BF16)
        cnt = ph.sb("cnt", [P, 3, HI])
        ones = ph.sb("ones", [P, P])
        onec = ph.sb("onec", [P, NBLK])
        tot = ph.sb("tot", [P, 2, NBLK])
        toti = ph.sb("toti", [P, NBLK], I32)
        ex = ph.sb("ex", [P, 2, NBLK])
        cum = ph.sb("cum", [P, 2, NBLK])
        cumT = ph.sb("cumT", [P, 1])
        iotaj = ph.sb("iotaj", [P, NT])
        cmp = ph.sb("cmp", [P, NT])
        degT = ph.sb("degT", [P, 2, P])
        one_row = ph.sb("one_row", [NBLK, P])
        en = ph.sb("en", [P, 3, NBLK])
        eni = ph.sb("eni", [P, 3, NBLK], I32)
        psD, psS = ph.bank("psD"), ph.bank("psS")
        psA, psB, psC = ph.bank("psA"), ph.bank("psB"), ph.bank("psC")
        s_const, s_load, s_key, s_tmpl = ph.sem("s_const"), ph.sem("s_load"), ph.sem("s_key"), ph.sem("s_tmpl")
        s_pad, s_fill, s_x, s_xpad = ph.sem("s_pad"), ph.sem("s_fill"), ph.sem("s_x"), ph.sem("s_xpad")
        s_oh, s_free = ph.sems("s_oh"), ph.sems("s_free")
        s_hist, s_d, s_pe, s_out = ph.sem("s_hist"), ph.sem("s_d"), ph.sem("s_pe"), ph.sem("s_out")
        block = ph.block()

        @block.sync
        def _(sp):
            sp.wait_ge(s_pad, 4)
            for arr, t in ((a.src, S.src_key), (a.dst, S.dst_key), (a.edge_type_2, types)):
                sp.dma_start(t[:, 0:TM], arr[0:P * TM].rearrange("(p t) -> p t", t=TM)).then_inc(s_load, 16)
                full = TAIL // P
                sp.dma_start(t[:, TM:TM + full],
                             arr[P * TM:P * (TM + full)].rearrange("(t p) -> p t", p=P),
                             allow_slow_non_contiguous=True).then_inc(s_load, 16)
                sp.dma_start(t[0:TAIL - P * full, TM + full:TM + full + 1],
                             arr[P * (TM + full):E].rearrange("(p t) -> p t", t=1),
                             allow_slow_non_contiguous=True).then_inc(s_load, 16)
            sp.dma_start(S.x[:, 0:NBLK - 1, :],
                         a.x[0:(NBLK - 1) * P, :].rearrange("(b p) d -> p b d", p=P)).then_inc(s_x, 16)
            sp.dma_start(S.x[0:NLAST, NBLK - 1, :], a.x[(NBLK - 1) * P:N, :]).then_inc(s_x, 16)
            sp.wait_ge(s_tmpl, 4)
            rec = S.records.rearrange("(p j) c -> p j c", p=P)
            with sp.Fori(0, NT // 26) as i:
                sp.dma_start(rec[:, bass.ds(i * 26, 26), :], tmpl[:]).then_inc(s_fill, 16)
            xs = S.by_src.rearrange("(p j) c -> p j c", p=P)
            sp.dma_start(xs[:, TE - 6:TE, :], zx[:]).then_inc(s_fill, 16)
            sp.wait_ge(s_fill, 16 * (NT // 26 + 1))
            sp.wait_ge(s_x, 32)
            sp.wait_ge(s_d, 7)
            sp.wait_ge(s_const, 10)
            sp.dma_start(S.deg_rows[0, :].rearrange("(b p) -> b p", p=P), degT[0:NBLK, 0, :]).then_inc(s_out, 16)
            sp.dma_start(S.deg_rows[1, :].rearrange("(b p) -> b p", p=P), degT[0:NBLK, 1, :]).then_inc(s_out, 16)
            sp.dma_start(S.deg_rows[2, :].rearrange("(b p) -> b p", p=P), one_row[:]).then_inc(s_out, 16)
            sp.wait_ge(s_out, 48)

        @block.gpsimd
        def _(pool):
            for t in (S.src_key, S.dst_key, types):
                pool.memset(t[:, TM:TE], PADKEY).then_inc(s_pad, 1)
            pool.memset(S.x[:, NBLK - 1, :], 0.0).then_inc(s_pad, 1)
            pool.iota(S.iota[:], pattern=[[1, P]], base=0, channel_multiplier=0,
                      allow_small_or_imprecise_dtypes=True).then_inc(s_const, 1)
            pool.memset(S.ident[:], 0.0).then_inc(s_const, 1)
            pool.memset(S.lower[:], 1.0).then_inc(s_const, 1)
            pool.memset(S.upper[:], 1.0).then_inc(s_const, 1)
            pool.wait_ge(s_const, 4)
            pool.affine_select(out=S.ident[:], in_=S.ident[:], compare_op=ALU.not_equal, fill=1.0, base=0,
                               pattern=[[-1, P]], channel_multiplier=1).then_inc(s_const, 1)
            pool.affine_select(out=S.lower[:], in_=S.lower[:], compare_op=ALU.is_gt, fill=0.0, base=0,
                               pattern=[[-1, P]], channel_multiplier=1).then_inc(s_const, 1)
            pool.affine_select(out=S.upper[:], in_=S.upper[:], compare_op=ALU.is_gt, fill=0.0, base=0,
                               pattern=[[1, P]], channel_multiplier=-1).then_inc(s_const, 1)
            pool.iota(iotaj[:], pattern=[[1, NT]], base=0, channel_multiplier=0,
                      allow_small_or_imprecise_dtypes=True).then_inc(s_const, 1)
            pool.memset(one_row[:], 1.0).then_inc(s_const, 1)
            pool.memset(ones[:], 1.0).then_inc(s_const, 1)

        @block.vector
        def _(v):
            v.memset(tmpl[:], 0.0).then_inc(s_tmpl, 1)
            v.memset(zx[:], 0.0).then_inc(s_tmpl, 1)
            v.wait_ge(s_tmpl, 2)
            v.memset(tmpl[:, :, C_DL:C_DL0 + 1], -1.0).then_inc(s_tmpl, 1)
            v.memset(tmpl[:].bitcast(I32)[:, :, C_SPOS:C_SPOS + 1], FAR).then_inc(s_tmpl, 1)
            v.memset(zb[:], 0.0).then_inc(s_key, 1)
            v.memset(onec[:], 1.0).then_inc(s_key, 1)
            v.wait_ge(s_const, 5)
            v.tensor_copy(S.ident_b[:], S.ident[:]).then_inc(s_key, 1)
            v.tensor_copy(S.iota_b[:], S.iota[:]).then_inc(s_key, 1)
            v.wait_ge(s_load, 144)
            n = 4
            for q, t in enumerate((S.src_key, S.dst_key)):
                kf, lo, hi = S.key_f[:, :, q], S.lo[:, :, q], S.hi[:, :, q]
                v.tensor_copy(kf, t[:]).then_inc(s_key, 1)
                v.tensor_scalar(ti[:], t[:], P - 1, None, ALU.bitwise_and).then_inc(s_key, 1)
                n += 2
                v.wait_ge(s_key, n)
                v.tensor_copy(lo, ti[:]).then_inc(s_key, 1)
                n += 1
                v.wait_ge(s_key, n)
                v.tensor_scalar(ti[:], t[:], 7, None, ALU.logical_shift_right).then_inc(s_key, 1)
                n += 1
                v.wait_ge(s_key, n)
                v.tensor_copy(hi, ti[:]).then_inc(s_key, 1)
                n += 1
                v.wait_ge(s_key, n)
            v.tensor_copy(f0[:], types[:]).then_inc(s_key, 1)
            v.wait_ge(s_key, n + 1)
            v.tensor_scalar(f0[:], f0[:], 0.0, None, ALU.is_equal).then_inc(s_key, 1)
            v.wait_ge(s_key, n + 2)
            v.scalar_tensor_tensor(S.dst_lo0[:], S.lo[:, :, 1], 1.0, f0[:], ALU.add, ALU.mult).then_inc(s_key, 1)
            v.scalar_tensor_tensor(dhi0[:], S.hi[:, :, 1], -127.0, f0[:], ALU.add, ALU.mult).then_inc(s_key, 1)
            v.wait_ge(s_key, n + 4)
            v.tensor_scalar(S.dst_lo0[:], S.dst_lo0[:], -1.0, None, ALU.add).then_inc(s_key, 1)
            v.tensor_scalar(dhi0[:], dhi0[:], 127.0, None, ALU.add).then_inc(s_key, 1)
            v.wait_ge(s_key, n + 6)
            def step(s, g, b, r):
                wait(v, s_free[b], r)
                for k in range(G2):
                    t = bass.ds(g * G2 + k, 1)
                    v.tensor_scalar(ohd[b][:, k, 0:P], S.iota_b[:], S.lo[:, t, 1], None, ALU.is_equal)
                    v.tensor_scalar(ohd[b][:, k, P:P + HI], S.iota_b[:, 0:HI], S.hi[:, t, 1], None, ALU.is_equal)
                    v.tensor_scalar(ohd[b][:, k, P + HI:], S.iota_b[:, 0:HI], dhi0[:, t], None, ALU.is_equal)
                    v.tensor_scalar(ohs[b][:, k, 0:P], S.iota_b[:], S.lo[:, t, 0], None, ALU.is_equal)
                    last = v.tensor_scalar(ohs[b][:, k, P:], S.iota_b[:, 0:HI], S.hi[:, t, 0], None, ALU.is_equal)
                last.then_inc(s_oh[b], 1)
            runs(TE // G2, [0], NB, v, step)

            v.wait_ge(s_hist, 1)
            v.tensor_copy(cnt[:, 0:2, :], psD[:, 0:2 * HI].rearrange("p (a h) -> p a h", a=2)).then_inc(s_d, 1)
            v.tensor_copy(cnt[:, 2, :], psS[:, 0:HI]).then_inc(s_d, 1)
            v.wait_ge(s_pe, 1)
            v.tensor_copy(tot[:], psA[:, 0:2 * NBLK].rearrange("p (a h) -> p a h", a=2)).then_inc(s_d, 1)
            v.tensor_copy(ex[:], psB[:, 0:2 * NBLK].rearrange("p (a h) -> p a h", a=2)).then_inc(s_d, 1)
            v.wait_ge(s_pe, 2)
            v.tensor_copy(degT[0:NBLK, :, :], psC[0:NBLK, 0:2 * P].rearrange("p (a h) -> p a h", a=2)).then_inc(s_d, 1)
            v.wait_ge(s_d, 5)
            v.tensor_scalar(toti[:], tot[:, 0, :], 127.0, None, ALU.add).then_inc(s_d, 1)
            v.wait_ge(s_d, 6)
            v.tensor_scalar(toti[:], toti[:], 7, None, ALU.logical_shift_right).then_inc(s_d, 1)
            v.wait_ge(s_d, 7)
            v.tensor_copy(tot[:, 0, :], toti[:]).then_inc(s_d, 1)
            v.wait_ge(s_d, 8)
            for q in range(2):
                v.tensor_tensor_scan(cum[:, q, :], onec[:], tot[:, q, :], 0.0, ALU.mult, ALU.add).then_inc(s_d, 1)
            v.wait_ge(s_d, 10)
            v.tensor_tensor(tot[:], cum[:], tot[:], ALU.subtract).then_inc(s_d, 1)
            v.wait_ge(s_d, 11)
            v.tensor_tensor(S.base[:, 0:NBLK], tot[:, 1, :], ex[:, 1, :], ALU.add).then_inc(s_d, 1)
            v.scalar_tensor_tensor(S.base[:, HI:HI + NBLK], tot[:, 0, :], float(P), ex[:, 0, :],
                                   ALU.mult, ALU.add).then_inc(s_d, 1)
            for q in range(2):
                v.memset(S.base[:, q * HI + NBLK:q * HI + HI], FARPOS).then_inc(s_d, 1)
            v.wait_ge(s_d, 15)
            v.scalar_tensor_tensor(en[:, 0, :], S.base[:, 0:NBLK], -1.0, cnt[:, 2, 0:NBLK],
                                   ALU.add, ALU.add).then_inc(s_d, 1)
            v.tensor_scalar(en[:, 1, :], cnt[:, 2, 0:NBLK], 0.0, float(FAR), ALU.is_equal, ALU.mult).then_inc(s_d, 1)
            v.wait_ge(s_d, 17)
            v.tensor_scalar(eni[:, 0, :], en[:, 0, :], 0.0, None, ALU.max).then_inc(s_d, 1)
            v.wait_ge(s_d, 18)
            v.tensor_scalar(eni[:, 1, :], eni[:, 0, :], P - 1, None, ALU.bitwise_and).then_inc(s_d, 1)
            v.tensor_scalar(eni[:, 2, :], eni[:, 0, :], 7, None, ALU.logical_shift_right).then_inc(s_d, 1)
            v.wait_ge(s_d, 20)
            v.scalar_tensor_tensor(en[:, 0, :], eni[:, 1, :], float(TE), eni[:, 2, :], ALU.mult, ALU.add).then_inc(s_d, 1)
            v.wait_ge(s_d, 21)
            v.tensor_tensor(S.last[:], en[:, 0, :], en[:, 1, :], ALU.add).then_inc(s_d, 1)
            v.wait_ge(s_pe, 3)
            v.tensor_copy(cumT[0:NBLK, :], psC[0:NBLK, 0:1]).then_inc(s_d, 1)
            v.wait_ge(s_d, 23)
            v.wait_ge(s_const, 10)
            v.tensor_scalar(cmp[0:NBLK, :], iotaj[0:NBLK, :], cumT[0:NBLK, :], None, ALU.is_ge).then_inc(s_d, 1)
            for q, pb in enumerate((psA, psB, psC, psD)):
                v.wait_ge(s_pe, 4 + q)
                w = NT // 4
                v.tensor_scalar(S.blk[0:1, q * w:q * w + w], pb[0:1, 0:w], float(NBLK - 1), None, ALU.min).then_inc(s_d, 1)

        @block.tensor
        def _(pe):
            pe.wait_ge(s_key, 4)
            pe.matmul(psD[:, 0:2 * HI], S.ident_b[:], zb[:], start=True, stop=False, skip_group_check=True)
            pe.matmul(psS[:, 0:HI], S.ident_b[:], zb[:, 0:HI], start=True, stop=False, skip_group_check=True)

            def step(s, g, b, r):
                pe.wait_ge(s_oh[b], r + 1)
                for k in range(G2):
                    pe.matmul(psD[:, 0:2 * HI], ohd[b][:, k, 0:P], ohd[b][:, k, P:], start=False, stop=False,
                              skip_group_check=True)
                    last = pe.matmul(psS[:, 0:HI], ohs[b][:, k, 0:P], ohs[b][:, k, P:], start=False, stop=False,
                                     skip_group_check=True)
                last.then_inc(s_free[b], 1)
            runs(TE // G2, [0], NB, pe, step)
            pe.matmul(psD[:, 0:2 * HI], S.ident_b[:], zb[:], start=False, stop=True, skip_group_check=True)
            pe.matmul(psS[:, 0:HI], S.ident_b[:], zb[:, 0:HI], start=False, stop=True,
                      skip_group_check=True).then_inc(s_hist, 1)
            pe.wait_ge(s_d, 2)
            pe.wait_ge(s_const, 10)
            for q, c in ((0, 0), (1, 2)):
                pe.matmul(psA[:, q * NBLK:(q + 1) * NBLK], ones[:], cnt[:, c, 0:NBLK], start=True, stop=True)
                last = pe.matmul(psB[:, q * NBLK:(q + 1) * NBLK], S.upper[:], cnt[:, c, 0:NBLK], start=True, stop=True)
            last.then_inc(s_pe, 1)
            for q in range(2):
                last = pe.transpose(psC[0:NBLK, q * P:(q + 1) * P], cnt[:, q, 0:NBLK], S.ident[:])
            last.then_inc(s_pe, 1)
            pe.wait_ge(s_d, 10)
            pe.transpose(psC[0:NBLK, 0:P], cum[:, 0, :], S.ident[:]).then_inc(s_pe, 1)
            pe.wait_ge(s_d, 24)
            for q, pb in enumerate((psA, psB, psC, psD)):
                w = NT // 4
                pe.matmul(pb[0:1, 0:w], ones[0:NBLK, 0:1], cmp[0:NBLK, q * w:q * w + w],
                          start=True, stop=True).then_inc(s_pe, 1)


def place_phase(nc, S, a):
    with Phase(nc, "place") as ph:
        pl = ph.sbs("pl", NB, [P, G2, PC])
        kc = ph.sbs("kc", NB, [P, G2, 2])
        ohlo = ph.sbs("ohlo", NB, [P, G2, 2, P], BF16)
        ohhi = ph.sbs("ohhi", NB, [P, G2, 2, HI], BF16)
        ohT = ph.sbs("ohT", NB, [P, G2, 2, P])
        seen = ph.sbs("seen", 2, [P, 2 * HI])
        same = ph.sbs("same", 2, [P, G2, 2, P])
        found = ph.sbs("found", 2, [P, G2, 2, HI])
        rank = ph.sbs("rank", NB, [P, G2, 2])
        look = ph.sbs("look", NB, [P, G2, 2])
        posi = ph.sbs("posi", NB, [P, G2, 2], I32)
        pos7 = ph.sbs("pos7", NB, [P, 2, G2, 2], I32)
        place = ph.sbs("place", NB, [P, G2], I32)
        psT = [ph.bank(f"psT{k}", BF16) for k in range(2)]
        psK = [ph.bank(f"psK{k}") for k in range(2)]
        psG = [ph.bank(f"psG{k}") for k in range(2)]
        psR = ph.bank("psR")
        s_z, s_seen, s_R, s_i = ph.sem("s_z"), ph.sem("s_seen"), ph.sem("s_R"), ph.sem("s_i")
        s_oh, s_T, s_ohT, s_rank = ph.sems("s_oh"), ph.sems("s_T"), ph.sems("s_ohT"), ph.sems("s_rank")
        s_G, s_look, s_ef, s_meta = ph.sems("s_G"), ph.sems("s_look"), ph.sems("s_ef"), ph.sems("s_meta")
        s_place, s_sent, s_turn = ph.sems("s_place"), ph.sems("s_sent"), ph.sem("s_turn")
        block = ph.block()
        GT = TE // G2
        ATTRS = ((a.edge_attr_50, 0, 50), (a.edge_attr_4, 50, 4), (a.edge_attr_8, 54, 8))

        @block.sync
        def _(sp):
            sp.wait_ge(s_z, NB)
            with sp.Fori(0, TM // G2 // NB) as i:
                for b in range(NB):
                    sp.wait_ge(s_sent[b], i * (16 * G2))
                    for arr, c0, c in ATTRS:
                        sp.dma_start(pl[b][:, :, c0:c0 + c],
                                     arr[0:P * TM, :].rearrange("(p t) c -> p t c", t=TM)
                                     [:, bass.ds((i * NB + b) * G2, G2), :]).then_inc(s_ef[b], 16)
            r = TM // G2 // NB
            full = TAIL // P
            for b in range(NB):
                sp.wait_ge(s_sent[b], r * 16 * G2)
                for arr, c0, c in ATTRS:
                    if b == 0:
                        sp.dma_start(pl[b][:, 0:full, c0:c0 + c],
                                     arr[P * TM:P * (TM + full), :].rearrange("(t p) c -> p t c", p=P)
                                     ).then_inc(s_ef[b], 16)
                    elif b == 1:
                        sp.dma_start(pl[b][0:TAIL - P * full, 0, c0:c0 + c],
                                     arr[P * (TM + full):E, :]).then_inc(s_ef[b], 16)
                if b > 1:
                    sp.sem_inc(s_ef[b], 48)
            for b in range(NB):
                sp.wait_ge(s_sent[b], (r + 1) * 16 * G2)

        @block.gpsimd
        def _(pool):
            bound = pool.to_reg(P * NT - 1)
            pool.wait_ge(s_z, NB)

            def step(s, g, b, r):
                rec = pl[b][:].bitcast(I32)
                if s == 0:
                    wait(pool, s_sent[b], r * 16 * G2)
                    t = bass.ds(g * G2, G2)
                    pool.tensor_copy(rec[:, :, C_SRC], S.src_key[:, t])
                    pool.tensor_copy(pl[b][:, :, C_DL], S.lo[:, t, 1])
                    pool.tensor_copy(pl[b][:, :, C_DL0], S.dst_lo0[:, t]).then_inc(s_meta[b], 1)
                else:
                    pool.wait_ge(s_ef[b], (r + 1) * 48)
                    pool.wait_ge(s_place[b], r + 1)
                    pool.wait_ge(s_meta[b], r + 1)
                    pool.sem_inc(s_turn, 1)
                    for k in range(G2):
                        pool.indirect_dma_start(S.records[:], bass.IndirectOffsetOnAxis(ap=place[b][:, k:k + 1], axis=0),
                                                pl[b][:, k, :], None, bounds_check=bound, oob_is_err=False
                                                ).then_inc(s_sent[b], 16)
            runs(GT, [0, 2], NB, pool, step)
            for b in range(NB):
                pool.wait_ge(s_sent[b], (GT // NB) * 16 * G2)

        @block.vector
        def _(v):
            for b in range(NB):
                v.memset(pl[b][:], 0.0).then_inc(s_z, 1)

            def step(s, g, b, r):
                if s == 2:
                    wait(v, s_G[b], r)
                    t = bass.ds(g * G2, G2)
                    v.tensor_copy(kc[b][:], S.key_f[:, t, :])
                    for k in range(G2):
                        t = bass.ds(g * G2 + k, 1)
                        for q in range(2):
                            v.tensor_scalar(ohlo[b][:, k, q, :], S.iota_b[:], S.lo[:, t, q], None, ALU.is_equal)
                            last = v.tensor_scalar(ohhi[b][:, k, q, :], S.iota_b[:, 0:HI], S.hi[:, t, q], None,
                                                   ALU.is_equal)
                    last.then_inc(s_oh[b], 1)
                elif s == 1:
                    v.wait_ge(s_ohT[b], r + 1)
                    o, n = two_before(b, r)
                    wait(v, s_rank[o], n)
                    for k in range(G2):
                        for q in range(2):
                            c = (k * 2 + q) * P
                            last = v.scalar_tensor_tensor(same[b % 2][:, k, q, :], psK[b % 2][:, c:c + P], kc[b][:, k, q:q + 1],
                                                          S.lower[:], ALU.is_equal, ALU.mult,
                                                          accum_out=rank[b][:, k, q:q + 1])
                    last.then_inc(s_rank[b], 1)
                else:
                    v.wait_ge(s_G[b], r + 1)
                    o, n = two_before(b, r)
                    wait(v, s_look[o], n)
                    for k in range(G2):
                        for q in range(2):
                            c = k * 2 * HI + q * HI
                            last = v.tensor_tensor_reduce(out=found[b % 2][:, k, q, :], in0=psG[b % 2][:, c:c + HI],
                                                          in1=ohhi[b][:, k, q, :], scale=1.0, scalar=0.0,
                                                          op0=ALU.mult, op1=ALU.add,
                                                          accum_out=look[b][:, k, q:q + 1])
                    last.then_inc(s_look[b], 1)
                    v.wait_ge(s_look[b], r + 1)
                    wait(v, s_sent[b], r * 16 * G2)
                    v.tensor_tensor(posi[b][:], rank[b][:], look[b][:], ALU.add).then_inc(s_i, 1)
                    v.wait_ge(s_i, g * 3 + 1)
                    v.tensor_scalar(pos7[b][:, 0], posi[b][:], P - 1, None, ALU.bitwise_and).then_inc(s_i, 1)
                    v.tensor_scalar(pos7[b][:, 1], posi[b][:], 7, None, ALU.logical_shift_right).then_inc(s_i, 1)
                    v.wait_ge(s_i, g * 3 + 3)
                    v.scalar_tensor_tensor(pl[b][:].bitcast(I32)[:, :, C_SPOS], pos7[b][:, 0, :, 0], float(TE),
                                           pos7[b][:, 1, :, 0], ALU.mult, ALU.add)
                    v.scalar_tensor_tensor(place[b][:], pos7[b][:, 0, :, 1], float(NT),
                                           pos7[b][:, 1, :, 1], ALU.mult, ALU.add).then_inc(s_place[b], 1)
            runs(GT, [2, 1, 0], NB, v, step)

        @block.scalar
        def _(act):
            def step(s, g, b, r):
                if s == 1:
                    act.wait_ge(s_T[b], r + 1)
                    wait(act, s_G[b], r)
                    act.activation(ohT[b][:].rearrange("p a q e -> p (a q e)"), psT[b % 2][:, 0:4 * P],
                                   ACT.Copy).then_inc(s_ohT[b], 1)
                else:
                    for k in range(G2):
                        act.wait_ge(s_R, g * G2 + k + 1)
                        if k == 0:
                            o, n = (b + NB - 1) % NB, r if b == 0 else r + 1
                            wait(act, s_G[o], n)
                        act.activation(seen[k][:], psR[:, 0:2 * HI], ACT.Copy).then_inc(s_seen, 1)
            runs(GT, [1, 0], NB, act, step)

        @block.tensor
        def _(pe):
            pe.matmul(psR[:, 0:2 * HI], S.ident[:], S.base[:], start=True, stop=False,
                      skip_group_check=True).then_inc(s_R, 1)

            def step(s, g, b, r):
                if s == 1:
                    pe.wait_ge(s_oh[b], r + 1)
                    o, n = two_before(b, r)
                    wait(pe, s_rank[o], n)
                    for k in range(G2):
                        for q in range(2):
                            c = (k * 2 + q) * P
                            pe.transpose(psT[b % 2][:, c:c + P], ohlo[b][:, k, q, :], S.ident_b[:])
                            last = pe.matmul(psK[b % 2][:, c:c + P], kc[b][:, k, q:q + 1].to_broadcast([P, P]),
                                             S.ident[:], start=True, stop=True)
                    last.then_inc(s_T[b], 1)
                else:
                    pe.wait_ge(s_ohT[b], r + 1)
                    o, n = two_before(b, r)
                    wait(pe, s_look[o], n)
                    for k in range(G2):
                        pe.wait_ge(s_seen, g * G2 + k + 1)
                        for q in range(2):
                            last = pe.matmul(psR[:, q * HI:(q + 1) * HI], ohlo[b][:, k, q, :], ohhi[b][:, k, q, :],
                                             start=False, stop=False, skip_group_check=True)
                        last.then_inc(s_R, 1)
                        for q in range(2):
                            c = k * 2 * HI + q * HI
                            last = pe.matmul(psG[b % 2][:, c:c + HI], ohT[b][:, k, q, :],
                                             seen[k][:, q * HI:(q + 1) * HI], start=True, stop=True)
                    last.then_inc(s_G[b], 1)
            runs(GT, [1, 0], NB, pe, step)


def send_phase(nc, S, a):
    with Phase(nc, "send") as ph:
        pl = ph.sbs("pl", NB, [P, G2, PC])
        oh = ph.sbs("oh", NB, [P, G2, P])
        ohT = ph.sbs("ohT", NB, [P, G2, P])
        row = ph.sbs("row", NB, [P, G2, XC])
        psT = [ph.bank(f"psT{k}") for k in range(2)]
        psX = [ph.bank(f"psX{k}") for k in range(2)]
        s_rec, s_oh, s_T, s_ohT = ph.sems("s_rec"), ph.sems("s_oh"), ph.sems("s_T"), ph.sems("s_ohT")
        s_X, s_row, s_sent, s_turn = ph.sems("s_X"), ph.sems("s_row"), ph.sems("s_sent"), ph.sem("s_turn")
        block = ph.block()
        GT = NT // G2
        rec = S.records.rearrange("(p j) c -> p j c", p=P)

        @block.sync
        def _(sp):
            def step(s, g, b, r):
                wait(sp, s_sent[b], r * 16 * G2)
                sp.dma_start(pl[b][:], rec[:, bass.ds(g * G2, G2), :]).then_inc(s_rec[b], 16)
            runs(GT, [0], NB, sp, step)

        @block.gpsimd
        def _(pool):
            bound = pool.to_reg(P * TE - 1)

            def step(s, g, b, r):
                pool.wait_ge(s_row[b], r + 1)
                pool.sem_inc(s_turn, 1)
                for k in range(G2):
                    at = pl[b][:].bitcast(I32)[:, k, C_SPOS:C_SPOS + 1]
                    pool.indirect_dma_start(S.by_src[:], bass.IndirectOffsetOnAxis(ap=at, axis=0),
                                            row[b][:, k, :], None, bounds_check=bound, oob_is_err=False
                                            ).then_inc(s_sent[b], 16)
            runs(GT, [2], NB, pool, step)
            for b in range(NB):
                pool.wait_ge(s_sent[b], (GT // NB) * 16 * G2)

        @block.vector
        def _(v):
            def step(s, g, b, r):
                if s == 0:
                    v.wait_ge(s_rec[b], (r + 1) * 16)
                    wait(v, s_X[b], r)
                    for k in range(G2):
                        v.tensor_scalar(oh[b][:, k, :], S.iota[:], pl[b][:, k, C_DL:C_DL + 1], None, ALU.is_equal)
                    t = bass.ds(g * G2, G2)
                    v.tensor_copy(S.e_src[:, t], pl[b][:].bitcast(I32)[:, :, C_SRC])
                    v.tensor_copy(S.e_dl[:, t], pl[b][:, :, C_DL])
                    last = v.tensor_copy(S.e_dl0[:, t], pl[b][:, :, C_DL0])
                    last.then_inc(s_oh[b], 1)
                else:
                    v.wait_ge(s_X[b], r + 1)
                    wait(v, s_sent[b], r * 16 * G2)
                    v.tensor_copy(row[b][:, :, 0:D], psX[b % 2][:, 0:G2 * P].rearrange("p (k d) -> p k d", k=G2))
                    v.tensor_copy(row[b][:, :, D], pl[b][:].bitcast(I32)[:, :, C_SRC]).then_inc(s_row[b], 1)
            runs(GT, [0, 2], NB, v, step)

        @block.scalar
        def _(act):
            def step(s, g, b, r):
                act.wait_ge(s_T[b], r + 1)
                wait(act, s_X[b], r)
                act.activation(ohT[b][:].rearrange("p k e -> p (k e)"), psT[b % 2][:, 0:G2 * P],
                               ACT.Copy).then_inc(s_ohT[b], 1)
            runs(GT, [0], NB, act, step)

        @block.tensor
        def _(pe):
            def step(s, g, b, r):
                o, n = two_before(b, r)
                if s == 1:
                    pe.wait_ge(s_oh[b], r + 1)
                    wait(pe, s_ohT[o], n)
                    for k in range(G2):
                        last = pe.transpose(psT[b % 2][:, k * P:(k + 1) * P], oh[b][:, k, :], S.ident[:])
                    last.then_inc(s_T[b], 1)
                else:
                    pe.wait_ge(s_ohT[b], r + 1)
                    wait(pe, s_row[o], n)
                    for k in range(G2):
                        at = pe.value_load(S.blk[0:1, bass.ds(g * G2 + k, 1)], min_val=0, max_val=NBLK - 1)
                        last = pe.matmul(psX[b % 2][:, k * P:(k + 1) * P], ohT[b][:, k, :],
                                         S.x[:, bass.ds(at, 1), :].rearrange("p a d -> p (a d)"),
                                         start=True, stop=True)
                    last.then_inc(s_X[b], 1)
            runs(GT, [1, 0], NB, pe, step)


def max_phase(nc, S, a):
    with Phase(nc, "max") as ph:
        W = 4
        row = ph.sbs("row", NB, [P, W, XC])
        key = ph.sbs("key", NB, [P, W * P])
        step_down = ph.sbs("step_down", NB, [P, W * P])
        run = ph.sbs("run", NB, [P, W * P])
        back = ph.sbs("back", NB, [P, W * P])
        ps_x = [ph.bank(f"ps_x{k}") for k in range(2)]
        ps_k = [ph.bank(f"ps_k{k}") for k in range(2)]
        ps_o = [ph.bank(f"ps_o{k}") for k in range(2)]
        s_row, s_x, s_key, s_run, s_o, s_back, s_out = (ph.sems(n) for n in
                                                        ("s_row", "s_x", "s_key", "s_run", "s_o", "s_back", "s_out"))
        s_z, s_down = ph.sem("s_z"), ph.sem("s_down")
        block = ph.block()
        GT = TE // W
        by_src = S.by_src.rearrange("(p j) c -> p j c", p=P)
        running = S.running.rearrange("(p j) d -> p j d", p=P)

        @block.sync
        def _(sp):
            def step(s, g, b, r):
                wait(sp, s_x[b], r)
                sp.dma_start(row[b][:], by_src[:, bass.ds(g * W, W), :]).then_inc(s_row[b], 16)
            runs(GT, [0], NB, sp, step)

        @block.gpsimd
        def _(pool):
            pool.memset(run[NB - 1][:, W * P - 1:], -1e38).then_inc(s_z, 1)
            pool.memset(key[NB - 1][:, W * P - 1:], 0.0).then_inc(s_z, 1)

            def step(s, g, b, r):
                pool.wait_ge(s_back[b], r + 1)
                pool.dma_start(running[:, bass.ds(g * W, W), :],
                               back[b][:].rearrange("p (k d) -> p k d", k=W)).then_inc(s_out[b], 16)
            runs(GT, [0], NB, pool, step)
            for b in range(NB):
                pool.wait_ge(s_out[b], (GT // NB) * 16)

        @block.scalar
        def _(act):
            act.wait_ge(s_z, 2)

            def step(s, g, b, r):
                if s == 0:
                    act.wait_ge(s_x[b], r + 1)
                    wait(act, s_run[(b + 1) % NB], r if b < NB - 1 else r + 1)
                    act.activation(key[b][:], ps_k[b % 2][:, :], ACT.Copy, scale=-STEP).then_inc(s_key[b], 1)
                else:
                    act.wait_ge(s_o[b], r + 1)
                    wait(act, s_out[b], r * 16)
                    act.activation(back[b][:], ps_o[b % 2][:, :], ACT.Copy).then_inc(s_back[b], 1)
            runs(GT, [0, 1], NB, act, step)

        @block.vector
        def _(v):
            v.wait_ge(s_z, 2)

            def step(s, g, b, r):
                o = (b + NB - 1) % NB
                v.wait_ge(s_key[b], r + 1)
                wait(v, s_o[b], r)
                v.tensor_tensor(step_down[b][:, 1:], key[b][:, 1:], key[b][:, :W * P - 1], ALU.subtract)
                v.tensor_tensor(step_down[b][:, 0:1], key[b][:, 0:1], key[o][:, W * P - 1:],
                                ALU.subtract).then_inc(s_down, 1)
                v.wait_ge(s_down, g + 1)
                wait(v, s_run[o], r if b == 0 else r + 1)
                v.tensor_tensor_scan(run[b][:], step_down[b][:], ps_x[b % 2][:, :], run[o][:, W * P - 1:],
                                     ALU.add, ALU.max).then_inc(s_run[b], 1)
            runs(GT, [0], NB, v, step)

        @block.tensor
        def _(pe):
            def step(s, g, b, r):
                o, n = two_before(b, r)
                if s == 0:
                    pe.wait_ge(s_row[b], (r + 1) * 16)
                    wait(pe, s_run[o], n)
                    for k in range(W):
                        c = slice(k * P, (k + 1) * P)
                        pe.transpose(ps_x[b % 2][:, c], row[b][:, k, 0:D], S.ident[:])
                        last = pe.matmul(ps_k[b % 2][:, c], row[b][:, k, D:D + 1].to_broadcast([P, P]), S.ident[:],
                                         start=True, stop=True)
                    last.then_inc(s_x[b], 1)
                else:
                    pe.wait_ge(s_run[b], r + 1)
                    wait(pe, s_back[o], n)
                    for k in range(W):
                        c = slice(k * P, (k + 1) * P)
                        last = pe.transpose(ps_o[b % 2][:, c], run[b][:, c], S.ident[:])
                    last.then_inc(s_o[b], 1)
            runs(GT, [0, 1], NB, pe, step)


def normalize(v, ph, y, out, s, n):
    W = ph.ln
    v.tensor_reduce(W.mean[:], y, AX.X, ALU.add).then_inc(s, 1)
    v.wait_ge(s, n + 1)
    v.tensor_scalar(W.mean[:], W.mean[:], 1.0 / D, None, ALU.mult).then_inc(s, 1)
    v.wait_ge(s, n + 2)
    v.tensor_tensor(y, y, W.mean[:].rearrange("p (k a) -> p k a", a=1).to_broadcast([P, KB, D]),
                    ALU.subtract).then_inc(s, 1)
    v.wait_ge(s, n + 3)
    v.tensor_tensor(W.sq[:], y, y, ALU.mult).then_inc(s, 1)
    v.wait_ge(s, n + 4)
    v.tensor_reduce(W.var[:], W.sq[:], AX.X, ALU.add).then_inc(W.s_var, 1)
    v.wait_ge(W.s_root, W.turn)
    v.reciprocal(W.inv[:], W.root[:]).then_inc(s, 1)
    v.wait_ge(s, n + 5)
    v.tensor_tensor(out, y, W.inv[:].rearrange("p (k a) -> p k a", a=1).to_broadcast([P, KB, D]),
                    ALU.mult).then_inc(s, 1)
    return n + 6


def norm_buffers(ph, sq=None):
    W = Names()
    W.mean, W.var, W.root, W.inv = (ph.sb(n, [P, KB]) for n in ("mean", "var", "root", "inv"))
    W.sq = ph.sb("sq", [P, KB, D]) if sq is None else sq
    W.eps = ph.sb("eps", [P, 1])
    W.s_var, W.s_root, W.s_eps = ph.sem("s_var"), ph.sem("s_root"), ph.sem("s_eps")
    ph.ln = W


def root(act, ph, i):
    W = ph.ln
    act.wait_ge(W.s_var, i + 1)
    act.wait_ge(W.s_eps, 1)
    act.activation(W.root[:], W.var[:], ACT.Sqrt, bias=W.eps[:], scale=1.0 / D).then_inc(W.s_root, 1)


NIT = NBLK // KB
CH = KB * P // 2


def blocks_of(bank0, bank1, k):
    return (bank0, k * P) if k < 4 else (bank1, (k - 4) * P)


def node0_phase(nc, S, a):
    with Phase(nc, "node0") as ph:
        norm_buffers(ph)
        w0 = ph.sb("w0", [P, 2 * D])
        w0T = ph.sb("w0T", [P, 2, D])
        w1 = ph.sb("w1", [P, 2, 2 * D])
        b0 = ph.sb("b0", [P, D])
        b1 = ph.sb("b1", [P, 2 * D])
        at = ph.sb("at", [P, KB], I32)
        mx = ph.sb("mx", [P, KB, D])
        xc = ph.sb("xc", [P, KB, D])
        T = ph.sb("T", [P, 2, KB, P])
        y = ph.sb("y", [P, KB, D])
        ab = ph.sb("ab", [P, 2, KB, 2 * D])
        ps = [ph.bank(f"ps{k}") for k in range(8)]
        s_w, s_wT, s_wc = ph.sem("s_w"), ph.sem("s_wT"), ph.sem("s_wc")
        s_at, s_zero, s_mx, s_xc = ph.sem("s_at"), ph.sem("s_zero"), ph.sem("s_mx"), ph.sem("s_xc")
        s_T, s_Tc, s_y, s_v, s_n = ph.sem("s_T"), ph.sem("s_Tc"), ph.sem("s_y"), ph.sem("s_v"), ph.sem("s_n")
        s_T2, s_T2c, s_ab, s_abc, s_out = (ph.sem(n) for n in ("s_T2", "s_T2c", "s_ab", "s_abc", "s_out"))
        s_turn = ph.sem("s_turn")
        block = ph.block()

        @block.sync
        def _(sp):
            sp.dma_start(w0[:], a.L0_gnn_W).then_inc(s_w, 16)
            for q in range(2):
                sp.dma_start(w1[:, q, :], a.L1_gnn_msg_W1[q * D:(q + 1) * D, :]).then_inc(s_w, 16)
            sp.dma_start(b0[:], a.L0_gnn_b.rearrange("(a d) -> a d", a=1).to_broadcast([P, D])).then_inc(s_w, 16)
            sp.dma_start(b1[:], a.L1_gnn_msg_b1.rearrange("(a d) -> a d", a=1).to_broadcast([P, 2 * D])).then_inc(s_w, 16)
            with sp.Fori(0, NIT) as i:
                sp.wait_ge(s_abc, 8 * i + 8)
                for q, tab in enumerate((S.tab_a, S.tab_b)):
                    sp.dma_start(tab.rearrange("(k p) d -> p k d", p=P)[:, bass.ds(i * KB, KB), :],
                                 ab[:, q]).then_inc(s_out, 16)
            sp.wait_ge(s_out, 32 * NIT)

        @block.gpsimd
        def _(pool):
            pool.memset(ph.ln.eps[:], EPS).then_inc(ph.ln.s_eps, 1)
            bound = pool.to_reg(P * TE - 1)
            with pool.Fori(0, NIT) as i:
                pool.wait_ge(s_T, i)
                pool.sem_inc(s_turn, 1)
                pool.memset(mx[:], 0.0).then_inc(s_zero, 1)
                pool.tensor_copy(at[:], S.last[:, bass.ds(i * KB, KB)]).then_inc(s_zero, 1)
                pool.wait_ge(s_zero, 2 * i + 2)
                pool.sem_inc(s_turn, 1)
                for k in range(KB):
                    pool.indirect_dma_start(mx[:, k, :], None, S.running[:],
                                            bass.IndirectOffsetOnAxis(ap=at[:, k:k + 1], axis=0),
                                            bounds_check=bound, oob_is_err=False).then_inc(s_mx, 16)

        @block.tensor
        def _(pe):
            pe.wait_ge(s_w, 80)
            for q in range(2):
                last = pe.transpose(ps[0][:, q * P:(q + 1) * P], w0[:, q * D:(q + 1) * D], S.ident[:])
            last.then_inc(s_wT, 1)
            pe.wait_ge(s_wc, 1)
            with pe.Fori(0, NIT) as i:
                pe.wait_ge(s_mx, (i + 1) * 16 * KB)
                pe.wait_ge(s_xc, i + 1)
                wait(pe, s_abc, 8 * i)
                for q, t in ((0, xc), (1, mx)):
                    for k in range(KB):
                        bank, c = blocks_of(ps[2 * q], ps[2 * q + 1], k)
                        last = pe.transpose(bank[:, c:c + P], t[:, k, :], S.ident[:])
                last.then_inc(s_T, 1)
                pe.wait_ge(s_Tc, 4 * i + 4)
                for k in range(KB):
                    bank, c = blocks_of(ps[4], ps[5], k)
                    pe.matmul(bank[:, c:c + D], T[:, 0, k, :], w0T[:, 0, :], start=True, stop=False)
                    last = pe.matmul(bank[:, c:c + D], T[:, 1, k, :], w0T[:, 1, :], start=False, stop=True)
                last.then_inc(s_y, 1)
                pe.wait_ge(s_n, i + 1)
                for k in range(KB):
                    bank, c = blocks_of(ps[6], ps[7], k)
                    last = pe.transpose(bank[:, c:c + P], xc[:, k, :], S.ident[:])
                last.then_inc(s_T2, 1)
                pe.wait_ge(s_T2c, 2 * i + 2)
                for k in range(KB):
                    for q in range(2):
                        last = pe.matmul(ps[k][:, q * 256:(q + 1) * 256], T[:, 0, k, :], w1[:, q, :],
                                         start=True, stop=True)
                last.then_inc(s_ab, 1)

        @block.scalar
        def _(act):
            with act.Fori(0, NIT) as i:
                act.wait_ge(s_T, i + 1)
                for q in range(2):
                    act.activation(T[:, q, 0:4, :].rearrange("p k e -> p (k e)"), ps[2 * q][:, :],
                                   ACT.Copy).then_inc(s_Tc, 1)
                    act.activation(T[:, q, 4:KB, :].rearrange("p k e -> p (k e)"), ps[2 * q + 1][:, 0:3 * P],
                                   ACT.Copy).then_inc(s_Tc, 1)
                root(act, ph, i)
                act.wait_ge(s_T2, i + 1)
                act.activation(T[:, 0, 0:4, :].rearrange("p k e -> p (k e)"), ps[6][:, :], ACT.Copy).then_inc(s_T2c, 1)
                act.activation(T[:, 0, 4:KB, :].rearrange("p k e -> p (k e)"), ps[7][:, 0:3 * P],
                               ACT.Copy).then_inc(s_T2c, 1)

        @block.vector
        def _(v):
            v.wait_ge(s_wT, 1)
            v.tensor_copy(w0T[:], ps[0][:, 0:2 * P].rearrange("p (q d) -> p q d", q=2)).then_inc(s_wc, 1)
            VN = 8
            with v.Fori(0, NIT) as i:
                rows = S.x[:, bass.ds(i * KB, KB), :]
                v.wait_ge(s_ab, i)
                v.tensor_scalar(xc[:], rows, 1.0, None, ALU.mult).then_inc(s_xc, 1)
                v.wait_ge(s_y, i + 1)
                n = VN * i
                v.wait_ge(s_xc, i + 1)
                v.tensor_tensor(y[:, 0:4, :], xc[:, 0:4, :], ps[4][:, :].rearrange("p (k d) -> p k d", k=4), ALU.add)
                v.tensor_tensor(y[:, 4:KB, :], xc[:, 4:KB, :], ps[5][:, 0:3 * P].rearrange("p (k d) -> p k d", k=3),
                                ALU.add).then_inc(s_v, 1)
                v.wait_ge(s_v, n + 1)
                v.tensor_tensor(y[:], y[:], b0[:].rearrange("p (a d) -> p a d", a=1).to_broadcast([P, KB, D]),
                                ALU.add).then_inc(s_v, 1)
                v.wait_ge(s_v, n + 2)
                ph.ln.turn = i + 1
                n = normalize(v, ph, y[:], xc[:], s_v, n + 2)
                v.wait_ge(s_v, n)
                v.tensor_scalar(rows, xc[:], 1.0, None, ALU.mult).then_inc(s_n, 1)
                v.wait_ge(s_ab, i + 1)
                wait(v, s_out, 32 * i)
                for k in range(KB):
                    v.tensor_copy(ab[:, 0, k, :], ps[k][:, 0:256])
                    v.tensor_tensor(ab[:, 1, k, :], ps[k][:, 256:512], b1[:], ALU.add).then_inc(s_abc, 1)
                v.sem_inc(s_abc, 1)


def gather_on(pool, b, ix, rows, table, s_ix, s_got, s_turn, r):
    pool.wait_ge(s_ix[b], r + 1)
    pool.sem_inc(s_turn, 1)
    for k in range(G2):
        pool.indirect_dma_start(rows[b][:, k, :], None, table[:],
                                bass.IndirectOffsetOnAxis(ap=ix[b][:, k:k + 1], axis=0)).then_inc(s_got[b], 16)


def add_to_blocks(v, S, agg, psA, b, r, g, s_C, s_half, s_acc):
    v.wait_ge(s_C[b], r + 1)
    for k in range(G2):
        at = v.value_load(S.blk[0:1, bass.ds(g * G2 + k, 1)], min_val=0, max_val=NBLK - 1)
        block = agg[:, bass.ds(at, 1), :].rearrange("p a c -> p (a c)")
        if k == 0:
            wait(v, s_acc[(b + NB - 1) % NB], r if b == 0 else r + 1)
        else:
            v.wait_ge(s_half[b], r + 1)
        v.tensor_tensor(block, block, psA[b % 2][:, k * 2 * D:(k + 1) * 2 * D],
                        ALU.add).then_inc((s_half if k == 0 else s_acc)[b], 1)


def edge1_phase(nc, S, a, agg):
    with Phase(nc, "edge1") as ph:
        H = 2 * D
        NE = 50
        pl = ph.sbs("pl", NB, [P, G2, PC])
        ix = ph.sbs("ix", NB, [P, G2], I32)
        fs = ph.sbs("fs", NB, [P, G2, H])
        fd = ph.sbs("fd", 2, [P, G2, H])
        oh = ph.sbs("oh", NB, [P, G2, P])
        ohT = ph.sbs("ohT", 2, [P, G2 * P])
        eT = ph.sbs("eT", 2, [P, G2 * P])
        hin = ph.sbs("hin", 2, [P, G2 * H])
        h = ph.sbs("h", 2, [P, G2, H])
        we = ph.sb("we", [P, H])
        psT = [ph.bank(f"psT{k}") for k in range(2)]
        psH = [ph.bank(f"psH{k}") for k in range(2)]
        psA = [ph.bank(f"psA{k}") for k in range(2)]
        s_w, s_turn, s_zero = ph.sem("s_w"), ph.sem("s_turn"), ph.sem("s_zero")
        s_half, s_acc = ph.sems("s_half"), ph.sems("s_acc")
        s_rec, s_fd, s_ix, s_got, s_oh = (ph.sems(n) for n in ("s_rec", "s_fd", "s_ix", "s_got", "s_oh"))
        s_T, s_TT, s_H, s_in, s_h, s_C = (ph.sems(n) for n in ("s_T", "s_TT", "s_H", "s_in", "s_h", "s_C"))
        block = ph.block()
        GT = NT // G2
        rec = S.records.rearrange("(p j) c -> p j c", p=P)

        @block.sync
        def _(sp):
            sp.dma_start(we[0:NE, :], a.L1_gnn_msg_W1[2 * D:2 * D + NE, :]).then_inc(s_w, 16)

            def step(s, g, b, r):
                wait(sp, s_T[b], r)
                sp.dma_start(pl[b][:], rec[:, bass.ds(g * G2, G2), :]).then_inc(s_rec[b], 16)
                o, n = two_before(b, r)
                wait(sp, s_H[o], n)
                for k in range(G2):
                    at = sp.value_load(S.blk[0:1, bass.ds(g * G2 + k, 1)], min_val=0, max_val=NBLK - 1)
                    sp.dma_start(fd[b % 2][:, k, :], S.tab_b[bass.ds(at * P, P), :]).then_inc(s_fd[b], 16)
            runs(GT, [0], NB, sp, step)

        @block.gpsimd
        def _(pool):
            runs(GT, [0], NB, pool,
                 lambda s, g, b, r: gather_on(pool, b, ix, fs, S.tab_a, s_ix, s_got, s_turn, r))

        @block.vector
        def _(v):
            v.memset(agg[:], 0.0).then_inc(s_zero, 1)
            v.wait_ge(s_zero, 1)

            def step(s, g, b, r):
                if s == 0:
                    wait(v, s_got[b], r * 16 * G2)
                    wait(v, s_in[b], r)
                    v.tensor_scalar(ix[b][:], S.e_src[:, bass.ds(g * G2, G2)], 1.0, None, ALU.mult).then_inc(s_ix[b], 1)
                elif s == 1:
                    wait(v, s_C[b], r)
                    for k in range(G2):
                        last = v.tensor_scalar(oh[b][:, k, :], S.iota[:], S.e_dl[:, bass.ds(g * G2 + k, 1)], None,
                                               ALU.is_equal)
                    last.then_inc(s_oh[b], 1)
                elif s == 2:
                    add_to_blocks(v, S, agg, psA, b, r, g, s_C, s_half, s_acc)
                else:
                    v.wait_ge(s_H[b], r + 1)
                    v.wait_ge(s_got[b], (r + 1) * 16 * G2)
                    o, n = two_before(b, r)
                    wait(v, s_h[o], n)
                    v.tensor_tensor(hin[b % 2][:], psH[b % 2][:, :], fs[b][:].rearrange("p k c -> p (k c)"),
                                    ALU.add).then_inc(s_in[b], 1)
            runs(GT, [0, 1, 4, 2], NB, v, step)

        @block.scalar
        def _(act):
            def step(s, g, b, r):
                o, n = two_before(b, r)
                if s == 0:
                    act.wait_ge(s_T[b], r + 1)
                    wait(act, s_H[o], n)
                    act.activation(ohT[b % 2][:], psT[b % 2][:, 0:G2 * P], ACT.Copy)
                    act.activation(eT[b % 2][0:NE, :], psT[b % 2][0:NE, G2 * P:2 * G2 * P], ACT.Copy).then_inc(s_TT[b], 1)
                else:
                    act.wait_ge(s_in[b], r + 1)
                    wait(act, s_C[o], n)
                    act.activation(h[b % 2][:].rearrange("p k c -> p (k c)"), hin[b % 2][:], ACT.Silu).then_inc(s_h[b], 1)
            runs(GT, [1, 2], NB, act, step)

        @block.tensor
        def _(pe):
            pe.wait_ge(s_w, 16)

            def step(s, g, b, r):
                o, n = two_before(b, r)
                if s == 0:
                    pe.wait_ge(s_TT[b], r + 1)
                    pe.wait_ge(s_fd[b], (r + 1) * 16 * G2)
                    wait(pe, s_in[o], n)
                    for k in range(G2):
                        c = slice(k * H, (k + 1) * H)
                        e = slice(k * P, (k + 1) * P)
                        pe.matmul(psH[b % 2][:, c], ohT[b % 2][:, e], fd[b % 2][:, k, :], start=True, stop=False)
                        last = pe.matmul(psH[b % 2][:, c], eT[b % 2][0:NE, e], we[0:NE, :], start=False, stop=True)
                    last.then_inc(s_H[b], 1)
                elif s == 1:
                    pe.wait_ge(s_oh[b], r + 1)
                    pe.wait_ge(s_rec[b], (r + 1) * 16)
                    wait(pe, s_TT[o], n)
                    for k in range(G2):
                        pe.transpose(psT[b % 2][:, k * P:(k + 1) * P], oh[b][:, k, :], S.ident[:])
                        last = pe.transpose(psT[b % 2][0:NE, (G2 + k) * P:(G2 + k + 1) * P], pl[b][:, k, 0:NE],
                                            S.ident[:])
                    last.then_inc(s_T[b], 1)
                else:
                    pe.wait_ge(s_h[b], r + 1)
                    wait(pe, s_acc[o], n)
                    for k in range(G2):
                        for q in range(2):
                            c = k * H + q * D
                            last = pe.matmul(psA[b % 2][:, c:c + D], h[b % 2][:, k, q * D:(q + 1) * D],
                                             oh[b][:, k, :], start=True, stop=True)
                    last.then_inc(s_C[b], 1)
            runs(GT, [2, 1, 3], NB, pe, step)


def node1_phase(nc, S, a, agg):
    with Phase(nc, "node1") as ph:
        norm_buffers(ph)
        M = 32
        w2 = ph.sb("w2", [P, 2, D])
        u1 = ph.sb("u1", [P, 2, 2 * D])
        u2 = ph.sb("u2", [P, 2, D])
        b2 = ph.sb("b2", [1, D])
        c1 = ph.sb("c1", [P, 2])
        c2 = ph.sb("c2", [P, D])
        up = ph.sb("up", [P, D])
        deg = ph.sb("deg", [1, KB * P])
        xc = ph.sb("xc", [P, KB, D])
        xT = ph.sb("xT", [P, KB, P])
        y = ph.sb("y", [P, KB, D])
        mT = y[:]
        uT = ph.sb("uT", [P, 2, KB, P])
        ps = [ph.bank(f"ps{k}") for k in range(8)]
        names = ("s_w", "s_up", "s_deg", "s_xc", "s_xT", "s_xTc", "s_m", "s_mc", "s_u", "s_uc", "s_y", "s_v", "s_n",
                 "s_T2", "s_T2c", "s_t", "s_tc", "s_out")
        (s_w, s_up, s_deg, s_xc, s_xT, s_xTc, s_m, s_mc, s_u, s_uc, s_y, s_v, s_n,
         s_T2, s_T2c, s_t, s_tc, s_out) = (ph.sem(n) for n in names)
        block = ph.block()
        cols = (slice(0, 4), slice(4, KB))

        @block.sync
        def _(sp):
            sp.wait_ge(s_up, 1)
            for q in range(2):
                rows = slice(q * D, (q + 1) * D)
                sp.dma_start(w2[:, q, :], a.L1_gnn_msg_W2[rows, :]).then_inc(s_w, 16)
                sp.dma_start(u1[:, q, :], a.L1_gnn_upd_W1[rows, :]).then_inc(s_w, 16)
                sp.dma_start(u2[:, q, :], a.L1_gnn_upd_W2[rows, :]).then_inc(s_w, 16)
            sp.dma_start(b2[:], a.L1_gnn_msg_b2.rearrange("(a d) -> a d", a=1)).then_inc(s_w, 16)
            sp.dma_start(c1[:], a.L1_gnn_upd_b1.rearrange("(q d) -> d q", q=2),
                         allow_slow_non_contiguous=True).then_inc(s_w, 16)
            sp.dma_start(c2[:], a.L1_gnn_upd_b2.rearrange("(a d) -> a d", a=1).to_broadcast([P, D])).then_inc(s_w, 16)
            sp.dma_start(up[0:M, 0:M], a.L2_gnn_W_up_s).then_inc(s_w, 16)
            for q in range(3):
                sp.dma_start(up[M + q:M + q + 3 * M - 2:3, M + q * M:M + (q + 1) * M], a.L2_gnn_W_up_v).then_inc(s_w, 16)
            with sp.Fori(0, NIT) as i:
                sp.wait_ge(s_m, i)
                sp.dma_start(deg[:], S.deg_rows[0:1, bass.ds(i * (KB * P), KB * P)]).then_inc(s_deg, 16)
                sp.wait_ge(s_tc, 2 * i + 2)
                sp.dma_start(S.tab_2.rearrange("(k p) d -> p k d", p=P)[:, bass.ds(i * KB, KB), :],
                             y[:]).then_inc(s_out, 16)
            sp.wait_ge(s_out, 16 * NIT)

        @block.gpsimd
        def _(pool):
            pool.memset(up[:], 0.0).then_inc(s_up, 1)
            pool.memset(ph.ln.eps[:], EPS).then_inc(ph.ln.s_eps, 1)

        @block.tensor
        def _(pe):
            pe.wait_ge(s_w, 13 * 16)
            pe.wait_ge(s_up, 1)
            with pe.Fori(0, NIT) as i:
                pe.wait_ge(s_xc, i + 1)
                pe.wait_ge(s_tc, 2 * i)
                for k in range(KB):
                    bank, c = blocks_of(ps[0], ps[1], k)
                    last = pe.transpose(bank[:, c:c + P], xc[:, k, :], S.ident[:])
                last.then_inc(s_xT, 1)
                pe.wait_ge(s_deg, 16 * i + 16)
                at = i * KB
                for hf, n in ((0, 4), (1, 3)):
                    out = ps[2 + hf][:, 0:n * P]
                    for q in range(2):
                        pe.matmul(out, w2[:, q, :], agg[:, bass.ds(at + 4 * hf, n), q * D:(q + 1) * D],
                                  start=(q == 0), stop=False)
                    last = pe.matmul(out, b2[:], deg[0:1, hf * 4 * P:(hf * 4 + n) * P], start=False, stop=True)
                last.then_inc(s_m, 1)
                pe.wait_ge(s_mc, 2 * i + 2)
                pe.wait_ge(s_xTc, 2 * i + 2)
                for q in range(2):
                    for hf, n in ((0, 4), (1, 3)):
                        out = ps[4 + 2 * q + hf][:, 0:n * P]
                        w = slice(q * D, (q + 1) * D)
                        pe.matmul(out, u1[:, 0, w], xT[:, cols[hf], :].rearrange("p k e -> p (k e)"), start=True, stop=False)
                        last = pe.matmul(out, u1[:, 1, w], mT[:, cols[hf], :].rearrange("p k e -> p (k e)"),
                                         start=False, stop=True)
                last.then_inc(s_u, 1)
                pe.wait_ge(s_uc, 4 * i + 4)
                for k in range(KB):
                    bank, c = blocks_of(ps[0], ps[1], k)
                    pe.matmul(bank[:, c:c + D], uT[:, 0, k, :], u2[:, 0, :], start=True, stop=False)
                    last = pe.matmul(bank[:, c:c + D], uT[:, 1, k, :], u2[:, 1, :], start=False, stop=True)
                last.then_inc(s_y, 1)
                pe.wait_ge(s_n, i + 1)
                for k in range(KB):
                    bank, c = blocks_of(ps[2], ps[3], k)
                    last = pe.transpose(bank[:, c:c + P], xc[:, k, :], S.ident[:])
                last.then_inc(s_T2, 1)
                pe.wait_ge(s_T2c, 2 * i + 2)
                for k in range(KB):
                    bank, c = blocks_of(ps[4], ps[5], k)
                    last = pe.matmul(bank[:, c:c + D], xT[:, k, :], up[:], start=True, stop=True)
                last.then_inc(s_t, 1)

        @block.scalar
        def _(act):
            def copy2(dst, b0, b1, done, scale=1.0):
                for hf, (bank, n) in enumerate(((b0, 4), (b1, 3))):
                    act.activation(dst[:, cols[hf], :].rearrange("p k e -> p (k e)"), bank[:, 0:n * P], ACT.Copy,
                                   scale=scale).then_inc(done, 1)
            with act.Fori(0, NIT) as i:
                act.wait_ge(s_xT, i + 1)
                copy2(xT, ps[0], ps[1], s_xTc)
                act.wait_ge(s_m, i + 1)
                act.wait_ge(s_out, 16 * i)
                copy2(mT, ps[2], ps[3], s_mc)
                act.wait_ge(s_u, i + 1)
                for q in range(2):
                    for hf, n in ((0, 4), (1, 3)):
                        act.activation(uT[:, q, cols[hf], :].rearrange("p k e -> p (k e)"), ps[4 + 2 * q + hf][:, 0:n * P],
                                       ACT.Silu, bias=c1[:, q:q + 1]).then_inc(s_uc, 1)
                root(act, ph, i)
                act.wait_ge(s_T2, i + 1)
                copy2(xT, ps[2], ps[3], s_T2c)
                act.wait_ge(s_t, i + 1)
                copy2(y, ps[4], ps[5], s_tc, scale=M ** -0.5)

        @block.vector
        def _(v):
            v.wait_ge(s_w, 13 * 16)
            VN = 8
            with v.Fori(0, NIT) as i:
                rows = S.x[:, bass.ds(i * KB, KB), :]
                v.wait_ge(s_T2, i)
                v.tensor_scalar(xc[:], rows, 1.0, None, ALU.mult).then_inc(s_xc, 1)
                n = VN * i
                v.wait_ge(s_y, i + 1)
                v.wait_ge(s_xc, i + 1)
                for hf, k in ((0, 4), (1, 3)):
                    last = v.scalar_tensor_tensor(y[:, cols[hf], :], xc[:, cols[hf], :], 2.0,
                                                  ps[hf][:, 0:k * P].rearrange("p (k d) -> p k d", k=k),
                                                  ALU.mult, ALU.add)
                last.then_inc(s_v, 1)
                v.wait_ge(s_v, n + 1)
                v.tensor_tensor(y[:], y[:], c2[:].rearrange("p (a d) -> p a d", a=1).to_broadcast([P, KB, D]),
                                ALU.add).then_inc(s_v, 1)
                v.wait_ge(s_v, n + 2)
                ph.ln.turn = i + 1
                n = normalize(v, ph, y[:], xc[:], s_v, n + 2)
                v.wait_ge(s_v, n)
                v.tensor_scalar(rows, xc[:], 1.0, None, ALU.mult).then_inc(s_n, 1)
                v.wait_ge(s_n, i + 1)


def edge2_phase(nc, S, a, agg):
    with Phase(nc, "edge2") as ph:
        M = 32
        R0, RN = 50, 12
        pl = ph.sbs("pl", NB, [P, G2, PC])
        ix = ph.sbs("ix", NB, [P, G2], I32)
        sv = ph.sbs("sv", NB, [P, G2, D])
        oh = ph.sbs("oh", 2, [P, G2, P])
        rT = ph.sbs("rT", 2, [P, G2 * P])
        hr = ph.sbs("hr", 2, [P, G2 * P])
        vy = ph.sbs("vy", 2, [P, G2, 3, M])
        dot = ph.sbs("dot", 2, [P, 2, G2, M])
        su = ph.sbs("su", 2, [P, G2, M])
        m = ph.sbs("m", 2, [P, G2, 2 * D])
        wr1 = ph.sb("wr1", [P, 8])
        wr2 = ph.sb("wr2", [P, D])
        psT = [ph.bank(f"psT{k}") for k in range(2)]
        psR = [ph.bank(f"psR{k}") for k in range(2)]
        psW = [ph.bank(f"psW{k}") for k in range(2)]
        psA = [ph.bank(f"psA{k}") for k in range(2)]
        s_w, s_turn, s_zero, s_c, s_go = (ph.sem(n) for n in ("s_w", "s_turn", "s_zero", "s_c", "s_go"))
        s_half, s_acc = ph.sems("s_half"), ph.sems("s_acc")
        s_rec, s_ix, s_got, s_oh = (ph.sems(n) for n in ("s_rec", "s_ix", "s_got", "s_oh"))
        s_T, s_TT, s_R, s_hr, s_W, s_m, s_C = (ph.sems(n) for n in ("s_T", "s_TT", "s_R", "s_hr", "s_W", "s_m", "s_C"))
        block = ph.block()
        GT = NT // G2
        rec = S.records.rearrange("(p j) c -> p j c", p=P)

        @block.sync
        def _(sp):
            sp.wait_ge(s_zero, 2)
            sp.dma_start(wr1[4:RN, :], a.L2_gnn_W_r1).then_inc(s_w, 16)
            sp.dma_start(wr2[0:8, :], a.L2_gnn_W_r2).then_inc(s_w, 16)

            def step(s, g, b, r):
                wait(sp, s_m[b], r)
                sp.dma_start(pl[b][:], rec[:, bass.ds(g * G2, G2), :]).then_inc(s_rec[b], 16)
            runs(GT, [0], NB, sp, step)

        @block.gpsimd
        def _(pool):
            runs(GT, [0], NB, pool,
                 lambda s, g, b, r: gather_on(pool, b, ix, sv, S.tab_2, s_ix, s_got, s_turn, r))

        @block.vector
        def _(v):
            v.memset(agg[:], 0.0).then_inc(s_zero, 1)
            v.memset(wr1[:], 0.0).then_inc(s_zero, 1)
            v.wait_ge(s_w, 32)
            v.tensor_scalar(wr2[0:8, :], wr2[0:8, :], 8 ** -0.5, None, ALU.mult).then_inc(s_zero, 1)
            v.wait_ge(s_zero, 3)
            v.tensor_scalar(wr2[0:8, 3 * M:], wr2[0:8, 3 * M:], 3 ** -0.5, None, ALU.mult).then_inc(s_zero, 1)
            v.wait_ge(s_zero, 4)

            def step(s, g, b, r):
                o, n = two_before(b, r)
                p = b % 2
                if s == 0:
                    wait(v, s_got[b], r * 16 * G2)
                    wait(v, s_m[b], r)
                    v.tensor_scalar(ix[b][:], S.e_src[:, bass.ds(g * G2, G2)], 1.0, None, ALU.mult).then_inc(s_ix[b], 1)
                elif s == 1:
                    wait(v, s_C[o], n)
                    for k in range(G2):
                        last = v.tensor_scalar(oh[p][:, k, :], S.iota[:], S.e_dl[:, bass.ds(g * G2 + k, 1)], None,
                                               ALU.is_equal)
                    last.then_inc(s_oh[b], 1)
                elif s == 2:
                    v.wait_ge(s_W[b], r + 1)
                    v.wait_ge(s_got[b], (r + 1) * 16 * G2)
                    wait(v, s_m[o], n)
                    wait(v, s_C[o], n)
                    w = psW[p][:, 0:G2 * D].rearrange("p (k c) -> p k c", k=G2)
                    send, mo = sv[b], m[p]
                    ss = send[:, :, 0:M]
                    vs = send[:, :, M:D].rearrange("p k (i m) -> p k i m", i=3)
                    yv = pl[b][:, :, R0 + 1:R0 + 4].rearrange("p k (i a) -> p k i a", a=1).to_broadcast([P, G2, 3, M])
                    vo = mo[:, :, 2 * M:].rearrange("p k (i m) -> p k i m", i=3)

                    def thrice(t):
                        return t.rearrange("p k (a m) -> p k a m", a=1).to_broadcast([P, G2, 3, M])
                    n0 = g * 4
                    v.tensor_tensor(vy[p][:], vs, yv, ALU.mult)
                    v.tensor_tensor(su[p][:], w[:, :, 2 * M:3 * M], ss, ALU.mult).then_inc(s_c, 1)
                    v.tensor_tensor(mo[:, :, 0:M], w[:, :, 0:M], ss, ALU.mult)
                    v.wait_ge(s_c, n0 + 1)
                    v.tensor_tensor(dot[p][:, 0], vy[p][:, :, 0, :], vy[p][:, :, 1, :], ALU.add).then_inc(s_c, 1)
                    v.tensor_tensor(vo[:, :, :, 0:M], thrice(w[:, :, M:2 * M]), vs, ALU.mult)
                    v.wait_ge(s_c, n0 + 2)
                    v.tensor_tensor(dot[p][:, 1], dot[p][:, 0], vy[p][:, :, 2, :], ALU.add).then_inc(s_c, 1)
                    v.tensor_tensor(vo[:, :, :, M:], thrice(su[p][:]), yv, ALU.mult).then_inc(s_c, 1)
                    v.wait_ge(s_c, n0 + 4)
                    v.tensor_tensor(mo[:, :, M:2 * M], w[:, :, 3 * M:], dot[p][:, 1], ALU.mult).then_inc(s_m[b], 1)
                else:
                    add_to_blocks(v, S, agg, psA, b, r, g, s_C, s_half, s_acc)
            runs(GT, [0, 3, 3, 4], NB, v, step)

        @block.scalar
        def _(act):
            def step(s, g, b, r):
                o, n = two_before(b, r)
                if s == 0:
                    act.wait_ge(s_T[b], r + 1)
                    wait(act, s_R[o], n)
                    act.activation(rT[b % 2][0:RN, :], psT[b % 2][0:RN, 0:G2 * P], ACT.Copy).then_inc(s_TT[b], 1)
                else:
                    act.wait_ge(s_R[b], r + 1)
                    wait(act, s_W[o], n)
                    act.activation(hr[b % 2][0:8, :], psR[b % 2][0:8, 0:G2 * P], ACT.Silu,
                                   scale=8 ** -0.5).then_inc(s_hr[b], 1)
            runs(GT, [1, 2], NB, act, step)

        @block.tensor
        def _(pe):
            pe.wait_ge(s_zero, 4)

            def step(s, g, b, r):
                o, n = two_before(b, r)
                if s == 0:
                    pe.wait_ge(s_m[b], r + 1)
                    pe.wait_ge(s_oh[b], r + 1)
                    wait(pe, s_acc[o], n)
                    for k in range(G2):
                        for q in range(2):
                            c = k * 2 * D + q * D
                            last = pe.matmul(psA[b % 2][:, c:c + D], m[b % 2][:, k, q * D:(q + 1) * D],
                                             oh[b % 2][:, k, :], start=True, stop=True)
                    last.then_inc(s_C[b], 1)
                elif s == 1:
                    pe.wait_ge(s_hr[b], r + 1)
                    wait(pe, s_m[o], n)
                    for k in range(G2):
                        last = pe.matmul(psW[b % 2][:, k * D:(k + 1) * D], hr[b % 2][0:8, k * P:(k + 1) * P],
                                         wr2[0:8, :], start=True, stop=True)
                    last.then_inc(s_W[b], 1)
                elif s == 2:
                    pe.wait_ge(s_TT[b], r + 1)
                    wait(pe, s_hr[o], n)
                    pe.sem_inc(s_go, 1)
                    pe.matmul(psR[b % 2][0:8, 0:G2 * P], wr1[0:RN, :], rT[b % 2][0:RN, :], start=True,
                              stop=True).then_inc(s_R[b], 1)
                else:
                    pe.wait_ge(s_rec[b], (r + 1) * 16)
                    wait(pe, s_TT[o], n)
                    for k in range(G2):
                        last = pe.transpose(psT[b % 2][0:RN, k * P:(k + 1) * P], pl[b][:, k, R0:R0 + RN], S.ident[:])
                    last.then_inc(s_T[b], 1)
            runs(GT, [4, 3, 2, 1], NB, pe, step)


def node2_phase(nc, S, a, agg):
    with Phase(nc, "node2") as ph:
        M, Z = 32, 160
        NS = 4
        wd = ph.sb("wd", [P, 2, Z])
        ws = ph.sb("ws", [P, NS, Z])
        kind = ph.sb("kind", [P, NBLK], I32)
        mask = ph.sb("mask", [P, NS, NBLK])
        xc = ph.sb("xc", [P, KB, D])
        xm = ph.sb("xm", [P, KB, D])
        norm_buffers(ph, sq=xm)
        ac = ph.sb("ac", [P, KB, 2 * D])
        xmT = ph.sbs("xmT", 2, [P, KB, P])
        z = ph.sb("z", [P, KB, Z])
        y = ac[:, :, 0:D]
        ps = [ph.bank(f"ps{k}") for k in range(8)]
        names = ("s_w", "s_zero", "s_k", "s_xc", "s_ac", "s_xm", "s_T", "s_Tc", "s_z", "s_zc", "s_v", "s_n", "s_out")
        (s_w, s_zero, s_k, s_xc, s_ac, s_xm, s_T, s_Tc, s_z, s_zc, s_v, s_n, s_out) = (ph.sem(n) for n in names)
        block = ph.block()
        cols = (slice(0, 4), slice(4, KB))

        @block.sync
        def _(sp):
            sp.wait_ge(s_zero, 3)
            sp.dma_start(wd[0:2 * M, 0, 0:2 * M], a.L2_gnn_W_dn_s).then_inc(s_w, 16)
            sp.dma_start(wd[2 * M:, 0, 2 * M:3 * M], a.L2_gnn_W_dn_v).then_inc(s_w, 16)
            sp.dma_start(wd[0:2 * M, 1, 3 * M:4 * M], a.L2_gnn_W_dn_v).then_inc(s_w, 16)
            sp.dma_start(wd[2 * M:, 1, 4 * M:5 * M], a.L2_gnn_W_dn_v).then_inc(s_w, 16)
            for k in range(NS):
                sp.dma_start(ws[0:M, k, 0:2 * M], a.L2_gnn_W_sk_s[k]).then_inc(s_w, 16)
                for q in range(3):
                    sp.dma_start(ws[M + q:M + q + 3 * M - 2:3, k, (2 + q) * M:(3 + q) * M],
                                 a.L2_gnn_W_sk_v[k]).then_inc(s_w, 16)
            sp.dma_start(kind[:, 0:NBLK - 1], a.node_type_4[0:(NBLK - 1) * P].rearrange("(b p) -> p b", p=P),
                         allow_slow_non_contiguous=True).then_inc(s_k, 16)
            sp.dma_start(kind[0:NLAST, NBLK - 1:], a.node_type_4[(NBLK - 1) * P:N].rearrange("(p b) -> p b", b=1),
                         allow_slow_non_contiguous=True).then_inc(s_k, 16)
            with sp.Fori(0, NIT) as i:
                sp.wait_ge(s_n, i + 1)
                sp.dma_start(S.tab_3.rearrange("(k p) d -> p k d", p=P)[:, bass.ds(i * KB, KB), :],
                             xc[:]).then_inc(s_out, 16)
            sp.wait_ge(s_out, 16 * NIT)

        @block.gpsimd
        def _(pool):
            pool.memset(wd[:], 0.0).then_inc(s_zero, 1)
            pool.memset(ws[:], 0.0).then_inc(s_zero, 1)
            pool.memset(kind[:], 0).then_inc(s_zero, 1)
            pool.memset(ph.ln.eps[:], EPS).then_inc(ph.ln.s_eps, 1)

        @block.tensor
        def _(pe):
            pe.wait_ge(s_w, 20 * 16)
            pe.wait_ge(s_v, 1)
            with pe.Fori(0, NIT) as i:
                def turn(k):
                    pe.wait_ge(s_xm, NS * i + k + 1)
                    pe.wait_ge(s_Tc, 2 * (NS * i + k))
                    for j in range(KB):
                        bank, c = blocks_of(ps[0], ps[1], j)
                        last = pe.transpose(bank[:, c:c + P], xm[:, j, :], S.ident[:])
                    last.then_inc(s_T, 1)

                def z_of(j):
                    return ps[2 + j // 3][:, (j % 3) * Z:(j % 3 + 1) * Z]
                turn(0)
                pe.wait_ge(s_ac, i + 1)
                pe.wait_ge(s_zc, 3 * i)
                for q in range(2):
                    for j in range(KB):
                        pe.matmul(z_of(j), ac[:, j, q * D:(q + 1) * D], wd[:, q, :], start=(q == 0 and j % 3 == 0),
                                  stop=False, skip_group_check=True)
                for k in range(NS):
                    if k + 1 < NS:
                        turn(k + 1)
                    pe.wait_ge(s_Tc, 2 * (NS * i + k + 1))
                    for j in range(KB):
                        last = pe.matmul(z_of(j), xmT[k % 2][:, j, :], ws[:, k, :], start=False, stop=(k == NS - 1),
                                         skip_group_check=True)
                last.then_inc(s_z, 1)

        @block.scalar
        def _(act):
            with act.Fori(0, NIT) as i:
                act.wait_ge(s_z, i)
                for k in range(NS):
                    act.wait_ge(s_T, NS * i + k + 1)
                    for hf, n in ((0, 4), (1, 3)):
                        act.activation(xmT[k % 2][:, cols[hf], :].rearrange("p k e -> p (k e)"), ps[hf][:, 0:n * P],
                                       ACT.Copy).then_inc(s_Tc, 1)
                act.wait_ge(s_z, i + 1)
                act.wait_ge(s_n, i)
                for q, n in enumerate((3, 3, 1)):
                    src = ps[2 + q][:, 0:n * Z].rearrange("p (k c) -> p k c", k=n)
                    act.activation(z[:, 3 * q:3 * q + n, 0:2 * M], src[:, :, 0:2 * M], ACT.Silu)
                    act.activation(z[:, 3 * q:3 * q + n, 2 * M:], src[:, :, 2 * M:], ACT.Copy).then_inc(s_zc, 1)
                root(act, ph, i)

        @block.vector
        def _(v):
            v.wait_ge(s_w, 20 * 16)
            v.wait_ge(s_k, 32)
            v.tensor_scalar(wd[:], wd[:], 1.0 / 64, None, ALU.mult).then_inc(s_v, 1)
            for k in range(NS):
                v.tensor_scalar(mask[:, k, :], kind[:], float(k), 0.5 * M ** -0.5, ALU.is_equal, ALU.mult).then_inc(s_v, 1)
            v.wait_ge(s_v, 5)
            VN = 9
            with v.Fori(0, NIT) as i:
                blocks = bass.ds(i * KB, KB)
                rows = S.x[:, blocks, :]
                v.wait_ge(s_out, 16 * i)
                v.tensor_scalar(xc[:], rows, 1.0, None, ALU.mult).then_inc(s_xc, 1)
                v.wait_ge(s_z, i)
                v.tensor_scalar(ac[:], agg[:, blocks, :], 1.0, None, ALU.mult).then_inc(s_ac, 1)
                v.wait_ge(s_xc, i + 1)
                for k in range(NS):
                    v.wait_ge(s_T, NS * i + k)
                    v.tensor_tensor(xm[:], xc[:], mask[:, k, blocks].rearrange("p (k a) -> p k a", a=1)
                                    .to_broadcast([P, KB, D]), ALU.mult).then_inc(s_xm, 1)
                v.wait_ge(s_zc, 3 * i + 3)
                n = VN * i + 5
                v.tensor_tensor(y[:, :, 0:M], z[:, :, 0:M], xc[:, :, 0:M], ALU.add)
                for q in range(3):
                    last = v.tensor_tensor(y[:, :, M + q:M + q + 3 * M - 2:3], z[:, :, (2 + q) * M:(3 + q) * M],
                                           z[:, :, M:2 * M], ALU.mult)
                last.then_inc(s_v, 1)
                v.wait_ge(s_v, n + 1)
                v.tensor_tensor(y[:, :, M:], y[:, :, M:], xc[:, :, M:], ALU.add).then_inc(s_v, 1)
                v.wait_ge(s_v, n + 2)
                ph.ln.turn = i + 1
                n = normalize(v, ph, y, xc[:], s_v, n + 2)
                v.wait_ge(s_v, n)
                v.tensor_scalar(rows, xc[:], 1.0, None, ALU.mult).then_inc(s_v, 1)
                v.wait_ge(s_v, n + 1)
                v.sem_inc(s_n, 1)


def edge3_phase(nc, S, a, agg):
    with Phase(nc, "edge3") as ph:
        ix = ph.sbs("ix", NB, [P, G2], I32)
        xs = ph.sbs("xs", NB, [P, G2, D])
        oh = ph.sbs("oh", 2, [P, G2, 2, P])
        psA = [ph.bank(f"psA{k}") for k in range(2)]
        s_turn, s_zero = (ph.sem(n) for n in ("s_turn", "s_zero"))
        s_half, s_acc = ph.sems("s_half"), ph.sems("s_acc")
        s_ix, s_got, s_oh, s_C = (ph.sems(n) for n in ("s_ix", "s_got", "s_oh", "s_C"))
        block = ph.block()
        GT = NT // G2

        @block.gpsimd
        def _(pool):
            runs(GT, [0], NB, pool,
                 lambda s, g, b, r: gather_on(pool, b, ix, xs, S.tab_3, s_ix, s_got, s_turn, r))

        @block.vector
        def _(v):
            v.memset(agg[:], 0.0).then_inc(s_zero, 1)
            v.scalar_tensor_tensor(S.e_dl[:], S.e_dl[:], -1.0, S.e_dl0[:], ALU.add, ALU.subtract).then_inc(s_zero, 1)
            v.wait_ge(s_zero, 2)

            def step(s, g, b, r):
                o, n = two_before(b, r)
                if s == 0:
                    wait(v, s_got[b], r * 16 * G2)
                    wait(v, s_C[b], r)
                    v.tensor_scalar(ix[b][:], S.e_src[:, bass.ds(g * G2, G2)], 1.0, None, ALU.mult).then_inc(s_ix[b], 1)
                elif s == 1:
                    wait(v, s_C[o], n)
                    for k in range(G2):
                        at = bass.ds(g * G2 + k, 1)
                        v.tensor_scalar(oh[b % 2][:, k, 0, :], S.iota[:], S.e_dl0[:, at], None, ALU.is_equal)
                        last = v.tensor_scalar(oh[b % 2][:, k, 1, :], S.iota[:], S.e_dl[:, at], None, ALU.is_equal)
                    last.then_inc(s_oh[b], 1)
                else:
                    add_to_blocks(v, S, agg, psA, b, r, g, s_C, s_half, s_acc)
            runs(GT, [3, 0, 2], NB, v, lambda s, g, b, r: step((2, 0, 1)[s], g, b, r))

        @block.tensor
        def _(pe):
            def step(s, g, b, r):
                o, n = two_before(b, r)
                pe.wait_ge(s_oh[b], r + 1)
                pe.wait_ge(s_got[b], (r + 1) * 16 * G2)
                wait(pe, s_acc[o], n)
                for k in range(G2):
                    last = pe.matmul(psA[b % 2][:, k * 2 * D:(k + 1) * 2 * D], xs[b][:, k, :],
                                     oh[b % 2][:, k].rearrange("p t n -> p (t n)"), start=True, stop=True)
                last.then_inc(s_C[b], 1)
            runs(GT, [2], NB, pe, step)


def node3_phase(nc, S, a, agg, out):
    with Phase(nc, "node3") as ph:
        norm_buffers(ph)
        w = ph.sb("w", [P, 3, D])
        wT = ph.sb("wT", [P, 3, D])
        bd = ph.sb("bd", [1, 2, D])
        dif = ph.sb("dif", [1, D])
        bias = ph.sb("bias", [3, D])
        deg = ph.sb("deg", [3, KB * P])
        xc = ph.sb("xc", [P, KB, D])
        ac = ph.sb("ac", [P, KB, 2 * D])
        xT = ph.sb("xT", [P, KB, P])
        y = ph.sb("y", [P, KB, D])
        ps = [ph.bank(f"ps{k}") for k in range(4)]
        names = ("s_w", "s_b", "s_wT", "s_wc", "s_dif", "s_deg", "s_xc", "s_ac", "s_T", "s_Tc", "s_y", "s_v", "s_n", "s_out")
        (s_w, s_b, s_wT, s_wc, s_dif, s_deg, s_xc, s_ac, s_T, s_Tc, s_y, s_v, s_n, s_out) = (ph.sem(n) for n in names)
        block = ph.block()
        cols = (slice(0, 4), slice(4, KB))

        def row(t):
            return t.rearrange("(a d) -> a d", a=1)

        @block.sync
        def _(sp):
            for q, t in enumerate((a.L3_gnn_W_data, a.L3_gnn_W_control, a.L3_gnn_W_self)):
                sp.dma_start(w[:, q, :], t).then_inc(s_w, 16)
            sp.dma_start(bd[:, 0, :], row(a.L3_gnn_b_data)).then_inc(s_w, 16)
            sp.dma_start(bd[:, 1, :], row(a.L3_gnn_b_control)).then_inc(s_w, 16)
            sp.dma_start(bias[0:1, :], row(a.L3_gnn_b_control)).then_inc(s_b, 16)
            sp.dma_start(bias[2:3, :], row(a.L3_gnn_b_self)).then_inc(s_b, 16)
            sp.wait_ge(s_dif, 1)
            sp.dma_start(bias[1:2, :], dif[:]).then_inc(s_b, 16)
            with sp.Fori(0, NIT - 1) as i:
                sp.wait_ge(s_y, i)
                sp.dma_start(deg[:], S.deg_rows[:, bass.ds(i * (KB * P), KB * P)]).then_inc(s_deg, 16)
                sp.wait_ge(s_n, i + 1)
                sp.dma_start(out[0:(NBLK - KB) * P, :].rearrange("(k p) d -> p k d", p=P)[:, bass.ds(i * KB, KB), :],
                             xc[:]).then_inc(s_out, 16)
            i = NIT - 1
            sp.wait_ge(s_y, i)
            sp.dma_start(deg[:], S.deg_rows[:, i * KB * P:]).then_inc(s_deg, 16)
            sp.wait_ge(s_n, i + 1)
            sp.dma_start(out[i * KB * P:(NBLK - 1) * P, :].rearrange("(k p) d -> p k d", p=P),
                         xc[:, 0:KB - 1, :]).then_inc(s_out, 16)
            sp.dma_start(out[(NBLK - 1) * P:N, :], xc[0:NLAST, KB - 1, :]).then_inc(s_out, 16)
            sp.wait_ge(s_out, 16 * (NIT + 1))

        @block.gpsimd
        def _(pool):
            pool.memset(ph.ln.eps[:], EPS).then_inc(ph.ln.s_eps, 1)

        @block.tensor
        def _(pe):
            pe.wait_ge(s_w, 80)
            for q in range(3):
                last = pe.transpose(ps[0][:, q * D:(q + 1) * D], w[:, q, :], S.ident[:])
            last.then_inc(s_wT, 1)
            pe.wait_ge(s_wc, 1)
            pe.wait_ge(s_b, 48)
            with pe.Fori(0, NIT) as i:
                pe.wait_ge(s_xc, i + 1)
                for k in range(KB):
                    bank, c = blocks_of(ps[0], ps[1], k)
                    last = pe.transpose(bank[:, c:c + P], xc[:, k, :], S.ident[:])
                last.then_inc(s_T, 1)
                pe.wait_ge(s_Tc, 2 * i + 2)
                pe.wait_ge(s_ac, i + 1)
                pe.wait_ge(s_deg, 16 * i + 16)
                for k in range(KB):
                    bank, c = blocks_of(ps[2], ps[3], k)
                    o = bank[:, c:c + D]
                    pe.matmul(o, ac[:, k, 0:D], wT[:, 0, :], start=True, stop=False)
                    pe.matmul(o, ac[:, k, D:], wT[:, 1, :], start=False, stop=False)
                    pe.matmul(o, xT[:, k, :], wT[:, 2, :], start=False, stop=False)
                    last = pe.matmul(o, deg[:, k * P:(k + 1) * P], bias[:], start=False, stop=True)
                last.then_inc(s_y, 1)

        @block.scalar
        def _(act):
            with act.Fori(0, NIT) as i:
                act.wait_ge(s_T, i + 1)
                for hf, n in ((0, 4), (1, 3)):
                    act.activation(xT[:, cols[hf], :].rearrange("p k e -> p (k e)"), ps[hf][:, 0:n * P],
                                   ACT.Copy).then_inc(s_Tc, 1)
                root(act, ph, i)

        @block.vector
        def _(v):
            v.wait_ge(s_w, 80)
            v.tensor_tensor(dif[:], bd[:, 0, :], bd[:, 1, :], ALU.subtract).then_inc(s_dif, 1)
            v.wait_ge(s_wT, 1)
            v.tensor_copy(wT[:], ps[0][:, 0:3 * D].rearrange("p (q d) -> p q d", q=3)).then_inc(s_wc, 1)
            VN = 7
            with v.Fori(0, NIT) as i:
                blocks = bass.ds(i * KB, KB)
                v.wait_ge(s_out, 16 * i)
                v.tensor_scalar(xc[:], S.x[:, blocks, :], 1.0, None, ALU.mult).then_inc(s_xc, 1)
                v.wait_ge(s_y, i)
                v.tensor_scalar(ac[:], agg[:, blocks, :], 1.0, None, ALU.mult).then_inc(s_ac, 1)
                n = VN * i
                v.wait_ge(s_y, i + 1)
                v.wait_ge(s_xc, i + 1)
                for hf, k in ((0, 4), (1, 3)):
                    last = v.scalar_tensor_tensor(y[:, cols[hf], :], ps[2 + hf][:, 0:k * P].rearrange("p (k d) -> p k d", k=k),
                                                  0.0, xc[:, cols[hf], :], ALU.max, ALU.add)
                last.then_inc(s_v, 1)
                v.wait_ge(s_v, n + 1)
                ph.ln.turn = i + 1
                n = normalize(v, ph, y[:], xc[:], s_v, n + 1)
                v.wait_ge(s_v, n)
                v.sem_inc(s_n, 1)


def program(nc, a, out):
    with ExitStack() as ctx:
        S = Names()

        def dram(name, shape, dt=F32):
            return nc.dram_tensor(name, shape, dt, kind="Internal").ap()

        def sb(c, name, shape, dt=F32):
            return c.enter_context(nc.sbuf_tensor(name, shape, dt))

        S.records = dram("records", (P * NT, PC))
        S.by_src = dram("by_src", (P * TE, XC))
        S.running = dram("running", (P * TE, D))
        S.deg_rows = dram("deg_rows", (3, NBLK * P))
        S.tab_a = dram("tab_a", (NBLK * P, 2 * D))
        S.tab_b = dram("tab_b", (NBLK * P, 2 * D))
        S.tab_2 = dram("tab_2", (NBLK * P, D))
        S.tab_3 = dram("tab_3", (NBLK * P, D))
        S.x = sb(ctx, "x_res", [P, NBLK, D])
        S.iota = sb(ctx, "iota", [P, P])
        S.iota_b = sb(ctx, "iota_b", [P, P], BF16)
        S.ident = sb(ctx, "ident", [P, P])
        S.ident_b = sb(ctx, "ident_b", [P, P], BF16)
        S.lower = sb(ctx, "lower", [P, P])
        S.upper = sb(ctx, "upper", [P, P])
        S.blk = sb(ctx, "blk", [1, NT], I32)
        S.last = sb(ctx, "last", [P, NBLK], I32)
        with ExitStack() as c1:
            S.src_key = sb(c1, "src_key", [P, TE], I32)
            S.dst_key = sb(c1, "dst_key", [P, TE], I32)
            S.key_f = sb(c1, "key_f", [P, TE, 2])
            S.lo = sb(c1, "lo", [P, TE, 2])
            S.hi = sb(c1, "hi", [P, TE, 2])
            S.dst_lo0 = sb(c1, "dst_lo0", [P, TE])
            S.base = sb(c1, "base", [P, 2 * HI])
            count_phase(nc, S, a)
            place_phase(nc, S, a)
        S.e_src = sb(ctx, "e_src", [P, NT], I32)
        S.e_dl = sb(ctx, "e_dl", [P, NT])
        S.e_dl0 = sb(ctx, "e_dl0", [P, NT])
        send_phase(nc, S, a)
        max_phase(nc, S, a)
        node0_phase(nc, S, a)
        agg = sb(ctx, "agg", [P, NBLK, 2 * D])
        edge1_phase(nc, S, a, agg)
        node1_phase(nc, S, a, agg)
        edge2_phase(nc, S, a, agg)
        node2_phase(nc, S, a, agg)
        edge3_phase(nc, S, a, agg)
        node3_phase(nc, S, a, agg, out)


class Inputs:

    def __init__(self, t):
        self.x = t["x"]
        self.src = t["src"]
        self.dst = t["dst"]
        self.edge_attr_4 = t["edge_attr_4"]
        self.edge_attr_50 = t["edge_attr_50"]
        self.edge_attr_8 = t["edge_attr_8"]
        self.edge_type_2 = t["edge_type_2"]
        self.node_type_4 = t["node_type_4"]
        self.L0_gnn_W = t["L0_gnn_W"]
        self.L0_gnn_b = t["L0_gnn_b"]
        self.L1_gnn_msg_W1 = t["L1_gnn_msg_W1"]
        self.L1_gnn_msg_b1 = t["L1_gnn_msg_b1"]
        self.L1_gnn_msg_W2 = t["L1_gnn_msg_W2"]
        self.L1_gnn_msg_b2 = t["L1_gnn_msg_b2"]
        self.L1_gnn_upd_W1 = t["L1_gnn_upd_W1"]
        self.L1_gnn_upd_b1 = t["L1_gnn_upd_b1"]
        self.L1_gnn_upd_W2 = t["L1_gnn_upd_W2"]
        self.L1_gnn_upd_b2 = t["L1_gnn_upd_b2"]
        self.L2_gnn_W_up_s = t["L2_gnn_W_up_s"]
        self.L2_gnn_W_up_v = t["L2_gnn_W_up_v"]
        self.L2_gnn_W_r1 = t["L2_gnn_W_r1"]
        self.L2_gnn_W_r2 = t["L2_gnn_W_r2"]
        self.L2_gnn_W_dn_s = t["L2_gnn_W_dn_s"]
        self.L2_gnn_W_dn_v = t["L2_gnn_W_dn_v"]
        self.L2_gnn_W_sk_s = t["L2_gnn_W_sk_s"]
        self.L2_gnn_W_sk_v = t["L2_gnn_W_sk_v"]
        self.L3_gnn_W_data = t["L3_gnn_W_data"]
        self.L3_gnn_b_data = t["L3_gnn_b_data"]
        self.L3_gnn_W_control = t["L3_gnn_W_control"]
        self.L3_gnn_b_control = t["L3_gnn_b_control"]
        self.L3_gnn_W_self = t["L3_gnn_W_self"]
        self.L3_gnn_b_self = t["L3_gnn_b_self"]


_INS = ['x', 'src', 'dst', 'edge_attr_4', 'edge_attr_50', 'edge_attr_8', 'edge_type_2', 'node_type_4',
        'L0_gnn_W', 'L0_gnn_b', 'L1_gnn_msg_W1', 'L1_gnn_msg_b1', 'L1_gnn_msg_W2', 'L1_gnn_msg_b2',
        'L1_gnn_upd_W1', 'L1_gnn_upd_b1', 'L1_gnn_upd_W2', 'L1_gnn_upd_b2', 'L2_gnn_W_up_s', 'L2_gnn_W_up_v',
        'L2_gnn_W_r1', 'L2_gnn_W_r2', 'L2_gnn_W_dn_s', 'L2_gnn_W_dn_v', 'L2_gnn_W_sk_s', 'L2_gnn_W_sk_v',
        'L3_gnn_W_data', 'L3_gnn_b_data', 'L3_gnn_W_control', 'L3_gnn_b_control', 'L3_gnn_W_self', 'L3_gnn_b_self']


def kernel(**inputs):
    import numpy as _np
    import concourse.bacc as _bacc
    from concourse import mybir as _mybir
    from concourse.bass_utils import run_bass_kernel_spmd as _run

    nc = _bacc.Bacc("TRN2", target_bir_lowering=False, num_devices=1)
    arrays, args = {}, {}
    for name in _INS:
        array = _np.ascontiguousarray(inputs[name])
        arrays[f"in_{name}"] = array
        args[name] = nc.dram_tensor(f"in_{name}", array.shape, _mybir.dt.from_np(array.dtype), kind="ExternalInput").ap()
    out = nc.dram_tensor("out_x", (N, D), F32, kind="ExternalOutput").ap()
    program(nc, Inputs(args), out)
    r = _run(nc, [arrays], core_ids=[0])
    return r.results[0]["out_x"]
```

```python
from contextlib import ExitStack

import concourse.bass as bass
from concourse import mybir

F32 = mybir.dt.float32
I32 = mybir.dt.int32
BF16 = mybir.dt.bfloat16
ALU = mybir.AluOpType
ACT = mybir.ActivationFunctionType
AX = mybir.AxisListType

P = 128
N = 12500
E = 200000
D = 128
NBLK = -(-N // P)
NLAST = N - (NBLK - 1) * P
HI = NBLK + 1
PADKEY = NBLK * P
TM = 1560
TE = 1568
TAIL = E - P * TM
NT = 1664
PC = 66
C_SRC, C_SPOS, C_DL, C_DL0 = 62, 63, 64, 65
XC = D + 1
FAR = 1 << 20
FARPOS = float(1 << 26)
NB = 4
G2 = 2
KB = 7
EPS = 1e-5
STEP = 2e34


def runs(groups, lags, depth, eng, step):
    assert groups % depth == 0 and max(lags) <= depth
    for turn in range(depth):
        for s, lag in enumerate(lags):
            if turn >= lag:
                step(s, turn - lag, (turn - lag) % depth, (turn - lag) // depth)
    with eng.Fori(1, groups // depth) as i:
        for turn in range(depth):
            for s, lag in enumerate(lags):
                back = (lag - turn + depth - 1) // depth if lag > turn else 0
                step(s, i * depth + (turn - lag), (turn - lag) % depth, i - back)
    for turn in range(groups, groups + max(lags)):
        for s, lag in enumerate(lags):
            if turn - lag < groups:
                step(s, turn - lag, (turn - lag) % depth, (turn - lag) // depth)


def wait(eng, sem, value):
    if not isinstance(value, int) or value > 0:
        eng.wait_ge(sem, value)


def before(b, r, n, depth):
    return (b - n, r + 1) if b >= n else (b + depth - n, r)


def two_before(b, r, depth=NB):
    return before(b, r, 2, depth)


class Names:
    pass


class Phase:

    def __init__(self, nc, tag):
        self.nc, self.tag, self.ctx, self.semaphores = nc, tag, ExitStack(), []

    def __enter__(self):
        return self

    def __exit__(self, *a):
        self.ctx.close()
        self.nc.clear_and_free_semaphores(self.semaphores)
        self.nc.all_engine_barrier()

    def sb(self, name, shape, dt=F32):
        return self.ctx.enter_context(self.nc.sbuf_tensor(f"{self.tag}_{name}", shape, dt))

    def sbs(self, name, n, shape, dt=F32):
        return [self.sb(f"{name}{k}", shape, dt) for k in range(n)]

    def bank(self, name, dt=F32):
        cols = 512 if dt == F32 else 1024
        return self.ctx.enter_context(self.nc.psum_tensor(f"{self.tag}_{name}", [P, cols], dt))

    def sem(self, name):
        self.semaphores.append(self.nc.alloc_semaphore(f"{self.tag}_{name}"))
        return self.semaphores[-1]

    def sems(self, name, n=NB):
        return [self.sem(f"{name}{k}") for k in range(n)]

    def block(self):
        return self.ctx.enter_context(self.nc.Block())


def count_phase(nc, S, a):
    with Phase(nc, "count") as ph:
        zb = ph.sb("zb", [P, 2 * HI], BF16)
        tmpl = ph.sb("tmpl", [P, 26, PC])
        zx = ph.sb("zx", [P, 6, XC])
        types = ph.sb("types", [P, TE], I32)
        f0 = ph.sb("f0", [P, TE])
        dhi0 = ph.sb("dhi0", [P, TE])
        ti = ph.sb("ti", [P, TE], I32)
        ohd = ph.sbs("ohd", NB, [P, G2, P + 2 * HI], BF16)
        ohs = ph.sbs("ohs", NB, [P, G2, P + HI], BF16)
        dist = ph.sbs("dist", NB, [P, G2, HI], BF16)
        hi = ph.sbs("hi", NB, [P, G2])
        cnt = ph.sb("cnt", [P, 3, HI])
        ones = ph.sb("ones", [P, P])
        onec = ph.sb("onec", [P, NBLK])
        tot = ph.sb("tot", [P, 2, NBLK])
        toti = ph.sb("toti", [P, NBLK], I32)
        ex = ph.sb("ex", [P, 2, NBLK])
        cum = ph.sb("cum", [P, 2, NBLK])
        cumT = ph.sb("cumT", [P, 1])
        iotaj = ph.sb("iotaj", [P, NT])
        cmp = ph.sb("cmp", [P, NT])
        degT = ph.sb("degT", [P, 2, P])
        one_row = ph.sb("one_row", [NBLK, P])
        en = ph.sb("en", [P, 3, NBLK])
        eni = ph.sb("eni", [P, 3, NBLK], I32)
        psD, psS = ph.bank("psD"), ph.bank("psS")
        psA, psB, psC = ph.bank("psA"), ph.bank("psB"), ph.bank("psC")
        s_const, s_load, s_key, s_tmpl = ph.sem("s_const"), ph.sem("s_load"), ph.sem("s_key"), ph.sem("s_tmpl")
        s_pad, s_fill, s_x, s_xpad = ph.sem("s_pad"), ph.sem("s_fill"), ph.sem("s_x"), ph.sem("s_xpad")
        s_oh, s_free = ph.sems("s_oh"), ph.sems("s_free")
        s_oh_pool, s_oh_act = ph.sems("s_oh_pool"), ph.sems("s_oh_act")
        s_hi, s_go, s_dist = ph.sem("s_hi"), ph.sem("s_go"), ph.sem("s_dist")
        KEYS = 20
        s_hist, s_d, s_pe, s_out = ph.sem("s_hist"), ph.sem("s_d"), ph.sem("s_pe"), ph.sem("s_out")
        block = ph.block()

        @block.sync
        def _(sp):
            sp.wait_ge(s_pad, 4)
            for arr, t in ((a.src, S.src_key), (a.dst, S.dst_key), (a.edge_type_2, types)):
                sp.dma_start(t[:, 0:TM], arr[0:P * TM].rearrange("(p t) -> p t", t=TM)).then_inc(s_load, 16)
                full = TAIL // P
                sp.dma_start(t[:, TM:TM + full],
                             arr[P * TM:P * (TM + full)].rearrange("(t p) -> p t", p=P),
                             allow_slow_non_contiguous=True).then_inc(s_load, 16)
                sp.dma_start(t[0:TAIL - P * full, TM + full:TM + full + 1],
                             arr[P * (TM + full):E].rearrange("(p t) -> p t", t=1),
                             allow_slow_non_contiguous=True).then_inc(s_load, 16)
            sp.dma_start(S.x[:, 0:NBLK - 1, :],
                         a.x[0:(NBLK - 1) * P, :].rearrange("(b p) d -> p b d", p=P)).then_inc(s_x, 16)
            sp.dma_start(S.x[0:NLAST, NBLK - 1, :], a.x[(NBLK - 1) * P:N, :]).then_inc(s_x, 16)
            sp.wait_ge(s_tmpl, 4)
            rec = S.records.rearrange("(p j) c -> p j c", p=P)
            with sp.Fori(0, NT // 26) as i:
                sp.dma_start(rec[:, bass.ds(i * 26, 26), :], tmpl[:]).then_inc(s_fill, 16)
            xs = S.by_src.rearrange("(p j) c -> p j c", p=P)
            sp.dma_start(xs[:, TE - 6:TE, :], zx[:]).then_inc(s_fill, 16)
            sp.wait_ge(s_fill, 16 * (NT // 26 + 1))
            sp.wait_ge(s_x, 32)
            sp.wait_ge(s_d, 7)
            sp.wait_ge(s_const, 10)
            sp.dma_start(S.deg_rows[0, :].rearrange("(b p) -> b p", p=P), degT[0:NBLK, 0, :]).then_inc(s_out, 16)
            sp.dma_start(S.deg_rows[1, :].rearrange("(b p) -> b p", p=P), degT[0:NBLK, 1, :]).then_inc(s_out, 16)
            sp.dma_start(S.deg_rows[2, :].rearrange("(b p) -> b p", p=P), one_row[:]).then_inc(s_out, 16)
            sp.wait_ge(s_out, 48)

        @block.gpsimd
        def _(pool):
            for t in (S.src_key, S.dst_key, types):
                pool.memset(t[:, TM:TE], PADKEY).then_inc(s_pad, 1)
            pool.memset(S.x[:, NBLK - 1, :], 0.0).then_inc(s_pad, 1)
            pool.iota(S.iota[:], pattern=[[1, P]], base=0, channel_multiplier=0,
                      allow_small_or_imprecise_dtypes=True).then_inc(s_const, 1)
            pool.memset(S.ident[:], 0.0).then_inc(s_const, 1)
            pool.memset(S.lower[:], 1.0).then_inc(s_const, 1)
            pool.memset(S.upper[:], 1.0).then_inc(s_const, 1)
            pool.wait_ge(s_const, 4)
            pool.affine_select(out=S.ident[:], in_=S.ident[:], compare_op=ALU.not_equal, fill=1.0, base=0,
                               pattern=[[-1, P]], channel_multiplier=1).then_inc(s_const, 1)
            pool.affine_select(out=S.lower[:], in_=S.lower[:], compare_op=ALU.is_gt, fill=0.0, base=0,
                               pattern=[[-1, P]], channel_multiplier=1).then_inc(s_const, 1)
            pool.affine_select(out=S.upper[:], in_=S.upper[:], compare_op=ALU.is_gt, fill=0.0, base=0,
                               pattern=[[1, P]], channel_multiplier=-1).then_inc(s_const, 1)
            pool.iota(iotaj[:], pattern=[[1, NT]], base=0, channel_multiplier=0,
                      allow_small_or_imprecise_dtypes=True).then_inc(s_const, 1)
            pool.memset(one_row[:], 1.0).then_inc(s_const, 1)
            pool.memset(ones[:], 1.0).then_inc(s_const, 1)
            pool.wait_ge(s_key, KEYS)

            def step(s, g, b, r):
                wait(pool, s_free[b], r)
                pool.tensor_copy(hi[b][:], S.hi[:, bass.ds(g * G2, G2), 0]).then_inc(s_hi, 1)
                pool.wait_ge(s_hi, g + 1)
                pool.sem_inc(s_go, 1)
                for k in range(G2):
                    last = pool.tensor_scalar(ohs[b][:, k, P:], S.iota_b[:, 0:HI], hi[b][:, k:k + 1], None, ALU.is_equal)
                last.then_inc(s_oh_pool[b], 1)
            runs(TE // G2, [0], NB, pool, step)

        @block.scalar
        def _(act):
            act.wait_ge(s_const, 10)
            act.wait_ge(s_key, KEYS)

            def step(s, g, b, r):
                wait(act, s_free[b], r)
                for k in range(G2):
                    act.activation(dist[b][:, k, :], S.iota_b[:, 0:HI], ACT.Abs, scale=-1.0,
                                   bias=dhi0[:, bass.ds(g * G2 + k, 1)]).then_inc(s_dist, 1)
                act.wait_ge(s_dist, g * G2 + G2)
                act.activation(ohd[b][:, :, P + HI:], dist[b][:], ACT.Relu, scale=-1.0,
                               bias=ones[:, 0:1]).then_inc(s_oh_act[b], 1)
            runs(TE // G2, [0], NB, act, step)

        @block.vector
        def _(v):
            v.memset(tmpl[:], 0.0).then_inc(s_tmpl, 1)
            v.memset(zx[:], 0.0).then_inc(s_tmpl, 1)
            v.wait_ge(s_tmpl, 2)
            v.memset(tmpl[:, :, C_DL:C_DL0 + 1], -1.0).then_inc(s_tmpl, 1)
            v.memset(tmpl[:].bitcast(I32)[:, :, C_SPOS:C_SPOS + 1], FAR).then_inc(s_tmpl, 1)
            v.memset(zb[:], 0.0).then_inc(s_key, 1)
            v.memset(onec[:], 1.0).then_inc(s_key, 1)
            v.wait_ge(s_const, 5)
            v.tensor_copy(S.ident_b[:], S.ident[:]).then_inc(s_key, 1)
            v.tensor_copy(S.iota_b[:], S.iota[:]).then_inc(s_key, 1)
            v.wait_ge(s_load, 144)
            n = 4
            for q, t in enumerate((S.src_key, S.dst_key)):
                kf, lo, hi = S.key_f[:, :, q], S.lo[:, :, q], S.hi[:, :, q]
                v.tensor_copy(kf, t[:]).then_inc(s_key, 1)
                v.tensor_scalar(ti[:], t[:], P - 1, None, ALU.bitwise_and).then_inc(s_key, 1)
                n += 2
                v.wait_ge(s_key, n)
                v.tensor_copy(lo, ti[:]).then_inc(s_key, 1)
                n += 1
                v.wait_ge(s_key, n)
                v.tensor_scalar(ti[:], t[:], 7, None, ALU.logical_shift_right).then_inc(s_key, 1)
                n += 1
                v.wait_ge(s_key, n)
                v.tensor_copy(hi, ti[:]).then_inc(s_key, 1)
                n += 1
                v.wait_ge(s_key, n)
            v.tensor_copy(f0[:], types[:]).then_inc(s_key, 1)
            v.wait_ge(s_key, n + 1)
            v.tensor_scalar(f0[:], f0[:], 0.0, None, ALU.is_equal).then_inc(s_key, 1)
            v.wait_ge(s_key, n + 2)
            v.scalar_tensor_tensor(S.dst_lo0[:], S.lo[:, :, 1], 1.0, f0[:], ALU.add, ALU.mult).then_inc(s_key, 1)
            v.scalar_tensor_tensor(dhi0[:], S.hi[:, :, 1], -127.0, f0[:], ALU.add, ALU.mult).then_inc(s_key, 1)
            v.wait_ge(s_key, n + 4)
            v.tensor_scalar(S.dst_lo0[:], S.dst_lo0[:], -1.0, None, ALU.add).then_inc(s_key, 1)
            v.tensor_scalar(dhi0[:], dhi0[:], 127.0, None, ALU.add).then_inc(s_key, 1)
            v.wait_ge(s_key, n + 6)
            def step(s, g, b, r):
                wait(v, s_free[b], r)
                for k in range(G2):
                    t = bass.ds(g * G2 + k, 1)
                    v.tensor_scalar(ohd[b][:, k, 0:P], S.iota_b[:], S.lo[:, t, 1], None, ALU.is_equal)
                    v.tensor_scalar(ohd[b][:, k, P:P + HI], S.iota_b[:, 0:HI], S.hi[:, t, 1], None, ALU.is_equal)
                    last = v.tensor_scalar(ohs[b][:, k, 0:P], S.iota_b[:], S.lo[:, t, 0], None, ALU.is_equal)
                last.then_inc(s_oh[b], 1)
            runs(TE // G2, [0], NB, v, step)

            v.wait_ge(s_hist, 1)
            v.tensor_copy(cnt[:, 0:2, :], psD[:, 0:2 * HI].rearrange("p (a h) -> p a h", a=2)).then_inc(s_d, 1)
            v.tensor_copy(cnt[:, 2, :], psS[:, 0:HI]).then_inc(s_d, 1)
            v.wait_ge(s_pe, 1)
            v.tensor_copy(tot[:], psA[:, 0:2 * NBLK].rearrange("p (a h) -> p a h", a=2)).then_inc(s_d, 1)
            v.tensor_copy(ex[:], psB[:, 0:2 * NBLK].rearrange("p (a h) -> p a h", a=2)).then_inc(s_d, 1)
            v.wait_ge(s_pe, 2)
            v.tensor_copy(degT[0:NBLK, :, :], psC[0:NBLK, 0:2 * P].rearrange("p (a h) -> p a h", a=2)).then_inc(s_d, 1)
            v.wait_ge(s_d, 5)
            v.tensor_scalar(toti[:], tot[:, 0, :], 127.0, None, ALU.add).then_inc(s_d, 1)
            v.wait_ge(s_d, 6)
            v.tensor_scalar(toti[:], toti[:], 7, None, ALU.logical_shift_right).then_inc(s_d, 1)
            v.wait_ge(s_d, 7)
            v.tensor_copy(tot[:, 0, :], toti[:]).then_inc(s_d, 1)
            v.wait_ge(s_d, 8)
            for q in range(2):
                v.tensor_tensor_scan(cum[:, q, :], onec[:], tot[:, q, :], 0.0, ALU.mult, ALU.add).then_inc(s_d, 1)
            v.wait_ge(s_d, 10)
            v.tensor_tensor(tot[:], cum[:], tot[:], ALU.subtract).then_inc(s_d, 1)
            v.wait_ge(s_d, 11)
            v.tensor_tensor(S.base[:, 0:NBLK], tot[:, 1, :], ex[:, 1, :], ALU.add).then_inc(s_d, 1)
            v.scalar_tensor_tensor(S.base[:, HI:HI + NBLK], tot[:, 0, :], float(P), ex[:, 0, :],
                                   ALU.mult, ALU.add).then_inc(s_d, 1)
            for q in range(2):
                v.memset(S.base[:, q * HI + NBLK:q * HI + HI], FARPOS).then_inc(s_d, 1)
            v.wait_ge(s_d, 15)
            v.scalar_tensor_tensor(en[:, 0, :], S.base[:, 0:NBLK], -1.0, cnt[:, 2, 0:NBLK],
                                   ALU.add, ALU.add).then_inc(s_d, 1)
            v.tensor_scalar(en[:, 1, :], cnt[:, 2, 0:NBLK], 0.0, float(FAR), ALU.is_equal, ALU.mult).then_inc(s_d, 1)
            v.wait_ge(s_d, 17)
            v.tensor_scalar(eni[:, 0, :], en[:, 0, :], 0.0, None, ALU.max).then_inc(s_d, 1)
            v.wait_ge(s_d, 18)
            v.tensor_scalar(eni[:, 1, :], eni[:, 0, :], P - 1, None, ALU.bitwise_and).then_inc(s_d, 1)
            v.tensor_scalar(eni[:, 2, :], eni[:, 0, :], 7, None, ALU.logical_shift_right).then_inc(s_d, 1)
            v.wait_ge(s_d, 20)
            v.scalar_tensor_tensor(en[:, 0, :], eni[:, 1, :], float(TE), eni[:, 2, :], ALU.mult, ALU.add).then_inc(s_d, 1)
            v.wait_ge(s_d, 21)
            v.tensor_tensor(S.last[:], en[:, 0, :], en[:, 1, :], ALU.add).then_inc(s_d, 1)
            v.wait_ge(s_pe, 3)
            v.tensor_copy(cumT[0:NBLK, :], psC[0:NBLK, 0:1]).then_inc(s_d, 1)
            v.wait_ge(s_d, 23)
            v.wait_ge(s_const, 10)
            v.tensor_scalar(cmp[0:NBLK, :], iotaj[0:NBLK, :], cumT[0:NBLK, :], None, ALU.is_ge).then_inc(s_d, 1)
            for q, pb in enumerate((psA, psB, psC, psD)):
                v.wait_ge(s_pe, 4 + q)
                w = NT // 4
                v.tensor_scalar(S.blk[0:1, q * w:q * w + w], pb[0:1, 0:w], float(NBLK - 1), None, ALU.min).then_inc(s_d, 1)

        @block.tensor
        def _(pe):
            pe.wait_ge(s_key, 4)
            pe.matmul(psD[:, 0:2 * HI], S.ident_b[:], zb[:], start=True, stop=False, skip_group_check=True)
            pe.matmul(psS[:, 0:HI], S.ident_b[:], zb[:, 0:HI], start=True, stop=False, skip_group_check=True)

            def step(s, g, b, r):
                for made in (s_oh, s_oh_pool, s_oh_act):
                    pe.wait_ge(made[b], r + 1)
                for k in range(G2):
                    pe.matmul(psD[:, 0:2 * HI], ohd[b][:, k, 0:P], ohd[b][:, k, P:], start=False, stop=False,
                              skip_group_check=True)
                    last = pe.matmul(psS[:, 0:HI], ohs[b][:, k, 0:P], ohs[b][:, k, P:], start=False, stop=False,
                                     skip_group_check=True)
                last.then_inc(s_free[b], 1)
            runs(TE // G2, [0], NB, pe, step)
            pe.matmul(psD[:, 0:2 * HI], S.ident_b[:], zb[:], start=False, stop=True, skip_group_check=True)
            pe.matmul(psS[:, 0:HI], S.ident_b[:], zb[:, 0:HI], start=False, stop=True,
                      skip_group_check=True).then_inc(s_hist, 1)
            pe.wait_ge(s_d, 2)
            pe.wait_ge(s_const, 10)
            for q, c in ((0, 0), (1, 2)):
                pe.matmul(psA[:, q * NBLK:(q + 1) * NBLK], ones[:], cnt[:, c, 0:NBLK], start=True, stop=True)
                last = pe.matmul(psB[:, q * NBLK:(q + 1) * NBLK], S.upper[:], cnt[:, c, 0:NBLK], start=True, stop=True)
            last.then_inc(s_pe, 1)
            for q in range(2):
                last = pe.transpose(psC[0:NBLK, q * P:(q + 1) * P], cnt[:, q, 0:NBLK], S.ident[:])
            last.then_inc(s_pe, 1)
            pe.wait_ge(s_d, 10)
            pe.transpose(psC[0:NBLK, 0:P], cum[:, 0, :], S.ident[:]).then_inc(s_pe, 1)
            pe.wait_ge(s_d, 24)
            for q, pb in enumerate((psA, psB, psC, psD)):
                w = NT // 4
                pe.matmul(pb[0:1, 0:w], ones[0:NBLK, 0:1], cmp[0:NBLK, q * w:q * w + w],
                          start=True, stop=True).then_inc(s_pe, 1)


def place_phase(nc, S, a):
    with Phase(nc, "place") as ph:
        pl = ph.sbs("pl", NB, [P, G2, PC])
        kc = ph.sbs("kc", NB, [P, G2, 2])
        ohlo = ph.sbs("ohlo", NB, [P, G2, 2, P], BF16)
        ohhi = ph.sbs("ohhi", NB, [P, G2, 2, HI], BF16)
        hi = ph.sbs("hi", NB, [P, G2])
        ohT = ph.sbs("ohT", NB, [P, G2, 2, P])
        seen = ph.sbs("seen", 2, [P, 2 * HI])
        same = ph.sbs("same", 2, [P, G2, 2, P])
        found = ph.sbs("found", 2, [P, G2, 2, HI])
        rank = ph.sbs("rank", NB, [P, G2, 2])
        look = ph.sbs("look", NB, [P, G2, 2])
        posi = ph.sbs("posi", NB, [P, G2, 2], I32)
        pos7 = ph.sbs("pos7", NB, [P, 2, G2, 2], I32)
        place = ph.sbs("place", NB, [P, G2], I32)
        psT = [ph.bank(f"psT{k}", BF16) for k in range(2)]
        psK = [ph.bank(f"psK{k}") for k in range(2)]
        psG = [ph.bank(f"psG{k}") for k in range(2)]
        psR = ph.bank("psR")
        s_z, s_seen, s_R, s_i = ph.sem("s_z"), ph.sem("s_seen"), ph.sem("s_R"), ph.sem("s_i")
        s_oh, s_T, s_ohT, s_rank = ph.sems("s_oh"), ph.sems("s_T"), ph.sems("s_ohT"), ph.sems("s_rank")
        s_G, s_look, s_ef, s_meta = ph.sems("s_G"), ph.sems("s_look"), ph.sems("s_ef"), ph.sems("s_meta")
        s_hi = ph.sems("s_hi")
        s_place, s_sent, s_turn = ph.sems("s_place"), ph.sems("s_sent"), ph.sem("s_turn")
        block = ph.block()
        GT = TE // G2
        ATTRS = ((a.edge_attr_50, 0, 50), (a.edge_attr_4, 50, 4), (a.edge_attr_8, 54, 8))

        @block.sync
        def _(sp):
            sp.wait_ge(s_z, NB)
            with sp.Fori(0, TM // G2 // NB) as i:
                for b in range(NB):
                    sp.wait_ge(s_sent[b], i * (16 * G2))
                    for arr, c0, c in ATTRS:
                        sp.dma_start(pl[b][:, :, c0:c0 + c],
                                     arr[0:P * TM, :].rearrange("(p t) c -> p t c", t=TM)
                                     [:, bass.ds((i * NB + b) * G2, G2), :]).then_inc(s_ef[b], 16)
            r = TM // G2 // NB
            full = TAIL // P
            for b in range(NB):
                sp.wait_ge(s_sent[b], r * 16 * G2)
                for arr, c0, c in ATTRS:
                    if b == 0:
                        sp.dma_start(pl[b][:, 0:full, c0:c0 + c],
                                     arr[P * TM:P * (TM + full), :].rearrange("(t p) c -> p t c", p=P)
                                     ).then_inc(s_ef[b], 16)
                    elif b == 1:
                        sp.dma_start(pl[b][0:TAIL - P * full, 0, c0:c0 + c],
                                     arr[P * (TM + full):E, :]).then_inc(s_ef[b], 16)
                if b > 1:
                    sp.sem_inc(s_ef[b], 48)
            for b in range(NB):
                sp.wait_ge(s_sent[b], (r + 1) * 16 * G2)

        @block.gpsimd
        def _(pool):
            bound = pool.to_reg(P * NT - 1)
            pool.wait_ge(s_z, NB)

            def step(s, g, b, r):
                rec = pl[b][:].bitcast(I32)
                if s == 0:
                    wait(pool, s_sent[b], r * 16 * G2)
                    t = bass.ds(g * G2, G2)
                    pool.tensor_copy(hi[b][:], S.hi[:, t, 0]).then_inc(s_meta[b], 1)
                    pool.tensor_copy(rec[:, :, C_SRC], S.src_key[:, t])
                    pool.tensor_copy(pl[b][:, :, C_DL], S.lo[:, t, 1])
                    pool.tensor_copy(pl[b][:, :, C_DL0], S.dst_lo0[:, t]).then_inc(s_meta[b], 1)
                    pool.wait_ge(s_meta[b], r * 2 + 1)
                    pool.sem_inc(s_turn, 1)
                    for k in range(G2):
                        last = pool.tensor_scalar(ohhi[b][:, k, 0, :], S.iota_b[:, 0:HI], hi[b][:, k:k + 1], None,
                                                  ALU.is_equal)
                    last.then_inc(s_hi[b], 1)
                else:
                    pool.wait_ge(s_ef[b], (r + 1) * 48)
                    pool.wait_ge(s_place[b], r + 1)
                    pool.wait_ge(s_meta[b], (r + 1) * 2)
                    pool.sem_inc(s_turn, 1)
                    for k in range(G2):
                        pool.indirect_dma_start(S.records[:], bass.IndirectOffsetOnAxis(ap=place[b][:, k:k + 1], axis=0),
                                                pl[b][:, k, :], None, bounds_check=bound, oob_is_err=False
                                                ).then_inc(s_sent[b], 16)
            runs(GT, [0, 2], NB, pool, step)
            for b in range(NB):
                pool.wait_ge(s_sent[b], (GT // NB) * 16 * G2)

        @block.vector
        def _(v):
            for b in range(NB):
                v.memset(pl[b][:], 0.0).then_inc(s_z, 1)

            def step(s, g, b, r):
                if s == 0:
                    wait(v, s_G[b], r)
                    t = bass.ds(g * G2, G2)
                    v.tensor_copy(kc[b][:], S.key_f[:, t, :])
                    for k in range(G2):
                        t = bass.ds(g * G2 + k, 1)
                        for q in range(2):
                            v.tensor_scalar(ohlo[b][:, k, q, :], S.iota_b[:], S.lo[:, t, q], None, ALU.is_equal)
                        last = v.tensor_scalar(ohhi[b][:, k, 1, :], S.iota_b[:, 0:HI], S.hi[:, t, 1], None, ALU.is_equal)
                    last.then_inc(s_oh[b], 1)
                elif s == 2:
                    v.wait_ge(s_ohT[b], r + 1)
                    o, n = two_before(b, r)
                    wait(v, s_rank[o], n)
                    for k in range(G2):
                        for q in range(2):
                            c = (k * 2 + q) * P
                            last = v.scalar_tensor_tensor(same[b % 2][:, k, q, :], psK[b % 2][:, c:c + P], kc[b][:, k, q:q + 1],
                                                          S.lower[:], ALU.is_equal, ALU.mult,
                                                          accum_out=rank[b][:, k, q:q + 1])
                    last.then_inc(s_rank[b], 1)
                else:
                    v.wait_ge(s_G[b], r + 1)
                    o, n = two_before(b, r)
                    wait(v, s_look[o], n)
                    for k in range(G2):
                        for q in range(2):
                            c = k * 2 * HI + q * HI
                            last = v.tensor_tensor_reduce(out=found[b % 2][:, k, q, :], in0=psG[b % 2][:, c:c + HI],
                                                          in1=ohhi[b][:, k, q, :], scale=1.0, scalar=0.0,
                                                          op0=ALU.mult, op1=ALU.add,
                                                          accum_out=look[b][:, k, q:q + 1])
                    last.then_inc(s_look[b], 1)
                    v.wait_ge(s_look[b], r + 1)
                    wait(v, s_sent[b], r * 16 * G2)
                    v.tensor_tensor(posi[b][:], rank[b][:], look[b][:], ALU.add).then_inc(s_i, 1)
                    v.wait_ge(s_i, g * 3 + 1)
                    v.tensor_scalar(pos7[b][:, 0], posi[b][:], P - 1, None, ALU.bitwise_and).then_inc(s_i, 1)
                    v.tensor_scalar(pos7[b][:, 1], posi[b][:], 7, None, ALU.logical_shift_right).then_inc(s_i, 1)
                    v.wait_ge(s_i, g * 3 + 3)
                    v.scalar_tensor_tensor(pl[b][:].bitcast(I32)[:, :, C_SPOS], pos7[b][:, 0, :, 0], float(TE),
                                           pos7[b][:, 1, :, 0], ALU.mult, ALU.add)
                    v.scalar_tensor_tensor(place[b][:], pos7[b][:, 0, :, 1], float(NT),
                                           pos7[b][:, 1, :, 1], ALU.mult, ALU.add).then_inc(s_place[b], 1)
            runs(GT, [0, 2, 1], NB, v, step)

        @block.scalar
        def _(act):
            def step(s, g, b, r):
                if s == 1:
                    act.wait_ge(s_T[b], r + 1)
                    wait(act, s_G[b], r)
                    act.activation(ohT[b][:].rearrange("p a q e -> p (a q e)"), psT[b % 2][:, 0:4 * P],
                                   ACT.Copy).then_inc(s_ohT[b], 1)
                else:
                    for k in range(G2):
                        act.wait_ge(s_R, g * G2 + k + 1)
                        if k == 0:
                            o, n = (b + NB - 1) % NB, r if b == 0 else r + 1
                            wait(act, s_G[o], n)
                        act.activation(seen[k][:], psR[:, 0:2 * HI], ACT.Copy).then_inc(s_seen, 1)
            runs(GT, [1, 0], NB, act, step)

        @block.tensor
        def _(pe):
            pe.matmul(psR[:, 0:2 * HI], S.ident[:], S.base[:], start=True, stop=False,
                      skip_group_check=True).then_inc(s_R, 1)

            def step(s, g, b, r):
                if s == 1:
                    pe.wait_ge(s_oh[b], r + 1)
                    o, n = two_before(b, r)
                    wait(pe, s_rank[o], n)
                    for k in range(G2):
                        for q in range(2):
                            c = (k * 2 + q) * P
                            pe.transpose(psT[b % 2][:, c:c + P], ohlo[b][:, k, q, :], S.ident_b[:])
                            last = pe.matmul(psK[b % 2][:, c:c + P], kc[b][:, k, q:q + 1].to_broadcast([P, P]),
                                             S.ident[:], start=True, stop=True)
                    last.then_inc(s_T[b], 1)
                else:
                    pe.wait_ge(s_ohT[b], r + 1)
                    pe.wait_ge(s_hi[b], r + 1)
                    o, n = two_before(b, r)
                    wait(pe, s_look[o], n)
                    for k in range(G2):
                        pe.wait_ge(s_seen, g * G2 + k + 1)
                        for q in range(2):
                            last = pe.matmul(psR[:, q * HI:(q + 1) * HI], ohlo[b][:, k, q, :], ohhi[b][:, k, q, :],
                                             start=False, stop=False, skip_group_check=True)
                        last.then_inc(s_R, 1)
                        for q in range(2):
                            c = k * 2 * HI + q * HI
                            last = pe.matmul(psG[b % 2][:, c:c + HI], ohT[b][:, k, q, :],
                                             seen[k][:, q * HI:(q + 1) * HI], start=True, stop=True)
                    last.then_inc(s_G[b], 1)
            runs(GT, [1, 0], NB, pe, step)


def send_phase(nc, S, a):
    with Phase(nc, "send") as ph:
        DEEP = 8
        pl = ph.sbs("pl", DEEP, [P, G2, PC])
        oh = ph.sbs("oh", DEEP, [P, G2, P])
        ohT = ph.sbs("ohT", DEEP, [P, G2, P])
        row = ph.sbs("row", DEEP, [P, G2, XC])
        psT = [ph.bank(f"psT{k}") for k in range(2)]
        psX = [ph.bank(f"psX{k}") for k in range(2)]
        s_rec, s_oh, s_T, s_ohT = (ph.sems(n, DEEP) for n in ("s_rec", "s_oh", "s_T", "s_ohT"))
        s_X, s_row, s_sent = (ph.sems(n, DEEP) for n in ("s_X", "s_row", "s_sent"))
        s_turn = ph.sem("s_turn")
        block = ph.block()
        GT = NT // G2
        rec = S.records.rearrange("(p j) c -> p j c", p=P)

        @block.sync
        def _(sp):
            def step(s, g, b, r):
                wait(sp, s_sent[b], r * 16 * G2)
                sp.dma_start(pl[b][:], rec[:, bass.ds(g * G2, G2), :]).then_inc(s_rec[b], 16)
            runs(GT, [0], DEEP, sp, step)

        @block.gpsimd
        def _(pool):
            bound = pool.to_reg(P * TE - 1)

            def step(s, g, b, r):
                pool.wait_ge(s_row[b], r + 1)
                pool.sem_inc(s_turn, 1)
                for k in range(G2):
                    at = pl[b][:].bitcast(I32)[:, k, C_SPOS:C_SPOS + 1]
                    pool.indirect_dma_start(S.by_src[:], bass.IndirectOffsetOnAxis(ap=at, axis=0),
                                            row[b][:, k, :], None, bounds_check=bound, oob_is_err=False
                                            ).then_inc(s_sent[b], 16)
            runs(GT, [2], DEEP, pool, step)
            for b in range(DEEP):
                pool.wait_ge(s_sent[b], (GT // DEEP) * 16 * G2)

        @block.vector
        def _(v):
            def step(s, g, b, r):
                if s == 0:
                    v.wait_ge(s_rec[b], (r + 1) * 16)
                    wait(v, s_X[b], r)
                    for k in range(G2):
                        v.tensor_scalar(oh[b][:, k, :], S.iota[:], pl[b][:, k, C_DL:C_DL + 1], None, ALU.is_equal)
                    t = bass.ds(g * G2, G2)
                    v.tensor_copy(S.e_src[:, t], pl[b][:].bitcast(I32)[:, :, C_SRC])
                    v.tensor_copy(S.e_dl[:, t], pl[b][:, :, C_DL])
                    last = v.tensor_copy(S.e_dl0[:, t], pl[b][:, :, C_DL0])
                    last.then_inc(s_oh[b], 1)
                else:
                    v.wait_ge(s_X[b], r + 1)
                    wait(v, s_sent[b], r * 16 * G2)
                    v.tensor_copy(row[b][:, :, 0:D], psX[b % 2][:, 0:G2 * P].rearrange("p (k d) -> p k d", k=G2))
                    v.tensor_copy(row[b][:, :, D], pl[b][:].bitcast(I32)[:, :, C_SRC]).then_inc(s_row[b], 1)
            runs(GT, [0, 2], DEEP, v, step)

        @block.scalar
        def _(act):
            def step(s, g, b, r):
                act.wait_ge(s_T[b], r + 1)
                wait(act, s_X[b], r)
                act.activation(ohT[b][:].rearrange("p k e -> p (k e)"), psT[b % 2][:, 0:G2 * P],
                               ACT.Copy).then_inc(s_ohT[b], 1)
            runs(GT, [0], DEEP, act, step)

        @block.tensor
        def _(pe):
            def step(s, g, b, r):
                o, n = two_before(b, r, DEEP)
                if s == 1:
                    pe.wait_ge(s_oh[b], r + 1)
                    wait(pe, s_ohT[o], n)
                    for k in range(G2):
                        last = pe.transpose(psT[b % 2][:, k * P:(k + 1) * P], oh[b][:, k, :], S.ident[:])
                    last.then_inc(s_T[b], 1)
                else:
                    pe.wait_ge(s_ohT[b], r + 1)
                    wait(pe, s_row[o], n)
                    for k in range(G2):
                        at = pe.value_load(S.blk[0:1, bass.ds(g * G2 + k, 1)], min_val=0, max_val=NBLK - 1)
                        last = pe.matmul(psX[b % 2][:, k * P:(k + 1) * P], ohT[b][:, k, :],
                                         S.x[:, bass.ds(at, 1), :].rearrange("p a d -> p (a d)"),
                                         start=True, stop=True)
                    last.then_inc(s_X[b], 1)
            runs(GT, [1, 0], DEEP, pe, step)


def max_phase(nc, S, a):
    with Phase(nc, "max") as ph:
        W = 4
        row = ph.sbs("row", NB, [P, W, XC])
        key = ph.sbs("key", NB, [P, W * P])
        step_down = ph.sbs("step_down", NB, [P, W * P])
        run = ph.sbs("run", NB, [P, W * P])
        back = ph.sbs("back", NB, [P, W * P])
        ps_x = [ph.bank(f"ps_x{k}") for k in range(2)]
        ps_k = [ph.bank(f"ps_k{k}") for k in range(2)]
        ps_o = [ph.bank(f"ps_o{k}") for k in range(2)]
        s_row, s_x, s_key, s_run, s_o, s_back, s_out = (ph.sems(n) for n in
                                                        ("s_row", "s_x", "s_key", "s_run", "s_o", "s_back", "s_out"))
        s_z, s_down = ph.sem("s_z"), ph.sem("s_down")
        block = ph.block()
        GT = TE // W
        by_src = S.by_src.rearrange("(p j) c -> p j c", p=P)
        running = S.running.rearrange("(p j) d -> p j d", p=P)

        @block.sync
        def _(sp):
            def step(s, g, b, r):
                wait(sp, s_x[b], r)
                sp.dma_start(row[b][:], by_src[:, bass.ds(g * W, W), :]).then_inc(s_row[b], 16)
            runs(GT, [0], NB, sp, step)

        @block.gpsimd
        def _(pool):
            pool.memset(run[NB - 1][:, W * P - 1:], -1e38).then_inc(s_z, 1)
            pool.memset(key[NB - 1][:, W * P - 1:], 0.0).then_inc(s_z, 1)

            def step(s, g, b, r):
                pool.wait_ge(s_back[b], r + 1)
                pool.dma_start(running[:, bass.ds(g * W, W), :],
                               back[b][:].rearrange("p (k d) -> p k d", k=W)).then_inc(s_out[b], 16)
            runs(GT, [0], NB, pool, step)
            for b in range(NB):
                pool.wait_ge(s_out[b], (GT // NB) * 16)

        @block.scalar
        def _(act):
            act.wait_ge(s_z, 2)

            def step(s, g, b, r):
                if s == 0:
                    act.wait_ge(s_x[b], r + 1)
                    wait(act, s_run[(b + 1) % NB], r if b < NB - 1 else r + 1)
                    act.activation(key[b][:], ps_k[b % 2][:, :], ACT.Copy, scale=-STEP).then_inc(s_key[b], 1)
                else:
                    act.wait_ge(s_o[b], r + 1)
                    wait(act, s_out[b], r * 16)
                    act.activation(back[b][:], ps_o[b % 2][:, :], ACT.Copy).then_inc(s_back[b], 1)
            runs(GT, [0, 1], NB, act, step)

        @block.vector
        def _(v):
            v.wait_ge(s_z, 2)

            def step(s, g, b, r):
                o = (b + NB - 1) % NB
                v.wait_ge(s_key[b], r + 1)
                wait(v, s_o[b], r)
                v.tensor_tensor(step_down[b][:, 1:], key[b][:, 1:], key[b][:, :W * P - 1], ALU.subtract)
                v.tensor_tensor(step_down[b][:, 0:1], key[b][:, 0:1], key[o][:, W * P - 1:],
                                ALU.subtract).then_inc(s_down, 1)
                v.wait_ge(s_down, g + 1)
                wait(v, s_run[o], r if b == 0 else r + 1)
                v.tensor_tensor_scan(run[b][:], step_down[b][:], ps_x[b % 2][:, :], run[o][:, W * P - 1:],
                                     ALU.add, ALU.max).then_inc(s_run[b], 1)
            runs(GT, [0], NB, v, step)

        @block.tensor
        def _(pe):
            def step(s, g, b, r):
                o, n = two_before(b, r)
                if s == 0:
                    pe.wait_ge(s_row[b], (r + 1) * 16)
                    wait(pe, s_run[o], n)
                    for k in range(W):
                        c = slice(k * P, (k + 1) * P)
                        pe.transpose(ps_x[b % 2][:, c], row[b][:, k, 0:D], S.ident[:])
                        last = pe.matmul(ps_k[b % 2][:, c], row[b][:, k, D:D + 1].to_broadcast([P, P]), S.ident[:],
                                         start=True, stop=True)
                    last.then_inc(s_x[b], 1)
                else:
                    pe.wait_ge(s_run[b], r + 1)
                    wait(pe, s_back[o], n)
                    for k in range(W):
                        c = slice(k * P, (k + 1) * P)
                        last = pe.transpose(ps_o[b % 2][:, c], run[b][:, c], S.ident[:])
                    last.then_inc(s_o[b], 1)
            runs(GT, [0, 1], NB, pe, step)


def normalize(v, ph, y, out, s, n):
    W = ph.ln
    v.tensor_reduce(W.mean[:], y, AX.X, ALU.add).then_inc(s, 1)
    v.wait_ge(s, n + 1)
    v.tensor_scalar(W.mean[:], W.mean[:], 1.0 / D, None, ALU.mult).then_inc(s, 1)
    v.wait_ge(s, n + 2)
    v.tensor_tensor(y, y, W.mean[:].rearrange("p (k a) -> p k a", a=1).to_broadcast([P, KB, D]),
                    ALU.subtract).then_inc(s, 1)
    v.wait_ge(s, n + 3)
    v.tensor_tensor(W.sq[:], y, y, ALU.mult).then_inc(s, 1)
    v.wait_ge(s, n + 4)
    v.tensor_reduce(W.var[:], W.sq[:], AX.X, ALU.add).then_inc(W.s_var, 1)
    v.wait_ge(W.s_root, W.turn)
    v.reciprocal(W.inv[:], W.root[:]).then_inc(s, 1)
    v.wait_ge(s, n + 5)
    v.tensor_tensor(out, y, W.inv[:].rearrange("p (k a) -> p k a", a=1).to_broadcast([P, KB, D]),
                    ALU.mult).then_inc(s, 1)
    return n + 6


def norm_buffers(ph, sq=None):
    W = Names()
    W.mean, W.var, W.root, W.inv = (ph.sb(n, [P, KB]) for n in ("mean", "var", "root", "inv"))
    W.sq = ph.sb("sq", [P, KB, D]) if sq is None else sq
    W.eps = ph.sb("eps", [P, 1])
    W.s_var, W.s_root, W.s_eps = ph.sem("s_var"), ph.sem("s_root"), ph.sem("s_eps")
    ph.ln = W


def root(act, ph, i):
    W = ph.ln
    act.wait_ge(W.s_var, i + 1)
    act.wait_ge(W.s_eps, 1)
    act.activation(W.root[:], W.var[:], ACT.Sqrt, bias=W.eps[:], scale=1.0 / D).then_inc(W.s_root, 1)


NIT = NBLK // KB
CH = KB * P // 2


def blocks_of(bank0, bank1, k):
    return (bank0, k * P) if k < 4 else (bank1, (k - 4) * P)


def node0_phase(nc, S, a):
    with Phase(nc, "node0") as ph:
        norm_buffers(ph)
        w0 = ph.sb("w0", [P, 2 * D])
        w0T = ph.sb("w0T", [P, 2, D])
        w1 = ph.sb("w1", [P, 2, 2 * D])
        b0 = ph.sb("b0", [P, D])
        b1 = ph.sb("b1", [P, 2 * D])
        at = ph.sb("at", [P, KB], I32)
        mx = ph.sb("mx", [P, KB, D])
        xc = ph.sb("xc", [P, KB, D])
        T = ph.sb("T", [P, 2, KB, P])
        y = ph.sb("y", [P, KB, D])
        ab = ph.sb("ab", [P, 2, KB, 2 * D])
        ps = [ph.bank(f"ps{k}") for k in range(8)]
        s_w, s_wT, s_wc = ph.sem("s_w"), ph.sem("s_wT"), ph.sem("s_wc")
        s_at, s_zero, s_mx, s_xc = ph.sem("s_at"), ph.sem("s_zero"), ph.sem("s_mx"), ph.sem("s_xc")
        s_T, s_Tc, s_y, s_v, s_n = ph.sem("s_T"), ph.sem("s_Tc"), ph.sem("s_y"), ph.sem("s_v"), ph.sem("s_n")
        s_T2, s_T2c, s_ab, s_abc, s_out = (ph.sem(n) for n in ("s_T2", "s_T2c", "s_ab", "s_abc", "s_out"))
        s_turn = ph.sem("s_turn")
        block = ph.block()

        @block.sync
        def _(sp):
            sp.dma_start(w0[:], a.L0_gnn_W).then_inc(s_w, 16)
            for q in range(2):
                sp.dma_start(w1[:, q, :], a.L1_gnn_msg_W1[q * D:(q + 1) * D, :]).then_inc(s_w, 16)
            sp.dma_start(b0[:], a.L0_gnn_b.rearrange("(a d) -> a d", a=1).to_broadcast([P, D])).then_inc(s_w, 16)
            sp.dma_start(b1[:], a.L1_gnn_msg_b1.rearrange("(a d) -> a d", a=1).to_broadcast([P, 2 * D])).then_inc(s_w, 16)
            with sp.Fori(0, NIT) as i:
                sp.wait_ge(s_abc, 8 * i + 8)
                for q, tab in enumerate((S.tab_a, S.tab_b)):
                    sp.dma_start(tab.rearrange("(k p) d -> p k d", p=P)[:, bass.ds(i * KB, KB), :],
                                 ab[:, q]).then_inc(s_out, 16)
            sp.wait_ge(s_out, 32 * NIT)

        @block.gpsimd
        def _(pool):
            pool.memset(ph.ln.eps[:], EPS).then_inc(ph.ln.s_eps, 1)
            bound = pool.to_reg(P * TE - 1)
            with pool.Fori(0, NIT) as i:
                pool.wait_ge(s_T, i)
                pool.sem_inc(s_turn, 1)
                pool.memset(mx[:], 0.0).then_inc(s_zero, 1)
                pool.tensor_copy(at[:], S.last[:, bass.ds(i * KB, KB)]).then_inc(s_zero, 1)
                pool.wait_ge(s_zero, 2 * i + 2)
                pool.sem_inc(s_turn, 1)
                for k in range(KB):
                    pool.indirect_dma_start(mx[:, k, :], None, S.running[:],
                                            bass.IndirectOffsetOnAxis(ap=at[:, k:k + 1], axis=0),
                                            bounds_check=bound, oob_is_err=False).then_inc(s_mx, 16)

        @block.tensor
        def _(pe):
            pe.wait_ge(s_w, 80)
            for q in range(2):
                last = pe.transpose(ps[0][:, q * P:(q + 1) * P], w0[:, q * D:(q + 1) * D], S.ident[:])
            last.then_inc(s_wT, 1)
            pe.wait_ge(s_wc, 1)
            with pe.Fori(0, NIT) as i:
                pe.wait_ge(s_mx, (i + 1) * 16 * KB)
                pe.wait_ge(s_xc, i + 1)
                wait(pe, s_abc, 8 * i)
                for q, t in ((0, xc), (1, mx)):
                    for k in range(KB):
                        bank, c = blocks_of(ps[2 * q], ps[2 * q + 1], k)
                        last = pe.transpose(bank[:, c:c + P], t[:, k, :], S.ident[:])
                last.then_inc(s_T, 1)
                pe.wait_ge(s_Tc, 4 * i + 4)
                for k in range(KB):
                    bank, c = blocks_of(ps[4], ps[5], k)
                    pe.matmul(bank[:, c:c + D], T[:, 0, k, :], w0T[:, 0, :], start=True, stop=False)
                    last = pe.matmul(bank[:, c:c + D], T[:, 1, k, :], w0T[:, 1, :], start=False, stop=True)
                last.then_inc(s_y, 1)
                pe.wait_ge(s_n, i + 1)
                for k in range(KB):
                    bank, c = blocks_of(ps[6], ps[7], k)
                    last = pe.transpose(bank[:, c:c + P], xc[:, k, :], S.ident[:])
                last.then_inc(s_T2, 1)
                pe.wait_ge(s_T2c, 2 * i + 2)
                for k in range(KB):
                    for q in range(2):
                        last = pe.matmul(ps[k][:, q * 256:(q + 1) * 256], T[:, 0, k, :], w1[:, q, :],
                                         start=True, stop=True)
                last.then_inc(s_ab, 1)

        @block.scalar
        def _(act):
            with act.Fori(0, NIT) as i:
                act.wait_ge(s_T, i + 1)
                for q in range(2):
                    act.activation(T[:, q, 0:4, :].rearrange("p k e -> p (k e)"), ps[2 * q][:, :],
                                   ACT.Copy).then_inc(s_Tc, 1)
                    act.activation(T[:, q, 4:KB, :].rearrange("p k e -> p (k e)"), ps[2 * q + 1][:, 0:3 * P],
                                   ACT.Copy).then_inc(s_Tc, 1)
                root(act, ph, i)
                act.wait_ge(s_T2, i + 1)
                act.activation(T[:, 0, 0:4, :].rearrange("p k e -> p (k e)"), ps[6][:, :], ACT.Copy).then_inc(s_T2c, 1)
                act.activation(T[:, 0, 4:KB, :].rearrange("p k e -> p (k e)"), ps[7][:, 0:3 * P],
                               ACT.Copy).then_inc(s_T2c, 1)

        @block.vector
        def _(v):
            v.wait_ge(s_wT, 1)
            v.tensor_copy(w0T[:], ps[0][:, 0:2 * P].rearrange("p (q d) -> p q d", q=2)).then_inc(s_wc, 1)
            VN = 8
            with v.Fori(0, NIT) as i:
                rows = S.x[:, bass.ds(i * KB, KB), :]
                v.wait_ge(s_ab, i)
                v.tensor_scalar(xc[:], rows, 1.0, None, ALU.mult).then_inc(s_xc, 1)
                v.wait_ge(s_y, i + 1)
                n = VN * i
                v.wait_ge(s_xc, i + 1)
                v.tensor_tensor(y[:, 0:4, :], xc[:, 0:4, :], ps[4][:, :].rearrange("p (k d) -> p k d", k=4), ALU.add)
                v.tensor_tensor(y[:, 4:KB, :], xc[:, 4:KB, :], ps[5][:, 0:3 * P].rearrange("p (k d) -> p k d", k=3),
                                ALU.add).then_inc(s_v, 1)
                v.wait_ge(s_v, n + 1)
                v.tensor_tensor(y[:], y[:], b0[:].rearrange("p (a d) -> p a d", a=1).to_broadcast([P, KB, D]),
                                ALU.add).then_inc(s_v, 1)
                v.wait_ge(s_v, n + 2)
                ph.ln.turn = i + 1
                n = normalize(v, ph, y[:], xc[:], s_v, n + 2)
                v.wait_ge(s_v, n)
                v.tensor_scalar(rows, xc[:], 1.0, None, ALU.mult).then_inc(s_n, 1)
                v.wait_ge(s_ab, i + 1)
                wait(v, s_out, 32 * i)
                for k in range(KB):
                    v.tensor_copy(ab[:, 0, k, :], ps[k][:, 0:256])
                    v.tensor_tensor(ab[:, 1, k, :], ps[k][:, 256:512], b1[:], ALU.add).then_inc(s_abc, 1)
                v.sem_inc(s_abc, 1)


def gather_on(pool, b, ix, rows, table, s_ix, s_got, s_turn, r):
    pool.wait_ge(s_ix[b], r + 1)
    pool.sem_inc(s_turn, 1)
    for k in range(G2):
        pool.indirect_dma_start(rows[b % len(rows)][:, k, :], None, table[:],
                                bass.IndirectOffsetOnAxis(ap=ix[b][:, k:k + 1], axis=0)).then_inc(s_got[b], 16)


def one_hot(v, out, S, keys, g):
    shape = [P, G2, P]
    return v.tensor_tensor(out, S.iota[:].rearrange("p (k n) -> p k n", k=1).to_broadcast(shape),
                           keys[:, bass.ds(g * G2, G2)].rearrange("p (k n) -> p k n", n=1).to_broadcast(shape),
                           ALU.is_equal)


def load_blocks(v, S, g):
    return [v.value_load(S.blk[0:1, bass.ds(g * G2 + k, 1)], min_val=0, max_val=NBLK - 1) for k in range(G2)]


def add_to_block(v, agg, at, psA, b, r, k, s_C, s_half, s_acc, depth=NB):
    block = agg[:, bass.ds(at[k], 1), :].rearrange("p a c -> p (a c)")
    if k == 0:
        v.wait_ge(s_C[b], r + 1)
        wait(v, s_acc[(b + depth - 1) % depth], r if b == 0 else r + 1)
    else:
        v.wait_ge(s_half[b], r + 1)
    v.tensor_tensor(block, block, psA[b % 2][:, k * 2 * D:(k + 1) * 2 * D],
                    ALU.add).then_inc((s_half if k == 0 else s_acc)[b], 1)


def edge1_phase(nc, S, a, agg):
    with Phase(nc, "edge1") as ph:
        H = 2 * D
        NE, EP = 50, 64
        DEEP = 8
        pl = ph.sbs("pl", NB, [P, G2, EP])
        ix = ph.sbs("ix", DEEP, [P, G2], I32)
        fs = ph.sbs("fs", NB, [P, G2, H])
        fd = ph.sbs("fd", 2, [P, G2, H])
        oh = ph.sbs("oh", NB, [P, G2, P])
        ohb = ph.sbs("ohb", 2, [P, G2, P], BF16)
        ohT = ph.sbs("ohT", 2, [P, G2 * P])
        eT = ph.sbs("eT", 2, [P, P])
        h = ph.sbs("h", 2, [P, G2, H])
        we = ph.sb("we", [P, G2, H])
        psT = [ph.bank(f"psT{k}", BF16) for k in range(2)]
        psE = [ph.bank(f"psE{k}") for k in range(2)]
        psH = [ph.bank(f"psH{k}") for k in range(2)]
        psA = [ph.bank(f"psA{k}") for k in range(2)]
        s_w, s_turn, s_zero = ph.sem("s_w"), ph.sem("s_turn"), ph.sem("s_zero")
        s_half, s_acc = ph.sems("s_half", DEEP), ph.sems("s_acc", DEEP)
        s_rec, s_fd, s_ix, s_got, s_oh = (ph.sems(n, DEEP) for n in ("s_rec", "s_fd", "s_ix", "s_got", "s_oh"))
        s_T, s_TT, s_H, s_in, s_h, s_C = (ph.sems(n, DEEP) for n in ("s_T", "s_TT", "s_H", "s_in", "s_h", "s_C"))
        block = ph.block()
        GT = NT // G2
        rec = S.records.rearrange("(p j) c -> p j c", p=P)

        @block.sync
        def _(sp):
            sp.wait_ge(s_zero, 2 + NB)
            for k in range(G2):
                sp.dma_start(we[EP * k:EP * k + NE, k, :], a.L1_gnn_msg_W1[2 * D:2 * D + NE, :]).then_inc(s_w, 16)

            def step(s, g, b, r):
                o, n = before(b, r, NB, DEEP)
                wait(sp, s_T[o], n)
                sp.dma_start(pl[b % NB][:, :, 0:NE], rec[:, bass.ds(g * G2, G2), 0:NE]).then_inc(s_rec[b], 16)
                o, n = two_before(b, r, DEEP)
                wait(sp, s_H[o], n)
                for k in range(G2):
                    at = sp.value_load(S.blk[0:1, bass.ds(g * G2 + k, 1)], min_val=0, max_val=NBLK - 1)
                    sp.dma_start(fd[b % 2][:, k, :], S.tab_b[bass.ds(at * P, P), :]).then_inc(s_fd[b], 16)
            runs(GT, [0], DEEP, sp, step)

        @block.gpsimd
        def _(pool):
            runs(GT, [0], DEEP, pool,
                 lambda s, g, b, r: gather_on(pool, b, ix, fs, S.tab_a, s_ix, s_got, s_turn, r))

        @block.vector
        def _(v):
            v.memset(agg[:], 0.0).then_inc(s_zero, 1)
            for t in (*pl, we):
                v.memset(t[:], 0.0).then_inc(s_zero, 1)
            v.wait_ge(s_zero, 2 + NB)
            at = []

            def step(s, g, b, r):
                if s == 0:
                    wait(v, s_got[b], r * 16 * G2)
                    o, n = before(b, r, NB, DEEP)
                    wait(v, s_h[o], n)
                    v.tensor_scalar(ix[b][:], S.e_src[:, bass.ds(g * G2, G2)], 1.0, None, ALU.mult).then_inc(s_ix[b], 1)
                elif s == 1:
                    o, n = before(b, r, NB, DEEP)
                    wait(v, s_C[o], n)
                    o, n = two_before(b, r, DEEP)
                    wait(v, s_T[o], n)
                    one_hot(v, oh[b % NB][:], S, S.e_dl, g)
                    one_hot(v, ohb[b % 2][:], S, S.e_dl, g).then_inc(s_oh[b], 1)
                elif s == 2:
                    at[:] = load_blocks(v, S, g)
                elif s < 5:
                    add_to_block(v, agg, at, psA, b, r, s - 3, s_C, s_half, s_acc, DEEP)
                else:
                    v.wait_ge(s_H[b], r + 1)
                    v.wait_ge(s_got[b], (r + 1) * 16 * G2)
                    rows = fs[b % NB][:].rearrange("p k c -> p (k c)")
                    v.tensor_tensor(rows, psH[b % 2][:, :], rows, ALU.add).then_inc(s_in[b], 1)
            runs(GT, [0, 1, 4, 4, 4, 2], DEEP, v, step)

        @block.scalar
        def _(act):
            def step(s, g, b, r):
                o, n = two_before(b, r, DEEP)
                if s == 0:
                    act.wait_ge(s_T[b], r + 1)
                    wait(act, s_H[o], n)
                    act.activation(ohT[b % 2][:], psT[b % 2][:, 0:G2 * P], ACT.Copy)
                    act.activation(eT[b % 2][:], psE[b % 2][:, 0:P], ACT.Copy).then_inc(s_TT[b], 1)
                else:
                    act.wait_ge(s_in[b], r + 1)
                    wait(act, s_C[o], n)
                    act.activation(h[b % 2][:], fs[b % NB][:], ACT.Silu).then_inc(s_h[b], 1)
            runs(GT, [1, 2], DEEP, act, step)

        @block.tensor
        def _(pe):
            pe.wait_ge(s_w, 32)

            def step(s, g, b, r):
                o, n = two_before(b, r, DEEP)
                if s == 0:
                    pe.wait_ge(s_TT[b], r + 1)
                    pe.wait_ge(s_fd[b], (r + 1) * 16 * G2)
                    wait(pe, s_in[o], n)
                    for k in range(G2):
                        c = slice(k * H, (k + 1) * H)
                        e = slice(k * P, (k + 1) * P)
                        pe.matmul(psH[b % 2][:, c], ohT[b % 2][:, e], fd[b % 2][:, k, :], start=True, stop=False)
                        last = pe.matmul(psH[b % 2][:, c], eT[b % 2][:], we[:, k, :], start=False, stop=True)
                    last.then_inc(s_H[b], 1)
                elif s == 1:
                    pe.wait_ge(s_oh[b], r + 1)
                    pe.wait_ge(s_rec[b], (r + 1) * 16)
                    wait(pe, s_TT[o], n)
                    for k in range(G2):
                        pe.transpose(psT[b % 2][:, k * P:(k + 1) * P], ohb[b % 2][:, k, :], S.ident_b[:])
                    last = pe.transpose(psE[b % 2][:, 0:P], pl[b % NB][:].rearrange("p k c -> p (k c)"), S.ident[:])
                    last.then_inc(s_T[b], 1)
                else:
                    pe.wait_ge(s_h[b], r + 1)
                    wait(pe, s_acc[o], n)
                    for k in range(G2):
                        for q in range(2):
                            c = k * H + q * D
                            last = pe.matmul(psA[b % 2][:, c:c + D], h[b % 2][:, k, q * D:(q + 1) * D],
                                             oh[b % NB][:, k, :], start=True, stop=True)
                    last.then_inc(s_C[b], 1)
            runs(GT, [2, 1, 3], DEEP, pe, step)


def node1_phase(nc, S, a, agg):
    with Phase(nc, "node1") as ph:
        norm_buffers(ph)
        M = 32
        w2 = ph.sb("w2", [P, 2, D])
        u1 = ph.sb("u1", [P, 2, 2 * D])
        u2 = ph.sb("u2", [P, 2, D])
        b2 = ph.sb("b2", [1, D])
        c1 = ph.sb("c1", [P, 2])
        c2 = ph.sb("c2", [P, D])
        up = ph.sb("up", [P, D])
        deg = ph.sb("deg", [1, KB * P])
        xc = ph.sb("xc", [P, KB, D])
        xT = ph.sb("xT", [P, KB, P])
        y = ph.sb("y", [P, KB, D])
        mT = y[:]
        uT = ph.sb("uT", [P, 2, KB, P])
        ps = [ph.bank(f"ps{k}") for k in range(8)]
        names = ("s_w", "s_up", "s_deg", "s_xc", "s_xT", "s_xTc", "s_m", "s_mc", "s_u", "s_uc", "s_y", "s_v", "s_n",
                 "s_T2", "s_T2c", "s_t", "s_tc", "s_out")
        (s_w, s_up, s_deg, s_xc, s_xT, s_xTc, s_m, s_mc, s_u, s_uc, s_y, s_v, s_n,
         s_T2, s_T2c, s_t, s_tc, s_out) = (ph.sem(n) for n in names)
        block = ph.block()
        cols = (slice(0, 4), slice(4, KB))

        @block.sync
        def _(sp):
            sp.wait_ge(s_up, 1)
            for q in range(2):
                rows = slice(q * D, (q + 1) * D)
                sp.dma_start(w2[:, q, :], a.L1_gnn_msg_W2[rows, :]).then_inc(s_w, 16)
                sp.dma_start(u1[:, q, :], a.L1_gnn_upd_W1[rows, :]).then_inc(s_w, 16)
                sp.dma_start(u2[:, q, :], a.L1_gnn_upd_W2[rows, :]).then_inc(s_w, 16)
            sp.dma_start(b2[:], a.L1_gnn_msg_b2.rearrange("(a d) -> a d", a=1)).then_inc(s_w, 16)
            sp.dma_start(c1[:], a.L1_gnn_upd_b1.rearrange("(q d) -> d q", q=2),
                         allow_slow_non_contiguous=True).then_inc(s_w, 16)
            sp.dma_start(c2[:], a.L1_gnn_upd_b2.rearrange("(a d) -> a d", a=1).to_broadcast([P, D])).then_inc(s_w, 16)
            sp.dma_start(up[0:M, 0:M], a.L2_gnn_W_up_s).then_inc(s_w, 16)
            for q in range(3):
                sp.dma_start(up[M + q:M + q + 3 * M - 2:3, M + q * M:M + (q + 1) * M], a.L2_gnn_W_up_v).then_inc(s_w, 16)
            with sp.Fori(0, NIT) as i:
                sp.wait_ge(s_m, i)
                sp.dma_start(deg[:], S.deg_rows[0:1, bass.ds(i * (KB * P), KB * P)]).then_inc(s_deg, 16)
                sp.wait_ge(s_tc, 2 * i + 2)
                sp.dma_start(S.tab_2.rearrange("(k p) d -> p k d", p=P)[:, bass.ds(i * KB, KB), :],
                             y[:]).then_inc(s_out, 16)
            sp.wait_ge(s_out, 16 * NIT)

        @block.gpsimd
        def _(pool):
            pool.memset(up[:], 0.0).then_inc(s_up, 1)
            pool.memset(ph.ln.eps[:], EPS).then_inc(ph.ln.s_eps, 1)

        @block.tensor
        def _(pe):
            pe.wait_ge(s_w, 13 * 16)
            pe.wait_ge(s_up, 1)
            with pe.Fori(0, NIT) as i:
                pe.wait_ge(s_xc, i + 1)
                pe.wait_ge(s_tc, 2 * i)
                for k in range(KB):
                    bank, c = blocks_of(ps[0], ps[1], k)
                    last = pe.transpose(bank[:, c:c + P], xc[:, k, :], S.ident[:])
                last.then_inc(s_xT, 1)
                pe.wait_ge(s_deg, 16 * i + 16)
                at = i * KB
                for hf, n in ((0, 4), (1, 3)):
                    out = ps[2 + hf][:, 0:n * P]
                    for q in range(2):
                        pe.matmul(out, w2[:, q, :], agg[:, bass.ds(at + 4 * hf, n), q * D:(q + 1) * D],
                                  start=(q == 0), stop=False)
                    last = pe.matmul(out, b2[:], deg[0:1, hf * 4 * P:(hf * 4 + n) * P], start=False, stop=True)
                last.then_inc(s_m, 1)
                pe.wait_ge(s_mc, 2 * i + 2)
                pe.wait_ge(s_xTc, 2 * i + 2)
                for q in range(2):
                    for hf, n in ((0, 4), (1, 3)):
                        out = ps[4 + 2 * q + hf][:, 0:n * P]
                        w = slice(q * D, (q + 1) * D)
                        pe.matmul(out, u1[:, 0, w], xT[:, cols[hf], :].rearrange("p k e -> p (k e)"), start=True, stop=False)
                        last = pe.matmul(out, u1[:, 1, w], mT[:, cols[hf], :].rearrange("p k e -> p (k e)"),
                                         start=False, stop=True)
                last.then_inc(s_u, 1)
                pe.wait_ge(s_uc, 4 * i + 4)
                for k in range(KB):
                    bank, c = blocks_of(ps[0], ps[1], k)
                    pe.matmul(bank[:, c:c + D], uT[:, 0, k, :], u2[:, 0, :], start=True, stop=False)
                    last = pe.matmul(bank[:, c:c + D], uT[:, 1, k, :], u2[:, 1, :], start=False, stop=True)
                last.then_inc(s_y, 1)
                pe.wait_ge(s_n, i + 1)
                for k in range(KB):
                    bank, c = blocks_of(ps[2], ps[3], k)
                    last = pe.transpose(bank[:, c:c + P], xc[:, k, :], S.ident[:])
                last.then_inc(s_T2, 1)
                pe.wait_ge(s_T2c, 2 * i + 2)
                for k in range(KB):
                    bank, c = blocks_of(ps[4], ps[5], k)
                    last = pe.matmul(bank[:, c:c + D], xT[:, k, :], up[:], start=True, stop=True)
                last.then_inc(s_t, 1)

        @block.scalar
        def _(act):
            def copy2(dst, b0, b1, done, scale=1.0):
                for hf, (bank, n) in enumerate(((b0, 4), (b1, 3))):
                    act.activation(dst[:, cols[hf], :].rearrange("p k e -> p (k e)"), bank[:, 0:n * P], ACT.Copy,
                                   scale=scale).then_inc(done, 1)
            with act.Fori(0, NIT) as i:
                act.wait_ge(s_xT, i + 1)
                copy2(xT, ps[0], ps[1], s_xTc)
                act.wait_ge(s_m, i + 1)
                act.wait_ge(s_out, 16 * i)
                copy2(mT, ps[2], ps[3], s_mc)
                act.wait_ge(s_u, i + 1)
                for q in range(2):
                    for hf, n in ((0, 4), (1, 3)):
                        act.activation(uT[:, q, cols[hf], :].rearrange("p k e -> p (k e)"), ps[4 + 2 * q + hf][:, 0:n * P],
                                       ACT.Silu, bias=c1[:, q:q + 1]).then_inc(s_uc, 1)
                root(act, ph, i)
                act.wait_ge(s_T2, i + 1)
                copy2(xT, ps[2], ps[3], s_T2c)
                act.wait_ge(s_t, i + 1)
                copy2(y, ps[4], ps[5], s_tc, scale=M ** -0.5)

        @block.vector
        def _(v):
            v.wait_ge(s_w, 13 * 16)
            VN = 8
            with v.Fori(0, NIT) as i:
                rows = S.x[:, bass.ds(i * KB, KB), :]
                v.wait_ge(s_T2, i)
                v.tensor_scalar(xc[:], rows, 1.0, None, ALU.mult).then_inc(s_xc, 1)
                n = VN * i
                v.wait_ge(s_y, i + 1)
                v.wait_ge(s_xc, i + 1)
                for hf, k in ((0, 4), (1, 3)):
                    last = v.scalar_tensor_tensor(y[:, cols[hf], :], xc[:, cols[hf], :], 2.0,
                                                  ps[hf][:, 0:k * P].rearrange("p (k d) -> p k d", k=k),
                                                  ALU.mult, ALU.add)
                last.then_inc(s_v, 1)
                v.wait_ge(s_v, n + 1)
                v.tensor_tensor(y[:], y[:], c2[:].rearrange("p (a d) -> p a d", a=1).to_broadcast([P, KB, D]),
                                ALU.add).then_inc(s_v, 1)
                v.wait_ge(s_v, n + 2)
                ph.ln.turn = i + 1
                n = normalize(v, ph, y[:], xc[:], s_v, n + 2)
                v.wait_ge(s_v, n)
                v.tensor_scalar(rows, xc[:], 1.0, None, ALU.mult).then_inc(s_n, 1)
                v.wait_ge(s_n, i + 1)


def edge2_phase(nc, S, a, agg):
    with Phase(nc, "edge2") as ph:
        M = 32
        DEEP = 8
        R0, RN = 50, 12
        at = ph.sbs("at", DEEP, [P, G2, RN])
        ix = ph.sbs("ix", DEEP, [P, G2], I32)
        sv = ph.sbs("sv", DEEP, [P, G2, D])
        oh = ph.sbs("oh", 2, [P, G2, P])
        rT = ph.sbs("rT", 2, [P, P])
        hr = ph.sbs("hr", 2, [P, P])
        vy = ph.sbs("vy", 2, [P, G2, 3, M])
        dot = ph.sbs("dot", 2, [P, G2, M])
        su = ph.sbs("su", 2, [P, G2, M])
        m = ph.sbs("m", 2, [P, G2, 2 * D])
        wr1 = ph.sb("wr1", [P, G2, 8])
        wr2 = ph.sb("wr2", [P, G2, D])
        psT = [ph.bank(f"psT{k}") for k in range(2)]
        psR = [ph.bank(f"psR{k}") for k in range(2)]
        psW = [ph.bank(f"psW{k}") for k in range(2)]
        psA = [ph.bank(f"psA{k}") for k in range(2)]
        s_w, s_turn, s_zero, s_c, s_go = (ph.sem(n) for n in ("s_w", "s_turn", "s_zero", "s_c", "s_go"))
        s_half, s_acc = ph.sems("s_half", DEEP), ph.sems("s_acc", DEEP)
        s_rec, s_ix, s_got, s_oh = (ph.sems(n, DEEP) for n in ("s_rec", "s_ix", "s_got", "s_oh"))
        s_T, s_TT, s_R, s_hr, s_W, s_m, s_C = (ph.sems(n, DEEP) for n in ("s_T", "s_TT", "s_R", "s_hr", "s_W", "s_m", "s_C"))
        block = ph.block()
        GT = NT // G2
        rec = S.records.rearrange("(p j) c -> p j c", p=P)

        @block.sync
        def _(sp):
            sp.wait_ge(s_zero, 3)
            for k in range(G2):
                sp.dma_start(wr1[RN * k + 4:RN * (k + 1), k, :], a.L2_gnn_W_r1).then_inc(s_w, 16)
                sp.dma_start(wr2[8 * k:8 * (k + 1), k, :], a.L2_gnn_W_r2).then_inc(s_w, 16)

            def step(s, g, b, r):
                wait(sp, s_m[b], r)
                sp.dma_start(at[b][:], rec[:, bass.ds(g * G2, G2), R0:R0 + RN]).then_inc(s_rec[b], 16)
            runs(GT, [0], DEEP, sp, step)

        @block.gpsimd
        def _(pool):
            runs(GT, [0], DEEP, pool,
                 lambda s, g, b, r: gather_on(pool, b, ix, sv, S.tab_2, s_ix, s_got, s_turn, r))

        @block.vector
        def _(v):
            v.memset(agg[:], 0.0).then_inc(s_zero, 1)
            v.memset(wr1[:], 0.0).then_inc(s_zero, 1)
            v.memset(wr2[:], 0.0).then_inc(s_zero, 1)
            v.wait_ge(s_w, 32 * G2)
            w2 = wr2[0:8 * G2]
            v.tensor_scalar(w2, w2, 8 ** -0.5, None, ALU.mult).then_inc(s_zero, 1)
            v.wait_ge(s_zero, 4)
            v.tensor_scalar(w2[:, :, 3 * M:], w2[:, :, 3 * M:], 3 ** -0.5, None, ALU.mult).then_inc(s_zero, 1)
            v.wait_ge(s_zero, 5)
            blocks = []

            def step(s, g, b, r):
                o, n = two_before(b, r, DEEP)
                p = b % 2
                if s == 0:
                    wait(v, s_got[b], r * 16 * G2)
                    wait(v, s_m[b], r)
                    v.tensor_scalar(ix[b][:], S.e_src[:, bass.ds(g * G2, G2)], 1.0, None, ALU.mult).then_inc(s_ix[b], 1)
                elif s == 7:
                    blocks[:] = load_blocks(v, S, g)
                elif s == 5:
                    wait(v, s_C[o], n)
                    one_hot(v, oh[p][:], S, S.e_dl, g).then_inc(s_oh[b], 1)
                elif s == 2 or s == 4:
                    add_to_block(v, agg, blocks, psA, b, r, s // 2 - 1, s_C, s_half, s_acc, DEEP)
                else:
                    w = psW[p][:, 0:G2 * D].rearrange("p (k c) -> p k c", k=G2)
                    send, mo = sv[b], m[p]
                    ss = send[:, :, 0:M]
                    vs = send[:, :, M:D].rearrange("p k (i m) -> p k i m", i=3)
                    yv = at[b][:, :, 1:4].rearrange("p k (i a) -> p k i a", a=1).to_broadcast([P, G2, 3, M])
                    vo = mo[:, :, 2 * M:].rearrange("p k (i m) -> p k i m", i=3)

                    def thrice(t):
                        return t.rearrange("p k (a m) -> p k a m", a=1).to_broadcast([P, G2, 3, M])
                    if s == 1:
                        v.wait_ge(s_W[b], r + 1)
                        v.wait_ge(s_got[b], (r + 1) * 16 * G2)
                        wait(v, s_m[o], n)
                        wait(v, s_C[o], n)
                        v.tensor_tensor(vy[p][:], vs, yv, ALU.mult).then_inc(s_c, 1)
                        v.tensor_tensor(su[p][:], w[:, :, 2 * M:3 * M], ss, ALU.mult).then_inc(s_c, 1)
                        v.tensor_tensor(mo[:, :, 0:M], w[:, :, 0:M], ss, ALU.mult)
                    elif s == 3:
                        v.wait_ge(s_c, g * 3 + 1)
                        v.tensor_reduce(dot[p][:], vy[p][:].rearrange("p k i m -> p k m i"), axis=AX.X,
                                        op=ALU.add).then_inc(s_c, 1)
                        v.tensor_tensor(vo[:, :, :, 0:M], thrice(w[:, :, M:2 * M]), vs, ALU.mult)
                    else:
                        v.wait_ge(s_c, g * 3 + 3)
                        v.tensor_tensor(vo[:, :, :, M:], thrice(su[p][:]), yv, ALU.mult)
                        v.tensor_tensor(mo[:, :, M:2 * M], w[:, :, 3 * M:], dot[p][:], ALU.mult).then_inc(s_m[b], 1)
            runs(GT, [0, 6, 4, 6, 4, 6, 4, 4], DEEP, v, lambda s, *x: step((0, 7, 1, 2, 3, 4, 5, 6)[s], *x))

        @block.scalar
        def _(act):
            def step(s, g, b, r):
                o, n = two_before(b, r, DEEP)
                if s == 0:
                    act.wait_ge(s_T[b], r + 1)
                    wait(act, s_R[o], n)
                    act.activation(rT[b % 2][0:G2 * RN, :], psT[b % 2][0:G2 * RN, 0:P], ACT.Copy).then_inc(s_TT[b], 1)
                else:
                    act.wait_ge(s_R[b], r + 1)
                    wait(act, s_W[o], n)
                    act.activation(hr[b % 2][0:8 * G2, :], psR[b % 2][0:8 * G2, 0:P], ACT.Silu,
                                   scale=8 ** -0.5).then_inc(s_hr[b], 1)
            runs(GT, [1, 2], DEEP, act, step)

        @block.tensor
        def _(pe):
            pe.wait_ge(s_zero, 5)

            def step(s, g, b, r):
                o, n = two_before(b, r, DEEP)
                if s == 0:
                    pe.wait_ge(s_m[b], r + 1)
                    pe.wait_ge(s_oh[b], r + 1)
                    wait(pe, s_acc[o], n)
                    for k in range(G2):
                        for q in range(2):
                            c = k * 2 * D + q * D
                            last = pe.matmul(psA[b % 2][:, c:c + D], m[b % 2][:, k, q * D:(q + 1) * D],
                                             oh[b % 2][:, k, :], start=True, stop=True)
                    last.then_inc(s_C[b], 1)
                elif s == 1:
                    pe.wait_ge(s_hr[b], r + 1)
                    wait(pe, s_m[o], n)
                    pe.matmul(psW[b % 2][:, 0:G2 * D], hr[b % 2][0:8 * G2, :], wr2[0:8 * G2].rearrange("p k c -> p (k c)"),
                              start=True, stop=True).then_inc(s_W[b], 1)
                elif s == 2:
                    pe.wait_ge(s_TT[b], r + 1)
                    wait(pe, s_hr[o], n)
                    pe.sem_inc(s_go, 1)
                    pe.matmul(psR[b % 2][0:8 * G2, 0:P], wr1[0:G2 * RN].rearrange("p k c -> p (k c)"), rT[b % 2][0:G2 * RN, :], start=True,
                              stop=True).then_inc(s_R[b], 1)
                else:
                    pe.wait_ge(s_rec[b], (r + 1) * 16)
                    wait(pe, s_TT[o], n)
                    pe.transpose(psT[b % 2][0:G2 * RN, 0:P], at[b][:].rearrange("p k c -> p (k c)"), S.ident[:]).then_inc(s_T[b], 1)
            runs(GT, [5, 3, 2, 1], DEEP, pe, step)


def node2_phase(nc, S, a, agg):
    with Phase(nc, "node2") as ph:
        M, Z = 32, 160
        NS = 4
        wd = ph.sb("wd", [P, 2, Z])
        ws = ph.sb("ws", [P, NS, Z])
        kind = ph.sb("kind", [P, NBLK], I32)
        mask = ph.sb("mask", [P, NS, NBLK])
        xc = ph.sb("xc", [P, KB, D])
        xm = ph.sb("xm", [P, KB, D])
        norm_buffers(ph, sq=xm)
        ac = ph.sb("ac", [P, KB, 2 * D])
        xmT = ph.sbs("xmT", 2, [P, KB, P])
        z = ph.sb("z", [P, KB, Z])
        y = ac[:, :, 0:D]
        ps = [ph.bank(f"ps{k}") for k in range(8)]
        names = ("s_w", "s_zero", "s_k", "s_xc", "s_ac", "s_xm", "s_T", "s_Tc", "s_z", "s_zc", "s_v", "s_n", "s_out")
        (s_w, s_zero, s_k, s_xc, s_ac, s_xm, s_T, s_Tc, s_z, s_zc, s_v, s_n, s_out) = (ph.sem(n) for n in names)
        block = ph.block()
        cols = (slice(0, 4), slice(4, KB))

        @block.sync
        def _(sp):
            sp.wait_ge(s_zero, 3)
            sp.dma_start(wd[0:2 * M, 0, 0:2 * M], a.L2_gnn_W_dn_s).then_inc(s_w, 16)
            sp.dma_start(wd[2 * M:, 0, 2 * M:3 * M], a.L2_gnn_W_dn_v).then_inc(s_w, 16)
            sp.dma_start(wd[0:2 * M, 1, 3 * M:4 * M], a.L2_gnn_W_dn_v).then_inc(s_w, 16)
            sp.dma_start(wd[2 * M:, 1, 4 * M:5 * M], a.L2_gnn_W_dn_v).then_inc(s_w, 16)
            for k in range(NS):
                sp.dma_start(ws[0:M, k, 0:2 * M], a.L2_gnn_W_sk_s[k]).then_inc(s_w, 16)
                for q in range(3):
                    sp.dma_start(ws[M + q:M + q + 3 * M - 2:3, k, (2 + q) * M:(3 + q) * M],
                                 a.L2_gnn_W_sk_v[k]).then_inc(s_w, 16)
            sp.dma_start(kind[:, 0:NBLK - 1], a.node_type_4[0:(NBLK - 1) * P].rearrange("(b p) -> p b", p=P),
                         allow_slow_non_contiguous=True).then_inc(s_k, 16)
            sp.dma_start(kind[0:NLAST, NBLK - 1:], a.node_type_4[(NBLK - 1) * P:N].rearrange("(p b) -> p b", b=1),
                         allow_slow_non_contiguous=True).then_inc(s_k, 16)
            with sp.Fori(0, NIT) as i:
                sp.wait_ge(s_n, i + 1)
                sp.dma_start(S.tab_3.rearrange("(k p) d -> p k d", p=P)[:, bass.ds(i * KB, KB), :],
                             xc[:]).then_inc(s_out, 16)
            sp.wait_ge(s_out, 16 * NIT)

        @block.gpsimd
        def _(pool):
            pool.memset(wd[:], 0.0).then_inc(s_zero, 1)
            pool.memset(ws[:], 0.0).then_inc(s_zero, 1)
            pool.memset(kind[:], 0).then_inc(s_zero, 1)
            pool.memset(ph.ln.eps[:], EPS).then_inc(ph.ln.s_eps, 1)

        @block.tensor
        def _(pe):
            pe.wait_ge(s_w, 20 * 16)
            pe.wait_ge(s_v, 1)
            with pe.Fori(0, NIT) as i:
                def turn(k):
                    pe.wait_ge(s_xm, NS * i + k + 1)
                    pe.wait_ge(s_Tc, 2 * (NS * i + k))
                    for j in range(KB):
                        bank, c = blocks_of(ps[0], ps[1], j)
                        last = pe.transpose(bank[:, c:c + P], xm[:, j, :], S.ident[:])
                    last.then_inc(s_T, 1)

                def z_of(j):
                    return ps[2 + j // 3][:, (j % 3) * Z:(j % 3 + 1) * Z]
                turn(0)
                pe.wait_ge(s_ac, i + 1)
                pe.wait_ge(s_zc, 3 * i)
                for q in range(2):
                    for j in range(KB):
                        pe.matmul(z_of(j), ac[:, j, q * D:(q + 1) * D], wd[:, q, :], start=(q == 0 and j % 3 == 0),
                                  stop=False, skip_group_check=True)
                for k in range(NS):
                    if k + 1 < NS:
                        turn(k + 1)
                    pe.wait_ge(s_Tc, 2 * (NS * i + k + 1))
                    for j in range(KB):
                        last = pe.matmul(z_of(j), xmT[k % 2][:, j, :], ws[:, k, :], start=False, stop=(k == NS - 1),
                                         skip_group_check=True)
                last.then_inc(s_z, 1)

        @block.scalar
        def _(act):
            with act.Fori(0, NIT) as i:
                act.wait_ge(s_z, i)
                for k in range(NS):
                    act.wait_ge(s_T, NS * i + k + 1)
                    for hf, n in ((0, 4), (1, 3)):
                        act.activation(xmT[k % 2][:, cols[hf], :].rearrange("p k e -> p (k e)"), ps[hf][:, 0:n * P],
                                       ACT.Copy).then_inc(s_Tc, 1)
                act.wait_ge(s_z, i + 1)
                act.wait_ge(s_n, i)
                for q, n in enumerate((3, 3, 1)):
                    src = ps[2 + q][:, 0:n * Z].rearrange("p (k c) -> p k c", k=n)
                    act.activation(z[:, 3 * q:3 * q + n, 0:2 * M], src[:, :, 0:2 * M], ACT.Silu)
                    act.activation(z[:, 3 * q:3 * q + n, 2 * M:], src[:, :, 2 * M:], ACT.Copy).then_inc(s_zc, 1)
                root(act, ph, i)

        @block.vector
        def _(v):
            v.wait_ge(s_w, 20 * 16)
            v.wait_ge(s_k, 32)
            v.tensor_scalar(wd[:], wd[:], 1.0 / 64, None, ALU.mult).then_inc(s_v, 1)
            for k in range(NS):
                v.tensor_scalar(mask[:, k, :], kind[:], float(k), 0.5 * M ** -0.5, ALU.is_equal, ALU.mult).then_inc(s_v, 1)
            v.wait_ge(s_v, 5)
            VN = 9
            with v.Fori(0, NIT) as i:
                blocks = bass.ds(i * KB, KB)
                rows = S.x[:, blocks, :]
                v.wait_ge(s_out, 16 * i)
                v.tensor_scalar(xc[:], rows, 1.0, None, ALU.mult).then_inc(s_xc, 1)
                v.wait_ge(s_z, i)
                v.tensor_scalar(ac[:], agg[:, blocks, :], 1.0, None, ALU.mult).then_inc(s_ac, 1)
                v.wait_ge(s_xc, i + 1)
                for k in range(NS):
                    v.wait_ge(s_T, NS * i + k)
                    v.tensor_tensor(xm[:], xc[:], mask[:, k, blocks].rearrange("p (k a) -> p k a", a=1)
                                    .to_broadcast([P, KB, D]), ALU.mult).then_inc(s_xm, 1)
                v.wait_ge(s_zc, 3 * i + 3)
                n = VN * i + 5
                v.tensor_tensor(y[:, :, 0:M], z[:, :, 0:M], xc[:, :, 0:M], ALU.add)
                for q in range(3):
                    last = v.tensor_tensor(y[:, :, M + q:M + q + 3 * M - 2:3], z[:, :, (2 + q) * M:(3 + q) * M],
                                           z[:, :, M:2 * M], ALU.mult)
                last.then_inc(s_v, 1)
                v.wait_ge(s_v, n + 1)
                v.tensor_tensor(y[:, :, M:], y[:, :, M:], xc[:, :, M:], ALU.add).then_inc(s_v, 1)
                v.wait_ge(s_v, n + 2)
                ph.ln.turn = i + 1
                n = normalize(v, ph, y, xc[:], s_v, n + 2)
                v.wait_ge(s_v, n)
                v.tensor_scalar(rows, xc[:], 1.0, None, ALU.mult).then_inc(s_v, 1)
                v.wait_ge(s_v, n + 1)
                v.sem_inc(s_n, 1)


def edge3_phase(nc, S, a, agg):
    with Phase(nc, "edge3") as ph:
        DEEP = 8
        ix = ph.sbs("ix", DEEP, [P, G2], I32)
        xs = ph.sbs("xs", DEEP, [P, G2, D])
        oh = ph.sbs("oh", 2, [P, G2, 2, P])
        psA = [ph.bank(f"psA{k}") for k in range(2)]
        s_turn, s_zero = (ph.sem(n) for n in ("s_turn", "s_zero"))
        s_half, s_acc = ph.sems("s_half", DEEP), ph.sems("s_acc", DEEP)
        s_ix, s_got, s_oh, s_C = (ph.sems(n, DEEP) for n in ("s_ix", "s_got", "s_oh", "s_C"))
        block = ph.block()
        GT = NT // G2

        @block.gpsimd
        def _(pool):
            runs(GT, [0], DEEP, pool,
                 lambda s, g, b, r: gather_on(pool, b, ix, xs, S.tab_3, s_ix, s_got, s_turn, r))

        @block.vector
        def _(v):
            v.memset(agg[:], 0.0).then_inc(s_zero, 1)
            v.scalar_tensor_tensor(S.e_dl[:], S.e_dl[:], -1.0, S.e_dl0[:], ALU.add, ALU.subtract).then_inc(s_zero, 1)
            v.wait_ge(s_zero, 2)
            at = []

            def step(s, g, b, r):
                o, n = two_before(b, r, DEEP)
                if s == 0:
                    wait(v, s_got[b], r * 16 * G2)
                    wait(v, s_C[b], r)
                    v.tensor_scalar(ix[b][:], S.e_src[:, bass.ds(g * G2, G2)], 1.0, None, ALU.mult).then_inc(s_ix[b], 1)
                elif s == 1:
                    at[:] = load_blocks(v, S, g)
                elif s == 3:
                    wait(v, s_C[o], n)
                    one_hot(v, oh[b % 2][:, :, 0, :], S, S.e_dl0, g)
                    one_hot(v, oh[b % 2][:, :, 1, :], S, S.e_dl, g).then_inc(s_oh[b], 1)
                else:
                    add_to_block(v, agg, at, psA, b, r, s // 4, s_C, s_half, s_acc, DEEP)
            runs(GT, [0, 6, 6, 4, 6], DEEP, v, step)

        @block.tensor
        def _(pe):
            def step(s, g, b, r):
                o, n = two_before(b, r, DEEP)
                pe.wait_ge(s_oh[b], r + 1)
                pe.wait_ge(s_got[b], (r + 1) * 16 * G2)
                wait(pe, s_acc[o], n)
                for k in range(G2):
                    last = pe.matmul(psA[b % 2][:, k * 2 * D:(k + 1) * 2 * D], xs[b][:, k, :],
                                     oh[b % 2][:, k].rearrange("p t n -> p (t n)"), start=True, stop=True)
                last.then_inc(s_C[b], 1)
            runs(GT, [5], DEEP, pe, step)


def node3_phase(nc, S, a, agg, out):
    with Phase(nc, "node3") as ph:
        norm_buffers(ph)
        w = ph.sb("w", [P, 3, D])
        wT = ph.sb("wT", [P, 3, D])
        bd = ph.sb("bd", [1, 2, D])
        dif = ph.sb("dif", [1, D])
        bias = ph.sb("bias", [3, D])
        deg = ph.sb("deg", [3, KB * P])
        xc = ph.sb("xc", [P, KB, D])
        ac = ph.sb("ac", [P, KB, 2 * D])
        xT = ph.sb("xT", [P, KB, P])
        y = ph.sb("y", [P, KB, D])
        ps = [ph.bank(f"ps{k}") for k in range(4)]
        names = ("s_w", "s_b", "s_wT", "s_wc", "s_dif", "s_deg", "s_xc", "s_ac", "s_T", "s_Tc", "s_y", "s_v", "s_n", "s_out")
        (s_w, s_b, s_wT, s_wc, s_dif, s_deg, s_xc, s_ac, s_T, s_Tc, s_y, s_v, s_n, s_out) = (ph.sem(n) for n in names)
        block = ph.block()
        cols = (slice(0, 4), slice(4, KB))

        def row(t):
            return t.rearrange("(a d) -> a d", a=1)

        @block.sync
        def _(sp):
            for q, t in enumerate((a.L3_gnn_W_data, a.L3_gnn_W_control, a.L3_gnn_W_self)):
                sp.dma_start(w[:, q, :], t).then_inc(s_w, 16)
            sp.dma_start(bd[:, 0, :], row(a.L3_gnn_b_data)).then_inc(s_w, 16)
            sp.dma_start(bd[:, 1, :], row(a.L3_gnn_b_control)).then_inc(s_w, 16)
            sp.dma_start(bias[0:1, :], row(a.L3_gnn_b_control)).then_inc(s_b, 16)
            sp.dma_start(bias[2:3, :], row(a.L3_gnn_b_self)).then_inc(s_b, 16)
            sp.wait_ge(s_dif, 1)
            sp.dma_start(bias[1:2, :], dif[:]).then_inc(s_b, 16)
            with sp.Fori(0, NIT - 1) as i:
                sp.wait_ge(s_y, i)
                sp.dma_start(deg[:], S.deg_rows[:, bass.ds(i * (KB * P), KB * P)]).then_inc(s_deg, 16)
                sp.wait_ge(s_n, i + 1)
                sp.dma_start(out[0:(NBLK - KB) * P, :].rearrange("(k p) d -> p k d", p=P)[:, bass.ds(i * KB, KB), :],
                             xc[:]).then_inc(s_out, 16)
            i = NIT - 1
            sp.wait_ge(s_y, i)
            sp.dma_start(deg[:], S.deg_rows[:, i * KB * P:]).then_inc(s_deg, 16)
            sp.wait_ge(s_n, i + 1)
            sp.dma_start(out[i * KB * P:(NBLK - 1) * P, :].rearrange("(k p) d -> p k d", p=P),
                         xc[:, 0:KB - 1, :]).then_inc(s_out, 16)
            sp.dma_start(out[(NBLK - 1) * P:N, :], xc[0:NLAST, KB - 1, :]).then_inc(s_out, 16)
            sp.wait_ge(s_out, 16 * (NIT + 1))

        @block.gpsimd
        def _(pool):
            pool.memset(ph.ln.eps[:], EPS).then_inc(ph.ln.s_eps, 1)

        @block.tensor
        def _(pe):
            pe.wait_ge(s_w, 80)
            for q in range(3):
                last = pe.transpose(ps[0][:, q * D:(q + 1) * D], w[:, q, :], S.ident[:])
            last.then_inc(s_wT, 1)
            pe.wait_ge(s_wc, 1)
            pe.wait_ge(s_b, 48)
            with pe.Fori(0, NIT) as i:
                pe.wait_ge(s_xc, i + 1)
                for k in range(KB):
                    bank, c = blocks_of(ps[0], ps[1], k)
                    last = pe.transpose(bank[:, c:c + P], xc[:, k, :], S.ident[:])
                last.then_inc(s_T, 1)
                pe.wait_ge(s_Tc, 2 * i + 2)
                pe.wait_ge(s_ac, i + 1)
                pe.wait_ge(s_deg, 16 * i + 16)
                for k in range(KB):
                    bank, c = blocks_of(ps[2], ps[3], k)
                    o = bank[:, c:c + D]
                    pe.matmul(o, ac[:, k, 0:D], wT[:, 0, :], start=True, stop=False)
                    pe.matmul(o, ac[:, k, D:], wT[:, 1, :], start=False, stop=False)
                    pe.matmul(o, xT[:, k, :], wT[:, 2, :], start=False, stop=False)
                    last = pe.matmul(o, deg[:, k * P:(k + 1) * P], bias[:], start=False, stop=True)
                last.then_inc(s_y, 1)

        @block.scalar
        def _(act):
            with act.Fori(0, NIT) as i:
                act.wait_ge(s_T, i + 1)
                for hf, n in ((0, 4), (1, 3)):
                    act.activation(xT[:, cols[hf], :].rearrange("p k e -> p (k e)"), ps[hf][:, 0:n * P],
                                   ACT.Copy).then_inc(s_Tc, 1)
                root(act, ph, i)

        @block.vector
        def _(v):
            v.wait_ge(s_w, 80)
            v.tensor_tensor(dif[:], bd[:, 0, :], bd[:, 1, :], ALU.subtract).then_inc(s_dif, 1)
            v.wait_ge(s_wT, 1)
            v.tensor_copy(wT[:], ps[0][:, 0:3 * D].rearrange("p (q d) -> p q d", q=3)).then_inc(s_wc, 1)
            VN = 7
            with v.Fori(0, NIT) as i:
                blocks = bass.ds(i * KB, KB)
                v.wait_ge(s_out, 16 * i)
                v.tensor_scalar(xc[:], S.x[:, blocks, :], 1.0, None, ALU.mult).then_inc(s_xc, 1)
                v.wait_ge(s_y, i)
                v.tensor_scalar(ac[:], agg[:, blocks, :], 1.0, None, ALU.mult).then_inc(s_ac, 1)
                n = VN * i
                v.wait_ge(s_y, i + 1)
                v.wait_ge(s_xc, i + 1)
                for hf, k in ((0, 4), (1, 3)):
                    last = v.scalar_tensor_tensor(y[:, cols[hf], :], ps[2 + hf][:, 0:k * P].rearrange("p (k d) -> p k d", k=k),
                                                  0.0, xc[:, cols[hf], :], ALU.max, ALU.add)
                last.then_inc(s_v, 1)
                v.wait_ge(s_v, n + 1)
                ph.ln.turn = i + 1
                n = normalize(v, ph, y[:], xc[:], s_v, n + 1)
                v.wait_ge(s_v, n)
                v.sem_inc(s_n, 1)


def program(nc, a, out):
    with ExitStack() as ctx:
        S = Names()

        def dram(name, shape, dt=F32):
            return nc.dram_tensor(name, shape, dt, kind="Internal").ap()

        def sb(c, name, shape, dt=F32):
            return c.enter_context(nc.sbuf_tensor(name, shape, dt))

        S.records = dram("records", (P * NT, PC))
        S.by_src = dram("by_src", (P * TE, XC))
        S.running = dram("running", (P * TE, D))
        S.deg_rows = dram("deg_rows", (3, NBLK * P))
        S.tab_a = dram("tab_a", (NBLK * P, 2 * D))
        S.tab_b = dram("tab_b", (NBLK * P, 2 * D))
        S.tab_2 = dram("tab_2", (NBLK * P, D))
        S.tab_3 = dram("tab_3", (NBLK * P, D))
        S.x = sb(ctx, "x_res", [P, NBLK, D])
        S.iota = sb(ctx, "iota", [P, P])
        S.iota_b = sb(ctx, "iota_b", [P, P], BF16)
        S.ident = sb(ctx, "ident", [P, P])
        S.ident_b = sb(ctx, "ident_b", [P, P], BF16)
        S.lower = sb(ctx, "lower", [P, P])
        S.upper = sb(ctx, "upper", [P, P])
        S.blk = sb(ctx, "blk", [1, NT], I32)
        S.last = sb(ctx, "last", [P, NBLK], I32)
        with ExitStack() as c1:
            S.src_key = sb(c1, "src_key", [P, TE], I32)
            S.dst_key = sb(c1, "dst_key", [P, TE], I32)
            S.key_f = sb(c1, "key_f", [P, TE, 2])
            S.lo = sb(c1, "lo", [P, TE, 2])
            S.hi = sb(c1, "hi", [P, TE, 2])
            S.dst_lo0 = sb(c1, "dst_lo0", [P, TE])
            S.base = sb(c1, "base", [P, 2 * HI])
            count_phase(nc, S, a)
            place_phase(nc, S, a)
        S.e_src = sb(ctx, "e_src", [P, NT], I32)
        S.e_dl = sb(ctx, "e_dl", [P, NT])
        S.e_dl0 = sb(ctx, "e_dl0", [P, NT])
        send_phase(nc, S, a)
        max_phase(nc, S, a)
        node0_phase(nc, S, a)
        agg = sb(ctx, "agg", [P, NBLK, 2 * D])
        edge1_phase(nc, S, a, agg)
        node1_phase(nc, S, a, agg)
        edge2_phase(nc, S, a, agg)
        node2_phase(nc, S, a, agg)
        edge3_phase(nc, S, a, agg)
        node3_phase(nc, S, a, agg, out)


class Inputs:

    def __init__(self, t):
        self.x = t["x"]
        self.src = t["src"]
        self.dst = t["dst"]
        self.edge_attr_4 = t["edge_attr_4"]
        self.edge_attr_50 = t["edge_attr_50"]
        self.edge_attr_8 = t["edge_attr_8"]
        self.edge_type_2 = t["edge_type_2"]
        self.node_type_4 = t["node_type_4"]
        self.L0_gnn_W = t["L0_gnn_W"]
        self.L0_gnn_b = t["L0_gnn_b"]
        self.L1_gnn_msg_W1 = t["L1_gnn_msg_W1"]
        self.L1_gnn_msg_b1 = t["L1_gnn_msg_b1"]
        self.L1_gnn_msg_W2 = t["L1_gnn_msg_W2"]
        self.L1_gnn_msg_b2 = t["L1_gnn_msg_b2"]
        self.L1_gnn_upd_W1 = t["L1_gnn_upd_W1"]
        self.L1_gnn_upd_b1 = t["L1_gnn_upd_b1"]
        self.L1_gnn_upd_W2 = t["L1_gnn_upd_W2"]
        self.L1_gnn_upd_b2 = t["L1_gnn_upd_b2"]
        self.L2_gnn_W_up_s = t["L2_gnn_W_up_s"]
        self.L2_gnn_W_up_v = t["L2_gnn_W_up_v"]
        self.L2_gnn_W_r1 = t["L2_gnn_W_r1"]
        self.L2_gnn_W_r2 = t["L2_gnn_W_r2"]
        self.L2_gnn_W_dn_s = t["L2_gnn_W_dn_s"]
        self.L2_gnn_W_dn_v = t["L2_gnn_W_dn_v"]
        self.L2_gnn_W_sk_s = t["L2_gnn_W_sk_s"]
        self.L2_gnn_W_sk_v = t["L2_gnn_W_sk_v"]
        self.L3_gnn_W_data = t["L3_gnn_W_data"]
        self.L3_gnn_b_data = t["L3_gnn_b_data"]
        self.L3_gnn_W_control = t["L3_gnn_W_control"]
        self.L3_gnn_b_control = t["L3_gnn_b_control"]
        self.L3_gnn_W_self = t["L3_gnn_W_self"]
        self.L3_gnn_b_self = t["L3_gnn_b_self"]


_INS = ['x', 'src', 'dst', 'edge_attr_4', 'edge_attr_50', 'edge_attr_8', 'edge_type_2', 'node_type_4',
        'L0_gnn_W', 'L0_gnn_b', 'L1_gnn_msg_W1', 'L1_gnn_msg_b1', 'L1_gnn_msg_W2', 'L1_gnn_msg_b2',
        'L1_gnn_upd_W1', 'L1_gnn_upd_b1', 'L1_gnn_upd_W2', 'L1_gnn_upd_b2', 'L2_gnn_W_up_s', 'L2_gnn_W_up_v',
        'L2_gnn_W_r1', 'L2_gnn_W_r2', 'L2_gnn_W_dn_s', 'L2_gnn_W_dn_v', 'L2_gnn_W_sk_s', 'L2_gnn_W_sk_v',
        'L3_gnn_W_data', 'L3_gnn_b_data', 'L3_gnn_W_control', 'L3_gnn_b_control', 'L3_gnn_W_self', 'L3_gnn_b_self']


def kernel(**inputs):
    import numpy as _np
    import concourse.bacc as _bacc
    from concourse import mybir as _mybir
    from concourse.bass_utils import run_bass_kernel_spmd as _run

    nc = _bacc.Bacc("TRN2", target_bir_lowering=False, num_devices=1)
    arrays, args = {}, {}
    for name in _INS:
        array = _np.ascontiguousarray(inputs[name])
        arrays[f"in_{name}"] = array
        args[name] = nc.dram_tensor(f"in_{name}", array.shape, _mybir.dt.from_np(array.dtype), kind="ExternalInput").ap()
    out = nc.dram_tensor("out_x", (N, D), F32, kind="ExternalOutput").ap()
    program(nc, Inputs(args), out)
    r = _run(nc, [arrays], core_ids=[0])
    return r.results[0]["out_x"]
```
